# Optimizing a Trainium2 kernel written in Bass

```python
import numpy as np
import jax
import jax.numpy as jnp

def _softmax(x, axis=-1):
    return jax.nn.softmax(x, axis=axis)

def _gelu(x):
    return jax.nn.gelu(x, approximate=True)

def _silu(x):
    return jax.nn.silu(x)

def _sigmoid(x):
    return jax.nn.sigmoid(x)

def _layernorm(x, axis=-1, eps=1e-05):
    m = jnp.mean(x, axis=axis, keepdims=True)
    v = jnp.var(x, axis=axis, keepdims=True)
    return (x - m) / jnp.sqrt(v + eps)

def _scatter_add(tgt, idx, src, axis=0):
    return tgt.at[idx].add(src)

def _segment_sum(src, seg, n):
    return jax.ops.segment_sum(src, seg, n)
kernel_name = 'mk_gps_d1_gnn_r8_7c1fde'

def setup_inputs(seed: int=0):
    np.random.seed(seed)
    _w = jnp.asarray

    def _rec_inputs():
        import jax
        import jax.numpy as jnp
        _gk = jax.random.key(seed)
        x = -6.415e-05 + 1 * jax.random.normal(jax.random.fold_in(_gk, 1), (2500, 512), jnp.float32)
        src = jax.random.randint(jax.random.fold_in(_gk, 2), (40000,), 0, 2500, jnp.int32)
        dst = jnp.minimum((2500 * jax.random.uniform(jax.random.fold_in(_gk, 3), (40000,)) ** 2.0).astype(jnp.int32), 19999)
        _o = jnp.argsort(dst, stable=True)
        src = src[_o]
        dst = dst[_o]
        edge_type_10 = jax.random.randint(jax.random.fold_in(_gk, 12), (40000,), 0, 10, jnp.int32)
        edge_weight = 0.000747931 + 0.998196 * jax.random.normal(jax.random.fold_in(_gk, 13), (40000,), jnp.float32)
        return (x, src, dst, edge_type_10, edge_weight)
    x, src, dst, edge_type_10, edge_weight = _rec_inputs()

    def _L0_gnn_setup():
        import jax, jax.numpy as jnp
        import numpy as np
        N, E, H, D, C, L = (2500, 40000, 8, 64, 512, 2)

        def layer_norm(x, g, b, eps=1e-05):
            mu = x.mean(-1, keepdims=True)
            var = ((x - mu) ** 2).mean(-1, keepdims=True)
            return (x - mu) / jnp.sqrt(var + eps) * g + b
        key = jax.random.key(seed)
        ks = jax.random.split(key, 14)
        s = 0.02
        x = jax.random.normal(ks[0], (N, C), jnp.float32)
        edge_index = jax.random.randint(ks[1], (2, E), 0, N, jnp.int32)
        edge_type = jax.random.randint(ks[2], (E,), 0, 10, jnp.int32)
        edge_repre = jax.random.normal(ks[3], (E,), jnp.float32)
        Wq = jax.random.normal(ks[4], (L, C, C), jnp.float32) * s
        Wk = jax.random.normal(ks[5], (L, C, C), jnp.float32) * s
        Wv = jax.random.normal(ks[6], (L, C, C), jnp.float32) * s
        Ws = jax.random.normal(ks[7], (L, C, C), jnp.float32) * s
        bq = jnp.zeros((L, C), jnp.float32)
        bk = jnp.zeros((L, C), jnp.float32)
        bv = jnp.zeros((L, C), jnp.float32)
        bs = jnp.zeros((L, C), jnp.float32)
        W1 = jax.random.normal(ks[8], (C, 2 * C), jnp.float32) * s
        b1 = jnp.zeros((2 * C,), jnp.float32)
        W2 = jax.random.normal(ks[9], (2 * C, C), jnp.float32) * s
        b2 = jnp.zeros((C,), jnp.float32)
        ln_g = jnp.ones((C,), jnp.float32)
        ln_b = jnp.zeros((C,), jnp.float32)
        return {'x': x, 'edge_index': edge_index, 'edge_type': edge_type, 'edge_repre': edge_repre, 'Wq': Wq, 'bq': bq, 'Wk': Wk, 'bk': bk, 'Wv': Wv, 'bv': bv, 'Ws': Ws, 'bs': bs, 'W1': W1, 'b1': b1, 'W2': W2, 'b2': b2, 'ln_g': ln_g, 'ln_b': ln_b}
    _L0_gnn_all = _L0_gnn_setup()
    _L0_gnn_in = {k: v for k, v in _L0_gnn_all.items() if k in ('Wq', 'bq', 'Wk', 'bk', 'Wv', 'bv', 'Ws', 'bs', 'W1', 'b1', 'W2', 'b2', 'ln_g', 'ln_b')}
    del _L0_gnn_all

    def _L0_mix_setup():
        import jax, jax.numpy as jnp
        import numpy as np
        DIM = 512
        HEADS = 8
        DIM_HEAD = 64
        SLICE = 32
        INNER = HEADS * DIM_HEAD
        key = jax.random.key(seed)
        ks = jax.random.split(key, 8)
        B, N = (8, 1024)
        s = 0.02
        return {'x': jax.random.normal(ks[0], (B, N, DIM), dtype=jnp.float32), 'W_in': jax.random.normal(ks[1], (DIM, INNER), dtype=jnp.float32) * s, 'b_in': jnp.zeros((INNER,), dtype=jnp.float32), 'Wq': jax.random.normal(ks[2], (DIM_HEAD, SLICE), dtype=jnp.float32) * s, 'Wk': jax.random.normal(ks[3], (DIM_HEAD, SLICE), dtype=jnp.float32) * s, 'Wv': jax.random.normal(ks[4], (DIM_HEAD, DIM_HEAD), dtype=jnp.float32) * s, 'W_out': jax.random.normal(ks[5], (INNER, DIM), dtype=jnp.float32) * s, 'b_out': jnp.zeros((DIM,), dtype=jnp.float32)}
    _L0_mix_all = _L0_mix_setup()
    _L0_mix_in = {k: v for k, v in _L0_mix_all.items() if k in ('W_in', 'b_in', 'Wq', 'Wk', 'Wv', 'W_out', 'b_out')}
    del _L0_mix_all

    def _L0_ffn_setup():
        import jax, jax.numpy as jnp
        import numpy as np
        DIM = 512
        FFN_DIM = 1408
        GROUP = 128
        EPS = 1e-05

        def _quantize_weight(w, group_size):
            o, i = w.shape
            wg = w.reshape(o, i // group_size, group_size)
            scale = jnp.mean(jnp.abs(wg), axis=-1, keepdims=True) + EPS
            wq = jnp.clip(jnp.round(wg / scale), -1.0, 1.0) * scale
            return wq.reshape(o, i)

        def _bitlinear(x, w, group_size=GROUP):
            wq = w + jax.lax.stop_gradient(_quantize_weight(w, group_size) - w)
            return jnp.einsum('bsd,fd->bsf', x, wq)
        key = jax.random.key(seed)
        k_x, k_g, k_u, k_d = jax.random.split(key, 4)
        x = jax.random.normal(k_x, (8, 512, DIM), dtype=jnp.float32)
        sd_in = 1.0 / np.sqrt(DIM)
        sd_ffn = 1.0 / np.sqrt(FFN_DIM)
        w_gate = jax.random.normal(k_g, (FFN_DIM, DIM), dtype=jnp.float32) * sd_in
        w_up = jax.random.normal(k_u, (FFN_DIM, DIM), dtype=jnp.float32) * sd_in
        w_down = jax.random.normal(k_d, (DIM, FFN_DIM), dtype=jnp.float32) * sd_ffn
        return {'x': x, 'w_gate': w_gate, 'w_up': w_up, 'w_down': w_down}
    _L0_ffn_all = _L0_ffn_setup()
    _L0_ffn_in = {k: v for k, v in _L0_ffn_all.items() if k in ('w_gate', 'w_up', 'w_down')}
    del _L0_ffn_all
    return {'x': x, 'src': src, 'dst': dst, 'edge_type_10': edge_type_10, 'edge_weight': edge_weight, 'L0_gnn_Wq': _L0_gnn_in['Wq'], 'L0_gnn_bq': _L0_gnn_in['bq'], 'L0_gnn_Wk': _L0_gnn_in['Wk'], 'L0_gnn_bk': _L0_gnn_in['bk'], 'L0_gnn_Wv': _L0_gnn_in['Wv'], 'L0_gnn_bv': _L0_gnn_in['bv'], 'L0_gnn_Ws': _L0_gnn_in['Ws'], 'L0_gnn_bs': _L0_gnn_in['bs'], 'L0_gnn_W1': _L0_gnn_in['W1'], 'L0_gnn_b1': _L0_gnn_in['b1'], 'L0_gnn_W2': _L0_gnn_in['W2'], 'L0_gnn_b2': _L0_gnn_in['b2'], 'L0_gnn_ln_g': _L0_gnn_in['ln_g'], 'L0_gnn_ln_b': _L0_gnn_in['ln_b'], 'L0_mix_W_in': _L0_mix_in['W_in'], 'L0_mix_b_in': _L0_mix_in['b_in'], 'L0_mix_Wq': _L0_mix_in['Wq'], 'L0_mix_Wk': _L0_mix_in['Wk'], 'L0_mix_Wv': _L0_mix_in['Wv'], 'L0_mix_W_out': _L0_mix_in['W_out'], 'L0_mix_b_out': _L0_mix_in['b_out'], 'L0_ffn_w_gate': _L0_ffn_in['w_gate'], 'L0_ffn_w_up': _L0_ffn_in['w_up'], 'L0_ffn_w_down': _L0_ffn_in['w_down']}

def reference(x, src, dst, edge_type_10, edge_weight, L0_gnn_Wq, L0_gnn_bq, L0_gnn_Wk, L0_gnn_bk, L0_gnn_Wv, L0_gnn_bv, L0_gnn_Ws, L0_gnn_bs, L0_gnn_W1, L0_gnn_b1, L0_gnn_W2, L0_gnn_b2, L0_gnn_ln_g, L0_gnn_ln_b, L0_mix_W_in, L0_mix_b_in, L0_mix_Wq, L0_mix_Wk, L0_mix_Wv, L0_mix_W_out, L0_mix_b_out, L0_ffn_w_gate, L0_ffn_w_up, L0_ffn_w_down):
    import jax
    import jax.numpy as jnp

    def _L0_gnn_ref(x, edge_index, edge_type, edge_repre, Wq, bq, Wk, bk, Wv, bv, Ws, bs, W1, b1, W2, b2, ln_g, ln_b):
        import jax, jax.numpy as jnp
        import numpy as np
        N, E, H, D, C, L = (2500, 40000, 8, 64, 512, 2)

        def layer_norm(x, g, b, eps=1e-05):
            mu = x.mean(-1, keepdims=True)
            var = ((x - mu) ** 2).mean(-1, keepdims=True)
            return (x - mu) / jnp.sqrt(var + eps) * g + b
        src, dst = (edge_index[0], edge_index[1])
        enc = x
        scale = 1.0 / jnp.sqrt(jnp.float32(D))
        for l in range(L):
            q = (x @ Wq[l] + bq[l]).reshape(N, H, D)
            k = (x @ Wk[l] + bk[l]).reshape(N, H, D)
            v = (x @ Wv[l] + bv[l]).reshape(N, H, D)
            a = (q[dst] * k[src]).sum(-1) * scale
            amax = jax.ops.segment_max(a, dst, num_segments=N)
            amax = jnp.where(jnp.isfinite(amax), amax, 0.0)
            e = jnp.exp(a - amax[dst])
            denom = jax.ops.segment_sum(e, dst, num_segments=N)
            alpha = e / (denom[dst] + 1e-16)
            agg = jax.ops.segment_sum(alpha[:, :, None] * v[src], dst, num_segments=N).reshape(N, C)
            x = agg + (x @ Ws[l] + bs[l]) + enc
        x = layer_norm(x, ln_g, ln_b)
        x = jax.nn.relu(x @ W1 + b1) @ W2 + b2 + x
        x = layer_norm(x, ln_g, ln_b)
        return x + enc

    def _L0_mix_ref(x, W_in, b_in, Wq, Wk, Wv, W_out, b_out):
        import jax, jax.numpy as jnp
        import numpy as np
        DIM = 512
        HEADS = 8
        DIM_HEAD = 64
        SLICE = 32
        INNER = HEADS * DIM_HEAD
        B, N, C = x.shape
        x_mid = (x @ W_in + b_in).reshape(B, N, HEADS, DIM_HEAD).transpose(0, 2, 1, 3)
        q = x_mid @ Wq
        k = x_mid @ Wk
        v = x_mid @ Wv
        q = jax.nn.softmax(q, axis=-1)
        k = jax.nn.softmax(k, axis=-2)
        kv = jnp.einsum('bhns,bhnc->bhsc', k, v)
        qkv = jnp.einsum('bhns,bhsc->bhnc', q, kv)
        qkv = qkv.transpose(0, 2, 1, 3).reshape(B, N, INNER)
        return qkv @ W_out + b_out

    def _L0_ffn_ref(x, w_gate, w_up, w_down):
        import jax, jax.numpy as jnp
        import numpy as np
        DIM = 512
        FFN_DIM = 1408
        GROUP = 128
        EPS = 1e-05

        def _quantize_weight(w, group_size):
            o, i = w.shape
            wg = w.reshape(o, i // group_size, group_size)
            scale = jnp.mean(jnp.abs(wg), axis=-1, keepdims=True) + EPS
            wq = jnp.clip(jnp.round(wg / scale), -1.0, 1.0) * scale
            return wq.reshape(o, i)

        def _bitlinear(x, w, group_size=GROUP):
            wq = w + jax.lax.stop_gradient(_quantize_weight(w, group_size) - w)
            return jnp.einsum('bsd,fd->bsf', x, wq)
        gate = _bitlinear(x, w_gate)
        up = _bitlinear(x, w_up)
        h = jax.nn.silu(gate) * up
        return _bitlinear(h, w_down)
    edge_index = jnp.stack([src, dst])
    xn = _layernorm(x, axis=-1)
    x = x + _L0_gnn_ref(xn, edge_index, edge_type_10, edge_weight, L0_gnn_Wq, L0_gnn_bq, L0_gnn_Wk, L0_gnn_bk, L0_gnn_Wv, L0_gnn_bv, L0_gnn_Ws, L0_gnn_bs, L0_gnn_W1, L0_gnn_b1, L0_gnn_W2, L0_gnn_b2, L0_gnn_ln_g, L0_gnn_ln_b) + _L0_mix_ref(xn[None], L0_mix_W_in, L0_mix_b_in, L0_mix_Wq, L0_mix_Wk, L0_mix_Wv, L0_mix_W_out, L0_mix_b_out)[0]
    x = x + _L0_ffn_ref(_layernorm(x, axis=-1)[None], L0_ffn_w_gate, L0_ffn_w_up, L0_ffn_w_down)[0]
    return x

_drawn_inputs = setup_inputs


def setup_inputs(seed=0):
    import zlib

    import numpy as np

    out = dict(_drawn_inputs(seed))
    spreads = {'L0_gnn_bq': (0.0, 2.0),
     'L0_gnn_bk': (0.0, 2.0),
     'L0_gnn_bv': (0.0, 0.658),
     'L0_gnn_bs': (0.0, 0.672),
     'L0_gnn_b1': (0.0, 1.833),
     'L0_gnn_b2': (0.0, 0.796),
     'L0_gnn_ln_g': (1.0, 0.2),
     'L0_gnn_ln_b': (0.0, 0.392),
     'L0_mix_b_in': (0.0, 0.8),
     'L0_mix_b_out': (0.0, 0.76)}
    factors = {'L0_gnn_Wq': 4.442,
     'L0_gnn_Wk': 4.323,
     'L0_mix_W_in': 8.0,
     'L0_mix_Wq': 8.0,
     'L0_mix_Wk': 8.0,
     'L0_mix_Wv': 8.0,
     'L0_mix_W_out': 8.0,
     'L0_gnn_W1': 2.992,
     'L0_ffn_w_gate': 3.365,
     'L0_ffn_w_up': 3.164,
     'L0_ffn_w_down': 3.167}
    for name, (base, spread) in spreads.items():
        noise = np.random.default_rng([zlib.crc32(name.encode()), seed]).standard_normal(out[name].shape)
        drawn = base * np.exp(spread * noise) if base else spread * noise
        out[name] = jnp.asarray(drawn.astype(out[name].dtype))
    for name, factor in factors.items():
        out[name] = (out[name] * factor).astype(out[name].dtype)
    return out
```

```python
from contextlib import ExitStack

import concourse.bass as bass
from concourse import mybir

P = 128
N = 2500
C = 512
KC = C // P
H = 8
D = C // H
E = 40000
LAYERS = 2
NT = -(-N // P)
NP = NT * P
LAST = N - (NT - 1) * P
ET = -(-E // P)
EK = -(-ET // P)
CH = 16
G = -(-(ET + NT - 1) // CH)
SLOTS = CH * G
RUN = G * P
U = 16
TURNS = SLOTS // U
GN = 4
GROUPS = NT // GN
NODES = GN * P
NEG = -1e30
EPS = 1e-5
F1 = 2 * C
FFN = 1408
FK = FFN // P
SL = 32
HW = 4 * D + 4

F32 = mybir.dt.float32
BF16 = mybir.dt.bfloat16
I32 = mybir.dt.int32
ALU = mybir.AluOpType
ACT = mybir.ActivationFunctionType
AX = mybir.AxisListType
ROUND = 1.5 * 2.0 ** 23


class Memory:

    def __init__(self, nc, stack, prefix):
        self.nc, self.stack, self.prefix, self.sems = nc, stack, prefix, []
        stack.callback(self.clear)

    def clear(self):
        if self.sems:
            self.nc.clear_and_free_semaphores(self.sems)
            self.nc.all_engine_barrier()

    def sb(self, name, shape, dt=F32):
        return self.stack.enter_context(self.nc.sbuf_tensor(f"{self.prefix}_{name}", shape, dt))

    def ps(self, name, shape, dt=F32):
        return self.stack.enter_context(self.nc.psum_tensor(f"{self.prefix}_{name}", shape, dt))

    def sem(self, name):
        self.sems.append(self.nc.alloc_semaphore(f"{self.prefix}_{name}"))
        return self.sems[-1]


class Chain:

    def __init__(self, engine, sem, base=0):
        self.engine, self.sem, self.base, self.n = engine, sem, base, 0

    def then(self, ins):
        ins.then_inc(self.sem, 1)
        self.n += 1

    def wait(self):
        self.engine.wait_ge(self.sem, self.base + self.n)


def one(ap):
    return ap.rearrange("p o c -> p (o c)")


def make_constants(nc, mem, T):
    T["ident"] = mem.sb("ident", [P, P])
    T["identb"] = mem.sb("identb", [P, P], BF16)
    T["lane"] = mem.sb("lane", [P, P])
    T["laneb"] = mem.sb("laneb", [P, P], BF16)
    T["head_of"] = mem.sb("head_of", [P, H])
    T["of_head"] = mem.sb("of_head", [H, P])
    T["chunk_of"] = mem.sb("chunk_of", [P, CH])
    ident, identb, lane, laneb = T["ident"], T["identb"], T["lane"], T["laneb"]
    with ExitStack() as stack:
        m = Memory(nc, stack, "const")
        flip = m.ps("flip", [H, P])
        zeroed, built, masks, flipped, done = (m.sem(x) for x in ("zeroed", "built", "masks", "flipped", "done"))
        with nc.Block() as block:
            @block.gpsimd
            def _(pool):
                pool.memset(ident[:], 0.0).then_inc(zeroed, 1)
                pool.iota(lane[:], [[1, P]], base=0, channel_multiplier=0,
                          allow_small_or_imprecise_dtypes=True).then_inc(built, 1)
                pool.wait_ge(zeroed, 1)
                pool.affine_select(out=ident[:], in_=ident[:], compare_op=ALU.not_equal, fill=1.0, base=0,
                                   pattern=[[-1, P]], channel_multiplier=1).then_inc(built, 1)

            @block.vector
            def _(vec):
                vec.wait_ge(built, 2)
                vec.tensor_copy(identb[:], ident[:]).then_inc(done, 1)
                vec.tensor_copy(laneb[:], lane[:]).then_inc(done, 1)
                vec.tensor_reduce(T["head_of"][:], ident[:].rearrange("p (c h) -> p h c", h=H), AX.X,
                                  ALU.add).then_inc(masks, 1)
                vec.tensor_reduce(T["chunk_of"][:], ident[:].rearrange("p (c h) -> p c h", h=H), AX.X,
                                  ALU.add).then_inc(masks, 1)
                vec.wait_ge(flipped, 1)
                vec.tensor_copy(T["of_head"][:], flip[:]).then_inc(done, 1)

            @block.tensor
            def _(pe):
                pe.wait_ge(masks, 2)
                pe.transpose(flip[:], T["head_of"][:], ident[:]).then_inc(flipped, 1)


def share_edges(nc, mem, T):
    T["tile_of"] = mem.sb("tile_of", [P, SLOTS], I32)
    T["local"] = mem.sb("local", [P, SLOTS + U // 2])
    T["src"] = mem.sb("src", [P, SLOTS], I32)
    T["same"] = mem.sb("same", [P, RUN + 1], BF16)
    T["first"] = mem.sb("first", [P, RUN], BF16)
    T["last"] = mem.sb("last", [P, RUN], BF16)
    T["linked"] = mem.sb("linked", [H, 2 * CH, 2 * CH])


def index_edges(nc, a, T):
    with ExitStack() as stack:
        m = Memory(nc, stack, "index")
        raw = m.sb("raw", [P, 2, EK, P], I32)
        rows = m.sb("rows", [P, 2, EK, P])
        low = m.sb("low", [P, NT])
        junk = m.sb("junk", [P, EK * P])
        ones = m.sb("ones", [P, P])
        bound = m.sb("bound", [P, NT + 1])
        up = m.sb("up", [P, NT])
        ints = m.sb("ints", [P, 2, NT], I32)
        shifted = m.sb("shifted", [P, 2, NT], I32)
        flo = m.sb("flo", [P, NT])
        cnt = m.sb("cnt", [P, NT])
        some = m.sb("some", [P, NT])
        cum = m.sb("cum", [P, NT + 1])
        shift = m.sb("shift", [P, NT])
        dshift = m.sb("dshift", [P, NT])
        slot = m.sb("slot", [P, SLOTS])
        part = m.sb("part", [P, 1])
        tile_of = m.sb("tile_of", [P, SLOTS])
        etile = m.sb("etile", [P, SLOTS])
        step = m.sb("step", [P, SLOTS])
        pick = m.sb("pick", [P, EK, SLOTS])
        dst = m.sb("dst", [P, SLOTS])
        okl = m.sb("okl", [P, SLOTS])
        okh = m.sb("okh", [P, SLOTS])
        spread = m.sb("spread", [P, RUN])
        seg = m.sb("seg", [P, RUN])
        diff = m.sb("diff", [P, RUN])
        ends = m.sb("ends", [P, 2, CH])
        endv = m.sb("endv", [H, 2 * CH])
        neq = m.sb("neq", [H, 2 * CH, 2 * CH])
        psb = m.ps("psb", [P, NT])
        psd = m.ps("psd", [P, SLOTS])
        pss = m.ps("pss", [P, SLOTS])
        pse = m.ps("pse", [H, 2 * CH])
        pst = [m.ps(f"pst{i}", [P, 4 * P]) for i in range(2)]
        landed, filled, built, step_done, counted, summed, picked, placed, spread_done, turned, ends_done, ends_sum \
            = (m.sem(x) for x in ("landed", "filled", "built", "steps", "counted", "summed", "picked", "placed",
                                  "spread", "turned", "ends", "ends_sum"))
        copied = m.sem("copied")
        full = E // P - (EK - 1) * P
        rest = E % P
        flip_groups = [(g, min(4, G - g)) for g in range(0, G, 4)]
        with nc.Block() as block:
            @block.gpsimd
            def _(pool):
                pool.memset(raw[:, 0, :, :], -1).then_inc(filled, 1)
                pool.memset(raw[:, 1, :, :], 0).then_inc(filled, 1)
                pool.memset(ones[:], 1.0).then_inc(built, 1)
                pool.iota(slot[:], [[1, SLOTS]], base=0, channel_multiplier=0,
                          allow_small_or_imprecise_dtypes=True).then_inc(built, 1)
                pool.iota(part[:], [[0, 1]], base=0, channel_multiplier=1,
                          allow_small_or_imprecise_dtypes=True).then_inc(built, 1)

            @block.sync
            def _(sp):
                sp.wait_ge(filled, 2)
                whole = (EK - 1) * P * P
                for k, name in enumerate(("dst", "src")):
                    sp.dma_start(raw[:, k, 0:EK - 1, :],
                                 a[name][0:whole].rearrange("(k p e) -> p k e", p=P, e=P)).then_inc(landed, 16)
                    sp.dma_start(raw[0:full, k, EK - 1, :],
                                 a[name][whole:whole + full * P].rearrange("(p e) -> p e", e=P)).then_inc(landed, 16)
                    sp.dma_start(raw[full:full + 1, k, EK - 1, 0:rest],
                                 a[name][E - rest:E].rearrange("(p e) -> p e", p=1)).then_inc(landed, 16)

            @block.vector
            def _(vec):
                c = Chain(vec, step_done)
                vec.wait_ge(landed, 96)
                c.then(vec.tensor_scalar(rows[:, 0], raw[:, 0], 1.0, None, ALU.add))
                c.then(vec.tensor_copy(rows[:, 1], raw[:, 1]))
                c.wait()
                for d in range(NT):
                    c.then(vec.tensor_scalar(junk[:], rows[:, 0].rearrange("p k e -> p (k e)"),
                                             float(P * (d + 1)), 0.0, ALU.is_le, ALU.add,
                                             accum_out=low[:, d:d + 1]))
                    c.wait()
                vec.nop().then_inc(counted, 1)
                vec.wait_ge(summed, 1)
                c.then(vec.memset(bound[:, 0:1], 0.0))
                c.then(vec.tensor_scalar(bound[:, 1:NT + 1], psb[:], -float(EK * P * P - E), None, ALU.add))
                c.wait()
                c.then(vec.tensor_scalar(up[:], bound[:, 1:NT + 1], float(P - 1), None, ALU.add))
                c.then(vec.tensor_copy(ints[:, 0, :], bound[:, 0:NT]))
                c.then(vec.tensor_tensor(some[:], bound[:, 1:NT + 1], bound[:, 0:NT], ALU.is_gt))
                c.wait()
                c.then(vec.tensor_copy(ints[:, 1, :], up[:]))
                c.wait()
                c.then(vec.tensor_scalar(shifted[:], ints[:], 7, None, ALU.logical_shift_right))
                c.wait()
                c.then(vec.tensor_copy(flo[:], shifted[:, 0, :]))
                c.then(vec.tensor_tensor(cnt[:], shifted[:, 1, :], shifted[:, 0, :], ALU.subtract))
                c.wait()
                c.then(vec.tensor_tensor(cnt[:], cnt[:], some[:], ALU.mult))
                c.then(vec.memset(cum[:, 0:1], 0.0))
                c.wait()
                c.then(vec.tensor_tensor_scan(cum[:, 1:NT + 1], ones[:, 0:NT], cnt[:], 0.0, ALU.mult, ALU.add))
                c.wait()
                c.then(vec.tensor_tensor(shift[:], flo[:], cum[:, 0:NT], ALU.subtract))
                vec.wait_ge(built, 3)
                c.then(vec.memset(tile_of[:], 0.0))
                c.then(vec.tensor_copy(etile[:], slot[:]))
                c.wait()
                c.then(vec.tensor_tensor(dshift[:, 1:NT], shift[:, 1:NT], shift[:, 0:NT - 1], ALU.subtract))
                c.wait()
                for d in range(1, NT):
                    c.then(vec.scalar_tensor_tensor(out=tile_of[:], in0=slot[:], scalar=cum[:, d:d + 1],
                                                    in1=tile_of[:], op0=ALU.is_ge, op1=ALU.add))
                    c.then(vec.tensor_scalar(step[:], slot[:], cum[:, d:d + 1], dshift[:, d:d + 1], ALU.is_ge,
                                             ALU.mult))
                    c.wait()
                    c.then(vec.tensor_tensor(etile[:], etile[:], step[:], ALU.add))
                    c.wait()
                c.then(vec.tensor_copy(T["tile_of"][:], tile_of[:]))
                for k in range(EK):
                    c.then(vec.tensor_scalar(pick[:, k, :], etile[:], -float(P * k), part[:, 0:1], ALU.add,
                                             ALU.is_equal))
                c.wait()
                vec.nop().then_inc(picked, 1)
                vec.wait_ge(placed, 2)
                c.then(vec.memset(T["local"][:, SLOTS:], -1.0))
                c.then(vec.tensor_copy(T["src"][:], pss[:]))
                c.then(vec.tensor_scalar(dst[:], psd[:], -1.0, None, ALU.add))
                c.then(vec.tensor_scalar(step[:], tile_of[:], -float(P), None, ALU.mult))
                c.wait()
                c.then(vec.tensor_tensor(T["local"][:, 0:SLOTS], dst[:], step[:], ALU.add))
                c.wait()
                c.then(vec.tensor_scalar(okl[:], T["local"][:, 0:SLOTS], 0.0, None, ALU.is_ge))
                c.then(vec.tensor_scalar(okh[:], T["local"][:, 0:SLOTS], float(P), None, ALU.is_lt))
                c.then(vec.tensor_scalar(dst[:], dst[:], 1.0, None, ALU.add))
                c.wait()
                c.then(vec.tensor_tensor(okl[:], okl[:], okh[:], ALU.mult))
                c.wait()
                c.then(vec.tensor_tensor(dst[:], dst[:], okl[:], ALU.mult))
                c.wait()
                for cc in range(CH):
                    c.then(vec.tensor_copy(
                        spread[:].rearrange("p (g c h) -> p g c h", c=CH, h=H)[:, :, cc, :],
                        dst[:, cc * G:(cc + 1) * G].rearrange("p (g o) -> p g o", o=1).to_broadcast([P, G, H])))
                c.wait()
                vec.nop().then_inc(spread_done, 1)
                for n, (g, k) in enumerate(flip_groups):
                    vec.wait_ge(turned, n + 1)
                    vec.tensor_copy(seg[:, g * P:(g + k) * P], pst[n % 2][:, 0:k * P]).then_inc(copied, 1)
                vec.wait_ge(copied, len(flip_groups))
                same, first, last = T["same"], T["first"], T["last"]
                c.then(vec.memset(same[:, 0:1], NEG))
                c.then(vec.memset(same[:, RUN:RUN + 1], NEG))
                c.then(vec.tensor_tensor(diff[:, 1:RUN], seg[:, 1:RUN], seg[:, 0:RUN - 1], ALU.not_equal))
                c.then(vec.tensor_scalar(first[:], seg[:], seg[:, 0:1], NEG, ALU.not_equal, ALU.mult))
                c.then(vec.tensor_scalar(last[:], seg[:], seg[:, RUN - 1:RUN], NEG, ALU.not_equal, ALU.mult))
                c.then(vec.tensor_scalar(ends[:, 0, :], T["chunk_of"][:], seg[:, 0:1], None, ALU.mult))
                c.then(vec.tensor_scalar(ends[:, 1, :], T["chunk_of"][:], seg[:, RUN - 1:RUN], None, ALU.mult))
                c.wait()
                vec.nop().then_inc(ends_done, 1)
                c.then(vec.tensor_scalar(same[:, 1:RUN], diff[:, 1:RUN], NEG, None, ALU.mult))
                vec.wait_ge(ends_sum, 1)
                c.then(vec.tensor_copy(endv[:], pse[:]))
                c.wait()
                c.then(vec.tensor_tensor(neq[:], endv[:].unsqueeze(2).to_broadcast([H, 2 * CH, 2 * CH]),
                                         endv[:].unsqueeze(1).to_broadcast([H, 2 * CH, 2 * CH]), ALU.not_equal))
                c.wait()
                c.then(vec.tensor_scalar(T["linked"][:], neq[:], NEG, None, ALU.mult))
                c.wait()

            @block.tensor
            def _(pe):
                pe.wait_ge(built, 3)
                pe.wait_ge(counted, 1)
                pe.matmul(psb[:], ones[:], low[:], start=True, stop=True).then_inc(summed, 1)
                pe.wait_ge(picked, 1)
                for k, out in ((0, psd), (1, pss)):
                    for b in range(EK):
                        last = pe.matmul(out[:], rows[:, k, b, :], pick[:, b, :], start=(b == 0), stop=(b == EK - 1))
                    last.then_inc(placed, 1)
                pe.wait_ge(spread_done, 1)
                for n, (g, k) in enumerate(flip_groups):
                    if n >= 2:
                        pe.wait_ge(copied, n - 1)
                    for j in range(k):
                        last = pe.transpose(pst[n % 2][:, j * P:(j + 1) * P], spread[:, (g + j) * P:(g + j + 1) * P],
                                            T["ident"][:])
                    last.then_inc(turned, 1)
                pe.wait_ge(ends_done, 1)
                pe.matmul(pse[:], T["head_of"][:], ends[:].rearrange("p e c -> p (e c)"), start=True,
                          stop=True).then_inc(ends_sum, 1)


def normalise_input(nc, a, xn_dram):
    with ExitStack() as stack:
        m = Memory(nc, stack, "ln0")
        x = m.sb("x", [P, NT, C])
        stats = m.sb("stats", [P, NT, 6])
        mv = m.sb("mv", [P, NT, 2])
        eps = m.sb("eps", [P, 1])
        std = m.sb("std", [P, NT])
        rstd = m.sb("rstd", [P, NT])
        zeroed, landed, steps, have_mv, have_std, normed, stored = (
            m.sem(x_) for x_ in ("zeroed", "landed", "steps", "have_mv", "have_std", "normed", "stored"))
        with nc.Block() as block:
            @block.gpsimd
            def _(pool):
                pool.memset(x[:, NT - 1, :], 0.0).then_inc(zeroed, 1)
                pool.memset(eps[:], EPS).then_inc(zeroed, 1)

            @block.sync
            def _(sp):
                sp.wait_ge(zeroed, 1)
                sp.dma_start(x[:, 0:NT - 1, :],
                             a["x"][0:(NT - 1) * P, :].rearrange("(t p) c -> p t c", p=P)).then_inc(landed, 16)
                sp.dma_start(x[0:LAST, NT - 1, :], a["x"][(NT - 1) * P:N, :]).then_inc(landed, 16)
                sp.wait_ge(normed, NT)
                sp.dma_start(xn_dram.rearrange("(t p) c -> p t c", p=P), x[:]).then_inc(stored, 16)
                sp.wait_ge(stored, 16)

            @block.vector
            def _(vec):
                vec.wait_ge(landed, 32)
                for t in range(NT):
                    vec.bn_stats(stats[:, t, :], x[:, t, :]).then_inc(steps, 1)
                vec.wait_ge(steps, NT)
                for t in range(NT):
                    vec.bn_aggr(mv[:, t, :], stats[:, t, :]).then_inc(have_mv, 1)
                vec.wait_ge(have_std, 1)
                vec.reciprocal(rstd[:], std[:]).then_inc(steps, 1)
                vec.wait_ge(steps, NT + 1)
                vec.wait_ge(have_mv, NT)
                for t in range(NT):
                    vec.tensor_scalar(x[:, t, :], x[:, t, :], mv[:, t, 0:1], rstd[:, t:t + 1], ALU.subtract,
                                      ALU.mult).then_inc(normed, 1)

            @block.scalar
            def _(act):
                act.wait_ge(zeroed, 2)
                act.wait_ge(have_mv, NT)
                act.activation(std[:], mv[:, :, 1], ACT.Sqrt, bias=eps[:, 0:1]).then_inc(have_std, 1)


def turns(engine, n, body):
    body(0)
    with engine.Fori(1, n) as t:
        body(t)


def later(t):
    return not isinstance(t, int) or t > 0


def project_nodes(nc, a, T, layer, x_dram, enc_dram, k_dram, v_dram, base_dram):
    with ExitStack() as stack:
        m = Memory(nc, stack, f"proj{layer}")
        names = ("s", "k", "v", "q")
        S_, K_, V_, Q_ = range(4)
        w = m.sb("w", [P, 4, KC, C])
        bias = m.sb("bias", [P, 4, C])
        x = m.sb("x", [P, 2, C])
        enc = m.sb("enc", [P, 2, C])
        xT = m.sb("xT", [P, 2, KC, P])
        out = m.sb("out", [P, 2, 4, C])
        psT = [m.ps(f"psT{i}", [P, KC * P]) for i in range(2)]
        psP = [m.ps(f"psP{i}", [P, C]) for i in range(4)]
        w_in = m.sem("w_in")
        x_in = [m.sem(f"x_in{b}") for b in range(2)]
        enc_in = [m.sem(f"enc_in{b}") for b in range(2)]
        kv_out = [m.sem(f"kv_out{b}") for b in range(2)]
        base_out = [m.sem(f"base_out{b}") for b in range(2)]
        turned, xT_ready, projected, ready, split, summed = (
            m.sem(s) for s in ("turned", "xT_ready", "projected", "ready", "split", "summed"))
        qp = T["q_parts"]
        T2 = NT // 2
        with nc.Block() as block:
            @block.sync
            def _(sp):
                for j, n in enumerate(names):
                    sp.dma_start(w[:, j], a[f"L0_gnn_W{n}"][layer].rearrange("(k p) n -> p k n", p=P)).then_inc(w_in, 16)
                    sp.dma_start(bias[:, j], a[f"L0_gnn_b{n}"][layer, :].partition_broadcast(P)).then_inc(w_in, 16)

                def pair(t):
                    for b in range(2):
                        if later(t):
                            sp.wait_ge(turned, t * 2 + b - 1)
                        sp.dma_start(x[:, b, :], x_dram[bass.ds((t * 2 + b) * P, P), :]).then_inc(x_in[b], 16)
                    for b in range(2):
                        if later(t):
                            sp.wait_ge(base_out[b], t * 16)
                        sp.dma_start(enc[:, b, :], enc_dram[bass.ds((t * 2 + b) * P, P), :]).then_inc(enc_in[b], 16)
                    for b in range(2):
                        sp.wait_ge(summed, t * 2 + b + 1)
                        sp.dma_start(base_dram[bass.ds((t * 2 + b) * P, P), :], enc[:, b, :]).then_inc(base_out[b], 16)
                turns(sp, T2, pair)
                for b in range(2):
                    sp.wait_ge(base_out[b], 16 * T2)

            @block.tensor
            def _(pe):
                pe.wait_ge(w_in, 16 * 8)

                def pair(t):
                    for b in range(2):
                        pe.wait_ge(x_in[b], t * 16 + 16)
                        for k in range(KC):
                            last = pe.transpose(psT[b][:, k * P:(k + 1) * P], x[:, b, k * P:(k + 1) * P], T["ident"][:])
                        last.then_inc(turned, 1)
                    for b in range(2):
                        pe.wait_ge(xT_ready, t * 2 + b + 1)
                        for j in range(4):
                            if later(t) or b:
                                pe.wait_ge(ready, t * 8 + b * 4 + j - 3)
                            for k in range(KC):
                                last = pe.matmul(psP[j][:], xT[:, b, k, :], w[:, j, k, :], start=(k == 0),
                                                 stop=(k == KC - 1))
                            last.then_inc(projected, 1)
                turns(pe, T2, pair)

            @block.scalar
            def _(act):
                def pair(t):
                    for b in range(2):
                        act.wait_ge(turned, t * 2 + b + 1)
                        act.copy(xT[:, b].rearrange("p k n -> p (k n)"), psT[b][:]).then_inc(xT_ready, 1)
                    for b in range(2):
                        for j, dram in ((K_, k_dram), (V_, v_dram)):
                            act.wait_ge(ready, t * 8 + b * 4 + j + 1)
                            act.dma_start(dram[bass.ds((t * 2 + b) * P, P), :], out[:, b, j, :]).then_inc(kv_out[b], 16)
                turns(act, T2, pair)
                for b in range(2):
                    act.wait_ge(kv_out[b], 32 * T2)

            @block.vector
            def _(vec):
                vec.wait_ge(w_in, 16 * 8)

                def pair(t):
                    for b in range(2):
                        i = t * 2 + b
                        for j in range(4):
                            if later(t):
                                if j == S_:
                                    vec.wait_ge(summed, i - 1)
                                elif j == K_:
                                    vec.wait_ge(kv_out[b], t * 32)
                            vec.wait_ge(projected, t * 8 + b * 4 + j + 1)
                            vec.tensor_tensor(out[:, b, j, :], psP[j][:], bias[:, j, :], ALU.add).then_inc(ready, 1)
                        c = Chain(vec, split, i * 5)
                        q = out[:, b, Q_, :]
                        part = [one(qp[:, k, bass.ds(i, 1), :]) for k in range(3)]
                        vec.wait_ge(ready, t * 8 + b * 4 + Q_ + 1)
                        for k in range(2):
                            c.then(vec.tensor_scalar(part[k], q, 1.0, None, ALU.mult))
                            c.wait()
                            c.then(vec.tensor_tensor(q, q, part[k], ALU.subtract))
                            c.wait()
                        c.then(vec.tensor_scalar(part[2], q, 1.0, None, ALU.mult))
                turns(vec, T2, pair)

            @block.gpsimd
            def _(pool):
                def pair(t):
                    for b in range(2):
                        pool.wait_ge(enc_in[b], t * 16 + 16)
                        pool.wait_ge(ready, t * 8 + b * 4 + S_ + 1)
                        pool.tensor_tensor(enc[:, b, :], enc[:, b, :], out[:, b, S_, :], ALU.add).then_inc(summed, 1)
                turns(pool, T2, pair)


def gather(pool, T, t, half, bufs, index, table, landed, copied, started, freed, later_):
    h = U // 2
    if later_:
        pool.wait_ge(freed, (t - 1) * U + half * h + h)
    pool.tensor_copy(index[:, half, :], T["src"][:, bass.ds(t * U + half * h, h)]).then_inc(copied, 1)
    pool.wait_ge(copied, t * 2 + half + 1)
    pool.sem_inc(started, 1)
    for u in range(half * h, half * h + h):
        pool.indirect_dma_start(bufs[:, u, :], None, table,
                                bass.IndirectOffsetOnAxis(ap=index[:, half, u - half * h:u - half * h + 1], axis=0)
                                ).then_inc(landed[u], 16)


def score_edges(nc, a, T, layer, k_dram, scores):
    with ExitStack() as stack:
        m = Memory(nc, stack, f"score{layer}")
        h, B = U // 2, 4
        kbuf = m.sb("kbuf", [P, U, C])
        index = m.sb("index", [P, 2, h], I32)
        hot = m.sb("hot", [P, U, P], BF16)
        hotT = m.sb("hotT", [P, 2, B, P], BF16)
        prod = m.sb("prod", [P, 2, B, C])
        found = m.sb("found", [P, U, H])
        psT = [m.ps(f"psT{i}", [P, B, P], BF16) for i in range(2)]
        psQ = [m.ps(f"psQ{i}", [P, C]) for i in range(B)]
        landed = [m.sem(f"landed{u}") for u in range(U)]
        copied, hots, turned, hotT_ready, queried, multiplied, reduced, kept = (
            m.sem(x) for x in ("copied", "hots", "turned", "hotT_ready", "queried", "multiplied", "reduced", "kept"))
        started = m.sem("started")
        qp, local = T["q_parts"], T["local"]
        with nc.Block() as block:
            @block.gpsimd
            def _(pool):
                def turn(t):
                    for half in range(2):
                        gather(pool, T, t, half, kbuf, index, k_dram, landed, copied, started, multiplied, later(t))
                turns(pool, TURNS, turn)

            @block.vector
            def _(vec):
                def one_hot(slot, u, sem_value=None):
                    if sem_value is not None:
                        vec.wait_ge(turned, sem_value)
                    vec.tensor_scalar(hot[:, u, :], T["laneb"][:], local[:, bass.ds(slot, 1)], None,
                                      ALU.is_equal).then_inc(hots, 1)

                for u in range(h):
                    one_hot(u, u)

                def turn(t):
                    for j in range(U // B):
                        for u in range(j * B + h, j * B + h + B):
                            before = t * (U // B) + j + 2 - U // B + 1
                            first = u % B == 0
                            one_hot(t * U + u, u % U, before if first and (later(t) or u >= U) else None)
                        pb = j % 2
                        for i in range(B):
                            u = j * B + i
                            vec.wait_ge(landed[u], t * 16 + 16)
                            vec.wait_ge(queried, t * U + u + 1)
                            vec.tensor_tensor(prod[:, pb, i, :], psQ[i][:], kbuf[:, u, :],
                                              ALU.mult).then_inc(multiplied, 1)
                        vec.wait_ge(multiplied, t * U + j * B + B)
                        if later(t) and j == 0:
                            vec.wait_ge(kept, t)
                        vec.tensor_reduce(found[:, j * B:(j + 1) * B, :],
                                          prod[:, pb].rearrange("p i (h d) -> p i h d", h=H), AX.X,
                                          ALU.add).then_inc(reduced, 1)
                    vec.wait_ge(reduced, t * (U // B) + U // B)
                    vec.tensor_scalar(scores[:, bass.ds(t * U * H, U * H)], found[:].rearrange("p u h -> p (u h)"),
                                      1.0, None, ALU.mult).then_inc(kept, 1)
                turns(vec, TURNS, turn)

            @block.tensor
            def _(pe):
                def flip(batch, j):
                    pe.wait_ge(hots, batch * B + B)
                    for i in range(B):
                        last = pe.transpose(psT[j % 2][:, i, :], hot[:, (j * B + i) % U, :], T["identb"][:])
                    last.then_inc(turned, 1)

                flip(0, 0)

                def turn(t):
                    for j in range(U // B):
                        batch = t * (U // B) + j
                        flip(batch + 1, j + 1)
                        pe.wait_ge(hotT_ready, batch + 1)
                        for i in range(B):
                            u = j * B + i
                            d = pe.value_load(T["tile_of"][0:1, bass.ds(t * U + u, 1)], min_val=0, max_val=NT - 1)
                            if later(t) or j:
                                pe.wait_ge(multiplied, t * U + u - B + 1)
                            for k in range(3):
                                last = pe.matmul(psQ[i][:], hotT[:, j % 2, i, :], one(qp[:, k, bass.ds(d, 1), :]),
                                                 start=(k == 0), stop=(k == 2))
                            last.then_inc(queried, 1)
                turns(pe, TURNS, turn)

            @block.scalar
            def _(act):
                def turn(t):
                    for j in range(U // B):
                        batch = t * (U // B) + j
                        act.wait_ge(turned, batch + 1)
                        if later(t) or j >= 2:
                            act.wait_ge(queried, batch * B - B)
                        act.copy(hotT[:, j % 2].rearrange("p i e -> p (i e)"),
                                 psT[j % 2][:].rearrange("p i e -> p (i e)")).then_inc(hotT_ready, 1)
                turns(act, TURNS, turn)


def soften(nc, T, layer, scores, weights):
    with ExitStack() as stack:
        m = Memory(nc, stack, f"soft{layer}")
        near = m.sb("near", [P, G, P])
        rows = m.sb("rows", [P, RUN])
        run = m.sb("run", [P, RUN])
        top = m.sb("top", [P, RUN])
        ends = m.sb("ends", [P, 2, CH])
        pair = m.sb("pair", [H, 2 * CH, 2 * CH])
        best = m.sb("best", [H, 2 * CH])
        back = m.sb("back", [P, 2, CH])
        shared = m.sb("shared", [P, 2])
        pst = [m.ps(f"pst{i}", [P, 4, P]) for i in range(2)]
        psw = [m.ps(f"psw{i}", [P, 4, P]) for i in range(2)]
        pse = m.ps("pse", [H, 2 * CH])
        psb = m.ps("psb", [P, 2 * CH])
        nearby = m.sem("nearby")
        turned, in_rows, steps, ends_done, ends_in, best_done, best_out, ready, exped, returned, stored = (
            m.sem(x) for x in ("turned", "in_rows", "steps", "ends_done", "ends_in", "best_done", "best_out", "ready",
                               "exped", "returned", "stored"))
        parts = [(g, min(4, G - g)) for g in range(0, G, 4)]
        by_g = scores[:].rearrange("p (c g h) -> p g c h", c=CH, g=G)
        w_by_g = weights[:].rearrange("p (c g h) -> p g c h", c=CH, g=G)
        with nc.Block() as block:
            @block.tensor
            def _(pe):
                for n, (g, k) in enumerate(parts):
                    pe.wait_ge(nearby, n + 1)
                    if n >= 2:
                        pe.wait_ge(in_rows, n - 1)
                    for j in range(k):
                        last = pe.transpose(pst[n % 2][:, j, :], near[:, g + j, :], T["ident"][:])
                    last.then_inc(turned, 1)
                pe.wait_ge(ends_done, 1)
                pe.matmul(pse[:], T["head_of"][:], ends[:].rearrange("p e c -> p (e c)"), start=True,
                          stop=True).then_inc(ends_in, 1)
                pe.wait_ge(best_done, 1)
                pe.matmul(psb[:], T["of_head"][:], best[:], start=True, stop=True).then_inc(best_out, 1)
                for n, (g, k) in enumerate(parts):
                    pe.wait_ge(exped, n + 1)
                    if n >= 2:
                        pe.wait_ge(stored, n - 1)
                    for j in range(k):
                        last = pe.transpose(psw[n % 2][:, j, :], rows[:, (g + j) * P:(g + j + 1) * P], T["ident"][:])
                    last.then_inc(returned, 1)

            @block.scalar
            def _(act):
                for n, (g, k) in enumerate(parts):
                    act.copy(near[:, g:g + k, :].rearrange("p k (c h) -> p k c h", c=CH), by_g[:, g:g + k]
                             ).then_inc(nearby, 1)
                for n, (g, k) in enumerate(parts):
                    act.wait_ge(ready, n + 1)
                    act.activation(rows[:, g * P:(g + k) * P], rows[:, g * P:(g + k) * P], ACT.Exp,
                                   scale=float(D) ** -0.5).then_inc(exped, 1)

            @block.vector
            def _(vec):
                c = Chain(vec, steps)
                same, first, last = T["same"], T["first"], T["last"]
                for n, (g, k) in enumerate(parts):
                    vec.wait_ge(turned, n + 1)
                    vec.tensor_copy(rows[:, g * P:(g + k) * P], pst[n % 2][:, 0:k, :].rearrange("p k e -> p (k e)")
                                    ).then_inc(in_rows, 1)
                vec.wait_ge(in_rows, len(parts))
                c.then(vec.tensor_tensor_scan(run[:], same[:, 0:RUN], rows[:], NEG, ALU.add, ALU.max))
                c.wait()
                c.then(vec.tensor_tensor_scan(top[:, RUN - 1::-1], same[:, RUN:0:-1], run[:, RUN - 1::-1], NEG,
                                              ALU.add, ALU.max))
                c.wait()
                c.then(vec.tensor_scalar(ends[:, 0, :], T["chunk_of"][:], top[:, 0:1], None, ALU.mult))
                c.then(vec.tensor_scalar(ends[:, 1, :], T["chunk_of"][:], top[:, RUN - 1:RUN], None, ALU.mult))
                c.wait()
                vec.nop().then_inc(ends_done, 1)
                vec.wait_ge(ends_in, 1)
                c.then(vec.tensor_tensor(pair[:], T["linked"][:],
                                         pse[:].unsqueeze(1).to_broadcast([H, 2 * CH, 2 * CH]), ALU.add))
                c.wait()
                vec.tensor_reduce(best[:], pair[:], AX.X, ALU.max).then_inc(best_done, 1)
                vec.wait_ge(best_out, 1)
                c.then(vec.tensor_tensor(back[:], psb[:].rearrange("p (e c) -> p e c", e=2),
                                         T["chunk_of"][:].unsqueeze(1).to_broadcast([P, 2, CH]), ALU.mult))
                c.wait()
                c.then(vec.tensor_reduce(shared[:], back[:], AX.X, ALU.add))
                c.wait()
                c.then(vec.scalar_tensor_tensor(out=top[:], in0=first[:], scalar=shared[:, 0:1], in1=top[:],
                                                op0=ALU.add, op1=ALU.max))
                c.wait()
                c.then(vec.scalar_tensor_tensor(out=top[:], in0=last[:], scalar=shared[:, 1:2], in1=top[:],
                                                op0=ALU.add, op1=ALU.max))
                c.wait()
                for n, (g, k) in enumerate(parts):
                    s = slice(g * P, (g + k) * P)
                    vec.tensor_tensor(rows[:, s], rows[:, s], top[:, s], ALU.subtract).then_inc(ready, 1)
                for n, (g, k) in enumerate(parts):
                    vec.wait_ge(returned, n + 1)
                    vec.tensor_copy(w_by_g[:, g:g + k], psw[n % 2][:, 0:k, :].rearrange("p k (c h) -> p k c h", c=CH)
                                    ).then_inc(stored, 1)


def aggregate(nc, a, T, layer, v_dram, weights, agg):
    with ExitStack() as stack:
        m = Memory(nc, stack, f"agg{layer}")
        h, B, R = U // 2, 4, 4
        vbuf = m.sb("vbuf", [P, U, C])
        index = m.sb("index", [P, 2, h], I32)
        hot = m.sb("hot", [P, U, P])
        wt = m.sb("wt", [P, U, H])
        wv = m.sb("wv", [P, R, 2, HW])
        psA = [m.ps(f"psA{i}", [P, 2, C]) for i in range(4)]
        landed = [m.sem(f"landed{u}") for u in range(U)]
        copied, hots, staged, sums_in, weighted, added, summed, cleared = (
            m.sem(x) for x in ("copied", "hots", "staged", "sums_in", "weighted", "added", "summed", "cleared"))
        started = m.sem("started")
        local = T["local"]
        with nc.Block() as block:
            @block.gpsimd
            def _(pool):
                pool.memset(agg[:], 0.0).then_inc(cleared, 1)

                def turn(t):
                    for half in range(2):
                        gather(pool, T, t, half, vbuf, index, v_dram, landed, copied, started, weighted, later(t))
                turns(pool, TURNS, turn)

            @block.vector
            def _(vec):
                vec.wait_ge(cleared, 1)

                def add(slot, u):
                    d = vec.value_load(T["tile_of"][0:1, bass.ds(slot, 1)], min_val=0, max_val=NT - 1)
                    at = agg[:, bass.ds(d, 1), :, :].rearrange("p o e w -> p (o e) w")
                    vec.wait_ge(summed, slot + 1)
                    if later(slot):
                        vec.wait_ge(added, slot)
                    vec.tensor_tensor(at, at, psA[u % 4][:, :, 0:HW], ALU.add).then_inc(added, 1)

                def stage(t):
                    vec.tensor_scalar(wt[:].rearrange("p u h -> p (u h)"), weights[:, bass.ds(t * U * H, U * H)],
                                      1.0, None, ALU.mult).then_inc(staged, 1)
                    vec.wait_ge(staged, t + 1)

                def turn(t):
                    if later(t):
                        vec.wait_ge(sums_in, t * U)
                        vec.wait_ge(weighted, t * U)
                    stage(t)
                    for u in range(U):
                        if later(t):
                            vec.wait_ge(summed, t * U + u + 1 - U)
                        vec.tensor_scalar(hot[:, u, :], T["lane"][:], local[:, bass.ds(t * U + u, 1)], None,
                                          ALU.is_equal).then_inc(hots, 1)
                        if later(t) or u >= R:
                            vec.wait_ge(summed, t * U + u + 1 - R)
                        vec.wait_ge(landed[u], t * 16 + 16)
                        vec.tensor_tensor(wv[:, u % R, :, 0:4 * D].rearrange("p e (h d) -> p e h d", h=4),
                                          vbuf[:, u, :].rearrange("p (e h d) -> p e h d", e=2, h=4),
                                          wt[:, u, :].rearrange("p (e h) -> p e h", e=2).unsqueeze(3)
                                          .to_broadcast([P, 2, 4, D]), ALU.mult).then_inc(weighted, 1)
                        if later(t) or u >= 2:
                            add(t * U + u - 2, (u - 2) % 4)
                turns(vec, TURNS, turn)
                for s in (SLOTS - 2, SLOTS - 1):
                    add(s, s % 4)

            @block.scalar
            def _(act):
                def turn(t):
                    act.wait_ge(staged, t + 1)
                    for u in range(U):
                        if later(t) or u >= R:
                            act.wait_ge(summed, t * U + u + 1 - R)
                        act.copy(wv[:, u % R, :, 4 * D:HW], wt[:, u, :].rearrange("p (e h) -> p e h", e=2)
                                 ).then_inc(sums_in, 1)
                turns(act, TURNS, turn)

            @block.tensor
            def _(pe):
                def turn(t):
                    for u in range(U):
                        pe.wait_ge(hots, t * U + u + 1)
                        pe.wait_ge(weighted, t * U + u + 1)
                        pe.wait_ge(sums_in, t * U + u + 1)
                        if later(t) or u >= 4:
                            pe.wait_ge(added, t * U + u - 3)
                        for e in range(2):
                            last = pe.matmul(psA[u % 4][:, e, 0:HW], hot[:, u, :], wv[:, u % R, e, :], start=True,
                                             stop=True)
                        last.then_inc(summed, 1)
                turns(pe, TURNS, turn)


def combine(nc, a, T, layer, agg, base_dram, out_dram):
    final = layer == LAYERS - 1
    with ExitStack() as stack:
        m = Memory(nc, stack, f"comb{layer}")
        x = m.sb("x", [P, NT, C])
        den = m.sb("den", [P, NT, 2, 4])
        gb = m.sb("gb", [P, 2, C])
        landed, steps, done, stored = (m.sem(s) for s in ("landed", "steps", "done", "stored"))
        ln = LayerNorm(nc, m, NT) if final else None
        with nc.Block() as block:
            @block.sync
            def _(sp):
                sp.dma_start(x[:], base_dram.rearrange("(t p) c -> p t c", p=P)).then_inc(landed, 16)
                if final:
                    sp.dma_start(gb[:, 0], a["L0_gnn_ln_g"].partition_broadcast(P)).then_inc(landed, 16)
                    sp.dma_start(gb[:, 1], a["L0_gnn_ln_b"].partition_broadcast(P)).then_inc(landed, 16)
                for t in range(NT):
                    sp.wait_ge(done, t + 1)
                    sp.dma_start(out_dram[t * P:(t + 1) * P, :], x[:, t, :]).then_inc(stored, 16)
                sp.wait_ge(stored, 16 * NT)

            @block.vector
            def _(vec):
                c = Chain(vec, steps)
                c.then(vec.tensor_scalar(den[:].rearrange("p t e h -> p (t e) h"),
                                         agg[:, :, :, 4 * D:HW].rearrange("p t e h -> p (t e) h"), 1e-16, None, ALU.add))
                c.wait()
                c.then(vec.reciprocal(den[:], den[:]))
                c.wait()
                for t in range(NT):
                    at = agg[:, t, :, 0:4 * D].rearrange("p e (h d) -> p e h d", h=4)
                    c.then(vec.tensor_tensor(at, at, den[:, t].unsqueeze(3).to_broadcast([P, 2, 4, D]), ALU.mult))
                vec.wait_ge(landed, 48 if final else 16)
                c.wait()
                for t in range(NT):
                    ins = vec.tensor_tensor(x[:, t, :].rearrange("p (e w) -> p e w", e=2),
                                            x[:, t, :].rearrange("p (e w) -> p e w", e=2), agg[:, t, :, 0:4 * D], ALU.add)
                    if final:
                        c.then(ins)
                    else:
                        ins.then_inc(done, 1)
                if final:
                    c.wait()
                    ln.stats(vec, lambda t: x[:, t, :])
                    ln.scale(vec)
                    for t in range(NT):
                        c.then(ln.apply(vec, t, x[:, t, :], x[:, t, :]))
                    c.wait()
                    for t in range(NT):
                        c.then(vec.tensor_tensor(x[:, t, :], x[:, t, :], gb[:, 0], ALU.mult))
                    c.wait()
                    for t in range(NT):
                        vec.tensor_tensor(x[:, t, :], x[:, t, :], gb[:, 1], ALU.add).then_inc(done, 1)

            @block.gpsimd
            def _(pool):
                if final:
                    ln.set_eps(pool)

            @block.scalar
            def _(act):
                if final:
                    ln.root(act)


class LayerNorm:

    def __init__(self, nc, m, n):
        self.n = n
        self.st = m.sb("ln_stats", [P, n, 6])
        self.mv = m.sb("ln_mv", [P, n, 2])
        self.eps = m.sb("ln_eps", [P, 1])
        self.std = m.sb("ln_std", [P, n])
        self.rstd = m.sb("ln_rstd", [P, n])
        self.all_st = m.sem("ln_all_st")
        self.have_eps, self.have_st, self.have_mv, self.have_std, self.have_rstd = (
            m.sem(x) for x in ("ln_have_eps", "ln_have_st", "ln_have_mv", "ln_have_std", "ln_have_rstd"))

    def set_eps(self, engine):
        engine.memset(self.eps[:], EPS).then_inc(self.have_eps, 1)

    def stats(self, vec, row, turn=0):
        for t in range(self.n):
            vec.bn_stats(self.st[:, t, :], row(t)).then_inc(self.have_st, 1)
        vec.wait_ge(self.have_st, (turn + 1) * self.n)
        vec.sem_inc(self.all_st, 1)
        for t in range(self.n):
            vec.bn_aggr(self.mv[:, t, :], self.st[:, t, :]).then_inc(self.have_mv, 1)

    def root(self, act, turn=0):
        if isinstance(turn, int) and turn == 0:
            act.wait_ge(self.have_eps, 1)
        act.wait_ge(self.have_mv, (turn + 1) * self.n)
        act.activation(self.std[:], self.mv[:, :, 1], ACT.Sqrt, bias=self.eps[:, 0:1]).then_inc(self.have_std, 1)

    def scale(self, vec, turn=0):
        vec.wait_ge(self.have_std, turn + 1)
        vec.reciprocal(self.rstd[:], self.std[:]).then_inc(self.have_rstd, 1)
        vec.wait_ge(self.have_rstd, turn + 1)
        vec.wait_ge(self.have_mv, (turn + 1) * self.n)

    def apply(self, vec, t, out, in_):
        return vec.tensor_scalar(out, in_, self.mv[:, t, 0:1], self.rstd[:, t:t + 1], ALU.subtract, ALU.mult)


def turn_group(pe, T, tile, psT, turned, free, wait_free):
    for n in range(GN):
        if wait_free(n) is not None:
            pe.wait_ge(free, wait_free(n))
        for k in range(KC):
            last = pe.transpose(psT[n % 2][:, k, :], tile[:, n, k * P:(k + 1) * P], T["ident"][:])
        last.then_inc(turned, 1)


def node_mlp(nc, a, T, y_dram, enc_dram, out_dram):
    with ExitStack() as stack:
        m = Memory(nc, stack, "mlp")
        FC = F1 // P
        w1 = m.sb("w1", [P, KC, F1])
        w2 = m.sb("w2", [P, FC, C])
        b1 = m.sb("b1", [P, FC])
        rowsb = m.sb("rowsb", [P, 3, C])
        y = m.sb("y", [P, GN, C])
        yres = m.sb("yres", [P, GN, C])
        enc = m.sb("enc", [P, GN, C])
        yT = m.sb("yT", [P, KC, NODES])
        hT = m.sb("hT", [P, FC, NODES])
        z = m.sb("z", [P, GN, C])
        psT = [m.ps(f"psT{i}", [P, KC, P]) for i in range(2)]
        psH = [m.ps(f"psH{i}", [P, NODES]) for i in range(2)]
        psO = [m.ps(f"psO{i}", [P, C]) for i in range(2)]
        w_in, y_in, yres_in, enc_in, turned, yT_in, hidden, hT_in, out_done, z_in, steps, done, stored = (
            m.sem(s) for s in ("w_in", "y_in", "yres_in", "enc_in", "turned", "yT_in", "hidden", "hT_in", "out_done",
                               "z_in", "steps", "done", "stored"))
        ln = LayerNorm(nc, m, GN)

        def rows_of(dram, g):
            return dram[bass.ds(g * NODES, NODES), :].rearrange("(t p) c -> p t c", p=P)

        def over(j):
            return rowsb[:, j, :].unsqueeze(1).to_broadcast([P, GN, C])

        with nc.Block() as block:
            @block.sync
            def _(sp):
                sp.dma_start(w1[:], a["L0_gnn_W1"].rearrange("(k p) n -> p k n", p=P)).then_inc(w_in, 16)
                sp.dma_start(w2[:], a["L0_gnn_W2"].rearrange("(k p) n -> p k n", p=P)).then_inc(w_in, 16)
                sp.dma_start(b1[:], a["L0_gnn_b1"].rearrange("(f p) -> p f", p=P), allow_slow_non_contiguous=True).then_inc(w_in, 16)
                for j, n in enumerate(("b2", "ln_g", "ln_b")):
                    sp.dma_start(rowsb[:, j], a[f"L0_gnn_{n}"].partition_broadcast(P)).then_inc(w_in, 16)

                def group(g):
                    if later(g):
                        sp.wait_ge(turned, g * GN)
                    sp.dma_start(y[:], rows_of(y_dram, g)).then_inc(y_in, 16)
                    if later(g):
                        sp.wait_ge(z_in, g * GN)
                        sp.wait_ge(done, g)
                        sp.dma_start(rows_of(out_dram, g - 1), z[:]).then_inc(stored, 16)
                    sp.dma_start(yres[:], rows_of(y_dram, g)).then_inc(yres_in, 16)
                    sp.dma_start(enc[:], rows_of(enc_dram, g)).then_inc(enc_in, 16)
                turns(sp, GROUPS, group)
                sp.wait_ge(done, GROUPS)
                sp.dma_start(rows_of(out_dram, GROUPS - 1), z[:]).then_inc(stored, 16)
                sp.wait_ge(stored, 16 * GROUPS)

            @block.tensor
            def _(pe):
                pe.wait_ge(w_in, 16 * 6)

                def group(g):
                    pe.wait_ge(y_in, g * 16 + 16)
                    turn_group(pe, T, y, psT, turned, yT_in, lambda n: g * GN + n - 1 if n >= 2 else
                               (g * GN + n - 1 if later(g) else None))
                    pe.wait_ge(yT_in, g * GN + GN)
                    for f in range(FC):
                        if later(g) or f >= 2:
                            pe.wait_ge(hT_in, g * FC + f - 1)
                        for k in range(KC):
                            last = pe.matmul(psH[f % 2][:], w1[:, k, f * P:(f + 1) * P], yT[:, k, :], start=(k == 0),
                                             stop=(k == KC - 1))
                        last.then_inc(hidden, 1)
                    pe.wait_ge(hT_in, g * FC + FC)
                    for n in range(GN):
                        if later(g) or n >= 2:
                            pe.wait_ge(z_in, g * GN + n - 1)
                        for f in range(FC):
                            last = pe.matmul(psO[n % 2][:], hT[:, f, n * P:(n + 1) * P], w2[:, f, :], start=(f == 0),
                                             stop=(f == FC - 1))
                        last.then_inc(out_done, 1)
                turns(pe, GROUPS, group)

            @block.scalar
            def _(act):
                def group(g):
                    for n in range(GN):
                        act.wait_ge(turned, g * GN + n + 1)
                        act.copy(yT[:, :, n * P:(n + 1) * P], psT[n % 2][:]).then_inc(yT_in, 1)
                    for f in range(FC):
                        act.wait_ge(hidden, g * FC + f + 1)
                        act.activation(hT[:, f, :], psH[f % 2][:], ACT.Relu, bias=b1[:, f:f + 1]).then_inc(hT_in, 1)
                    ln.root(act, g)
                turns(act, GROUPS, group)

            @block.gpsimd
            def _(pool):
                ln.set_eps(pool)

            @block.vector
            def _(vec):
                def group(g):
                    c = Chain(vec, steps, g * (1 + GN + 2))
                    vec.wait_ge(yres_in, g * 16 + 16)
                    if later(g):
                        vec.wait_ge(stored, g * 16)
                    for n in range(GN):
                        vec.wait_ge(out_done, g * GN + n + 1)
                        vec.tensor_tensor(z[:, n, :], psO[n % 2][:], yres[:, n, :], ALU.add).then_inc(z_in, 1)
                    vec.wait_ge(z_in, g * GN + GN)
                    c.then(vec.tensor_tensor(z[:], z[:], over(0), ALU.add))
                    c.wait()
                    ln.stats(vec, lambda n: z[:, n, :], g)
                    ln.scale(vec, g)
                    for n in range(GN):
                        c.then(ln.apply(vec, n, z[:, n, :], z[:, n, :]))
                    c.wait()
                    c.then(vec.tensor_tensor(z[:], z[:], over(1), ALU.mult))
                    c.wait()
                    c.then(vec.tensor_tensor(z[:], z[:], over(2), ALU.add))
                    c.wait()
                    vec.wait_ge(enc_in, g * 16 + 16)
                    vec.tensor_tensor(z[:], z[:], enc[:], ALU.add).then_inc(done, 1)
                turns(vec, GROUPS, group)


def mix_slices(nc, a, T, xn_dram, gnn_dram, x3_dram, y3_dram):
    with ExitStack() as stack:
        m = Memory(nc, stack, "mix")
        qT = m.sb("qT", [P, 2, NP])
        folded = m.sb("folded", [P, 2, C])
        project_slices(nc, a, T, xn_dram, qT, folded)
        spread_slices(nc, a, T, qT, folded, gnn_dram, x3_dram, y3_dram)


def project_slices(nc, a, T, xn_dram, qT, folded):
    with ExitStack() as stack:
        m = Memory(nc, stack, "slice")
        HS = H * SL
        VW = 4 * D + 1
        w_in = m.sb("w_in", [P, KC, C])
        w_out = m.sb("w_out", [P, KC, C])
        b_in = m.sb("b_in", [P, KC])
        wqkv = m.sb("wqkv", [P, 2 * (2 * SL + D)])
        x = m.sb("x", [P, GN, C])
        xT = m.sb("xT", [P, KC, NODES])
        mid = m.sb("mid", [P, KC, NODES])
        q = m.sb("q", [P, GN, HS])
        qsum = m.sb("qsum", [P, GN * H])
        kall = m.sb("kall", [P, NT, HS])
        vall = m.sb("vall", [P, NT, 2, VW])
        kmax = m.sb("kmax", [P, HS])
        ktop = m.sb("ktop", [P, 2])
        kdiag = m.sb("kdiag", [P, 2, P])
        ones = m.sb("ones", [P, P])
        ksum = m.sb("ksum", [P, 2])
        kv = m.sb("kv", [P, 2, 4 * D])
        kvT = m.sb("kvT", [P, 2, 2, P])
        psT = [m.ps(f"psT{i}", [P, KC, P]) for i in range(2)]
        psM = [m.ps(f"psM{i}", [P, NODES]) for i in range(2)]
        psQ = [m.ps(f"psQ{i}", [P, KC, 4 * D]) for i in range(2)]
        names = ("zeroed", "w_landed", "x_in", "turned", "xT_in", "middled", "mid_in", "projected", "q_in", "kv_in",
                 "kmaxed", "steps", "shifted", "exped", "normed", "q_turned", "qT_in", "kflip", "ktopped", "kspread",
                 "kshifted", "kexped", "kv_done", "kv_in2", "kvflip", "kvT_in", "fold_done", "ones_in", "fixed")
        s = {n: m.sem(n) for n in names}
        W2 = 2 * SL
        with nc.Block() as block:
            @block.gpsimd
            def _(pool):
                pool.memset(wqkv[:], 0.0).then_inc(s["zeroed"], 1)
                pool.memset(ones[:], 1.0).then_inc(s["ones_in"], 1)
                pool.memset(vall[:, :, :, 4 * D:VW], 1.0).then_inc(s["ones_in"], 1)
                pool.memset(kmax[:], -3e38).then_inc(s["ones_in"], 1)
                pool.memset(kv[:], 0.0).then_inc(s["ones_in"], 1)

            @block.sync
            def _(sp):
                sp.dma_start(w_in[:], a["L0_mix_W_in"].rearrange("(k p) n -> p k n", p=P)).then_inc(s["w_landed"], 16)
                sp.dma_start(w_out[:], a["L0_mix_W_out"].rearrange("(k p) n -> p k n", p=P)).then_inc(s["w_landed"], 16)
                sp.dma_start(b_in[:], a["L0_mix_b_in"].rearrange("(k p) -> p k", p=P), allow_slow_non_contiguous=True).then_inc(s["w_landed"], 16)
                sp.wait_ge(s["zeroed"], 1)
                for j in range(2):
                    r = slice(j * D, (j + 1) * D)
                    sp.dma_start(wqkv[r, j * SL:(j + 1) * SL], a["L0_mix_Wq"]).then_inc(s["w_landed"], 16)
                    sp.dma_start(wqkv[r, W2 + j * SL:W2 + (j + 1) * SL], a["L0_mix_Wk"]).then_inc(s["w_landed"], 16)
                    sp.dma_start(wqkv[r, 2 * W2 + j * D:2 * W2 + (j + 1) * D], a["L0_mix_Wv"]).then_inc(s["w_landed"], 16)

                def group(g):
                    if later(g):
                        sp.wait_ge(s["turned"], g * GN)
                    sp.dma_start(x[:], xn_dram[bass.ds(g * NODES, NODES), :].rearrange("(t p) c -> p t c", p=P)
                                 ).then_inc(s["x_in"], 16)
                turns(sp, GROUPS, group)

            @block.tensor
            def _(pe):
                pe.wait_ge(s["w_landed"], 16 * 9)

                def group(g):
                    pe.wait_ge(s["x_in"], g * 16 + 16)
                    if later(g):
                        pe.wait_ge(s["qT_in"], g * 2)
                    turn_group(pe, T, x, psT, s["turned"], s["xT_in"], lambda n: g * GN + n - 1 if n >= 2 else None)
                    pe.wait_ge(s["xT_in"], g * GN + GN)
                    for c in range(KC):
                        if later(g) or c >= 2:
                            pe.wait_ge(s["mid_in"], g * KC + c - 1)
                        for k in range(KC):
                            last = pe.matmul(psM[c % 2][:], w_in[:, k, c * P:(c + 1) * P], xT[:, k, :], start=(k == 0),
                                             stop=(k == KC - 1))
                        last.then_inc(s["middled"], 1)
                    pe.wait_ge(s["mid_in"], g * KC + KC)
                    for n in range(GN):
                        if later(g) or n >= 2:
                            pe.wait_ge(s["kv_in"], g * GN + n - 1)
                            pe.wait_ge(s["kmaxed"], g * GN + n - 1)
                        for c in range(KC):
                            last = pe.matmul(psQ[n % 2][:, c, :], mid[:, c, n * P:(n + 1) * P], wqkv[:], start=True,
                                             stop=True)
                        last.then_inc(s["projected"], 1)
                    pe.wait_ge(s["normed"], g + 1)
                    for e in range(2):
                        for n in range(GN):
                            last = pe.transpose(psT[e][:, n, :], q[:, n, e * P:(e + 1) * P], T["ident"][:])
                        last.then_inc(s["q_turned"], 1)
                turns(pe, GROUPS, group)

                pe.wait_ge(s["qT_in"], 2 * GROUPS)
                pe.wait_ge(s["kmaxed"], NT)
                for e in range(2):
                    last = pe.transpose(psT[0][:, e, :], kmax[:, e * P:(e + 1) * P], T["ident"][:])
                last.then_inc(s["kflip"], 1)
                pe.wait_ge(s["ktopped"], 2)
                pe.wait_ge(s["ones_in"], 4)
                for e in range(2):
                    last = pe.matmul(psT[1][:, e, :], ones[:], kdiag[:, e, :], start=True, stop=True)
                last.then_inc(s["kspread"], 1)
                pe.wait_ge(s["kexped"], GROUPS)
                pe.wait_ge(s["kv_in"], NT)
                for e in range(2):
                    for t in range(NT):
                        r = P if t < NT - 1 else LAST
                        last = pe.matmul(psM[e][:, 0:VW], kall[0:r, t, e * P:(e + 1) * P], vall[0:r, t, e, :],
                                         start=(t == 0), stop=(t == NT - 1))
                    last.then_inc(s["kv_done"], 1)
                pe.wait_ge(s["kv_in2"], 2)
                for e in range(2):
                    for c in range(2):
                        last = pe.transpose(psT[0][:, 2 * e + c, :], kv[:, e, c * P:(c + 1) * P], T["ident"][:])
                last.then_inc(s["kvflip"], 1)
                pe.wait_ge(s["kvT_in"], 1)
                for e in range(2):
                    for c in range(2):
                        last = pe.matmul(psM[e][:], kvT[:, e, c, :], w_out[:, 2 * e + c, :], start=(c == 0), stop=(c == 1))
                    last.then_inc(s["fold_done"], 1)

            @block.scalar
            def _(act):
                act.wait_ge(s["ones_in"], 4)

                def group(g):
                    for n in range(GN):
                        act.wait_ge(s["turned"], g * GN + n + 1)
                        act.copy(xT[:, :, n * P:(n + 1) * P], psT[n % 2][:]).then_inc(s["xT_in"], 1)
                    for c in range(KC):
                        act.wait_ge(s["middled"], g * KC + c + 1)
                        act.activation(mid[:, c, :], psM[c % 2][:], ACT.Identity, bias=b_in[:, c:c + 1]
                                       ).then_inc(s["mid_in"], 1)
                    for n in range(GN):
                        act.wait_ge(s["projected"], g * GN + n + 1)
                        ps = psQ[n % 2]
                        if n == 0 and later(g):
                            act.wait_ge(s["q_turned"], g * 2)
                        act.copy(q[:, n, :].rearrange("p (c w) -> p c w", c=KC), ps[:, :, 0:W2]).then_inc(s["q_in"], 1)
                        act.copy(one(kall[:, bass.ds(g * GN + n, 1), :]).rearrange("p (c w) -> p c w", c=KC),
                                 ps[:, :, W2:2 * W2])
                        for e in range(2):
                            last = act.copy(vall[:, bass.ds(g * GN + n, 1), e, 0:4 * D].rearrange(
                                "p o (c w) -> p (o c) w", c=2), ps[:, 2 * e:2 * e + 2, 2 * W2:])
                        last.then_inc(s["kv_in"], 1)
                    act.wait_ge(s["shifted"], g + 1)
                    act.activation(q[:], q[:], ACT.Exp).then_inc(s["exped"], 1)
                turns(act, GROUPS, group)
                for t in range(GROUPS):
                    r = slice(t * GN, (t + 1) * GN)
                    act.wait_ge(s["kshifted"], t + 1)
                    act.activation(kall[:, r, :], kall[:, r, :], ACT.Exp).then_inc(s["kexped"], 1)

            @block.vector
            def _(vec):
                vec.wait_ge(s["ones_in"], 4)

                def k_top(g, n, rows):
                    km = kmax[0:rows, :].rearrange("p (c w) -> p c w", c=KC)
                    vec.wait_ge(s["kv_in"], g * GN + n + 1)
                    if later(g) or n:
                        vec.wait_ge(s["kmaxed"], g * GN + n)
                    vec.tensor_tensor(km, km, psQ[n % 2][0:rows, :, W2:2 * W2], ALU.max).then_inc(s["kmaxed"], 1)

                def group(g, rows_of_last=P):
                    c = Chain(vec, s["steps"], g * 3)
                    for n in range(GN):
                        k_top(g, n, P if n < GN - 1 else rows_of_last)
                    vec.wait_ge(s["q_in"], g * GN + GN)
                    by_head = q[:].rearrange("p n (h s) -> p (n h) s", s=SL)
                    c.then(vec.tensor_reduce(qsum[:], by_head, AX.X, ALU.max))
                    c.wait()
                    vec.tensor_tensor(by_head, by_head, qsum[:].unsqueeze(2).to_broadcast([P, GN * H, SL]),
                                      ALU.subtract).then_inc(s["shifted"], 1)
                    vec.wait_ge(s["exped"], g + 1)
                    c.then(vec.tensor_reduce(qsum[:], by_head, AX.X, ALU.add))
                    c.wait()
                    c.then(vec.reciprocal(qsum[:], qsum[:]))
                    c.wait()
                    vec.tensor_tensor(by_head, by_head, qsum[:].unsqueeze(2).to_broadcast([P, GN * H, SL]),
                                      ALU.mult).then_inc(s["normed"], 1)
                    for e in range(2):
                        vec.wait_ge(s["q_turned"], g * 2 + e + 1)
                        vec.tensor_scalar(qT[:, e, bass.ds(g * NODES, NODES)], psT[e][:].rearrange("p k n -> p (k n)"),
                                          1.0, None, ALU.mult).then_inc(s["qT_in"], 1)
                group(0)
                with vec.Fori(1, GROUPS - 1) as g:
                    group(g)
                group(GROUPS - 1, LAST)

                c = Chain(vec, s["fixed"])
                vec.wait_ge(s["kflip"], 1)
                c.then(vec.tensor_reduce(ktop[:], psT[0][:, 0:2, :], AX.X, ALU.max))
                c.wait()
                for e in range(2):
                    vec.tensor_scalar(kdiag[:, e, :], T["ident"][:], ktop[:, e:e + 1], None, ALU.mult
                                      ).then_inc(s["ktopped"], 1)
                vec.wait_ge(s["kspread"], 1)
                vec.wait_ge(s["kv_in"], NT)
                for t in range(GROUPS):
                    r = slice(t * GN, (t + 1) * GN)
                    vec.tensor_tensor(kall[:, r, :], kall[:, r, :], psT[1][:, 0:2, :].rearrange("p e w -> p (e w)")
                                      .unsqueeze(1).to_broadcast([P, GN, HS]), ALU.subtract).then_inc(s["kshifted"], 1)
                for e in range(2):
                    vec.wait_ge(s["kv_done"], e + 1)
                    c.then(vec.reciprocal(ksum[:, e:e + 1], psM[e][:, 4 * D:VW]))
                    c.wait()
                    for j in range(4):
                        r = slice(j * SL, (j + 1) * SL)
                        last = vec.tensor_scalar(kv[r, e, j * D:(j + 1) * D], psM[e][r, j * D:(j + 1) * D],
                                                 ksum[r, e:e + 1], None, ALU.mult)
                    last.then_inc(s["kv_in2"], 1)
                vec.wait_ge(s["kvflip"], 1)
                vec.tensor_copy(kvT[:].rearrange("p e c w -> p (e c w)"), psT[0][:].rearrange("p k n -> p (k n)")
                                ).then_inc(s["kvT_in"], 1)
                for e in range(2):
                    vec.wait_ge(s["fold_done"], e + 1)
                    c.then(vec.tensor_copy(folded[:, e, :], psM[e][:]))


def spread_slices(nc, a, T, qT, folded, gnn_dram, x3_dram, y3_dram):
    with ExitStack() as stack:
        m = Memory(nc, stack, "spread")
        x = m.sb("x", [P, NT, C])
        gnn = m.sb("gnn", [P, NT, C])
        bias = m.sb("bias", [P, C])
        psX = [m.ps(f"psX{i}", [P, C]) for i in range(4)]
        zeroed, landed, summed, mixed, mixed_in, biased, normed, stored = (
            m.sem(s) for s in ("zeroed", "landed", "summed", "mixed", "mixed_in", "biased", "normed", "stored"))
        ln = LayerNorm(nc, m, NT)
        with nc.Block() as block:
            @block.sync
            def _(sp):
                sp.dma_start(gnn[:], gnn_dram.rearrange("(t p) c -> p t c", p=P)).then_inc(landed, 16)
                sp.dma_start(bias[:], a["L0_mix_b_out"].partition_broadcast(P)).then_inc(landed, 16)
                sp.wait_ge(zeroed, 1)
                sp.dma_start(x[:, 0:NT - 1, :],
                             a["x"][0:(NT - 1) * P, :].rearrange("(t p) c -> p t c", p=P)).then_inc(landed, 16)
                sp.dma_start(x[0:LAST, NT - 1, :], a["x"][(NT - 1) * P:N, :]).then_inc(landed, 16)
                for t in range(NT):
                    sp.wait_ge(biased, t + 1)
                    sp.dma_start(x3_dram[t * P:(t + 1) * P, :], x[:, t, :]).then_inc(stored, 16)
                for t in range(NT):
                    sp.wait_ge(normed, t + 1)
                    sp.dma_start(y3_dram[t * P:(t + 1) * P, :], gnn[:, t, :]).then_inc(stored, 16)
                sp.wait_ge(stored, 32 * NT)

            @block.gpsimd
            def _(pool):
                pool.memset(x[:, NT - 1, :], 0.0).then_inc(zeroed, 1)
                ln.set_eps(pool)
                pool.wait_ge(landed, 64)
                for t in range(NT):
                    pool.tensor_tensor(x[:, t, :], x[:, t, :], gnn[:, t, :], ALU.add).then_inc(summed, 1)

            @block.tensor
            def _(pe):
                for t in range(NT):
                    if t >= 4:
                        pe.wait_ge(mixed_in, t - 3)
                    for e in range(2):
                        last = pe.matmul(psX[t % 4][:], qT[:, e, t * P:(t + 1) * P], folded[:, e, :], start=(e == 0),
                                         stop=(e == 1))
                    last.then_inc(mixed, 1)

            @block.vector
            def _(vec):
                for t in range(NT):
                    vec.wait_ge(mixed, t + 1)
                    vec.wait_ge(summed, t + 1)
                    vec.tensor_tensor(x[:, t, :], x[:, t, :], psX[t % 4][:], ALU.add).then_inc(mixed_in, 1)
                for t in range(NT):
                    vec.wait_ge(mixed_in, t + 1)
                    vec.tensor_tensor(x[:, t, :], x[:, t, :], bias[:], ALU.add).then_inc(biased, 1)
                vec.wait_ge(biased, NT)
                ln.stats(vec, lambda t: x[:, t, :])
                ln.scale(vec)
                for t in range(NT):
                    ln.apply(vec, t, gnn[:, t, :], x[:, t, :]).then_inc(normed, 1)

            @block.scalar
            def _(act):
                ln.root(act)


def quantise_weights(nc, a, T, wT):
    with ExitStack() as stack:
        m = Memory(nc, stack, "quant")
        big = FK * C
        w = m.sb("w", [P, 2, big])
        mag = m.sb("mag", [P, big])
        n_groups = big // P
        scale = m.sb("scale", [P, n_groups])
        inv = m.sb("inv", [P, n_groups])
        psT = [m.ps(f"psT{i}", [P, 4, P]) for i in range(4)]
        landed = [m.sem(f"landed{i}") for i in range(3)]
        steps, ready, turned, taken = (m.sem(s) for s in ("steps", "ready", "turned", "taken"))
        sources = [(a["L0_ffn_w_gate"].rearrange("(f p) c -> p f c", p=P), FK, KC, wT[0]),
                   (a["L0_ffn_w_up"].rearrange("(f p) c -> p f c", p=P), FK, KC, wT[1]),
                   (a["L0_ffn_w_down"].rearrange("(k p) c -> p k c", p=P), KC, FK, wT[2])]
        batches = n_groups // 4
        with nc.Block() as block:
            @block.sync
            def _(sp):
                for i, (src, ro, co, _t) in enumerate(sources):
                    if i >= 2:
                        sp.wait_ge(turned, (i - 1) * batches)
                    sp.dma_start(w[:, i % 2, :].rearrange("p (r c) -> p r c", r=ro), src).then_inc(landed[i], 16)

            @block.vector
            def _(vec):
                c = Chain(vec, steps)
                for i in range(3):
                    wi = w[:, i % 2, :]
                    wg = wi.rearrange("p (g e) -> p g e", e=P)
                    mg = mag[:].rearrange("p (g e) -> p g e", e=P)

                    def over(x):
                        return x[:].unsqueeze(2).to_broadcast([P, n_groups, P])
                    vec.wait_ge(landed[i], 16)
                    c.then(vec.tensor_scalar(mag[:], wi, -1.0, None, ALU.mult))
                    c.wait()
                    c.then(vec.tensor_tensor(mag[:], mag[:], wi, ALU.max))
                    c.wait()
                    c.then(vec.tensor_reduce(scale[:], mg, AX.X, ALU.add))
                    c.wait()
                    c.then(vec.tensor_scalar(scale[:], scale[:], 1.0 / P, EPS, ALU.mult, ALU.add))
                    c.wait()
                    c.then(vec.reciprocal(inv[:], scale[:]))
                    c.wait()
                    c.then(vec.tensor_tensor(wg, wg, over(inv), ALU.mult))
                    c.wait()
                    c.then(vec.tensor_scalar(wi, wi, ROUND, ROUND, ALU.add, ALU.subtract))
                    c.wait()
                    c.then(vec.tensor_scalar(wi, wi, 1.0, -1.0, ALU.min, ALU.max))
                    c.wait()
                    vec.tensor_tensor(wg, wg, over(scale), ALU.mult).then_inc(ready, 1)

            @block.tensor
            def _(pe):
                for i, (_s, ro, co, _t) in enumerate(sources):
                    pe.wait_ge(ready, i + 1)
                    wv = w[:, i % 2, :].rearrange("p (r c e) -> p r c e", r=ro, e=P)
                    for b in range(batches):
                        n = i * batches + b
                        if n >= 4:
                            pe.wait_ge(taken, n - 3)
                        for j in range(4):
                            cc, rr = divmod(b * 4 + j, ro)
                            last = pe.transpose(psT[n % 4][:, j, :], wv[:, rr, cc, :], T["ident"][:])
                        last.then_inc(turned, 1)

            @block.scalar
            def _(act):
                for i, (_s, ro, co, t) in enumerate(sources):
                    flat = t[:].rearrange("p c r -> p (c r)")
                    for b in range(batches):
                        n = i * batches + b
                        act.wait_ge(turned, n + 1)
                        act.copy(flat[:, b * 4 * P:(b + 1) * 4 * P], psT[n % 4][:].rearrange("p k e -> p (k e)")
                                 ).then_inc(taken, 1)


def gated_ffn(nc, a, T, wT, x3_dram, y3_dram, out):
    with ExitStack() as stack:
        m = Memory(nc, stack, "ffn")
        y = m.sb("y", [P, GN, C])
        res = m.sb("res", [P, GN, C])
        yT = m.sb("yT", [P, KC, NODES])
        silu = m.sb("silu", [P, 2, NODES])
        hT = m.sb("hT", [P, FK, NODES])
        psT = [m.ps(f"psT{i}", [P, KC, P]) for i in range(2)]
        psG = [m.ps(f"psG{i}", [P, NODES]) for i in range(2)]
        psU = [m.ps(f"psU{i}", [P, NODES]) for i in range(2)]
        psO = [m.ps(f"psO{i}", [P, C]) for i in range(2)]
        y_in, res_in, turned, yT_in, gated, upped, silued, hT_in, out_done, done, stored = (
            m.sem(s) for s in ("y_in", "res_in", "turned", "yT_in", "gated", "upped", "silued", "hT_in", "out_done",
                               "done", "stored"))

        def rows_of(dram, g):
            return dram[bass.ds(g * NODES, NODES), :].rearrange("(t p) c -> p t c", p=P)

        with nc.Block() as block:
            @block.sync
            def _(sp):
                def group(g):
                    if later(g):
                        sp.wait_ge(turned, g * GN)
                    sp.dma_start(y[:], rows_of(y3_dram, g)).then_inc(y_in, 16)
                    if later(g):
                        sp.wait_ge(done, g * GN)
                        sp.dma_start(rows_of(out, g - 1), res[:]).then_inc(stored, 16)
                        sp.wait_ge(stored, g * 16)
                    sp.dma_start(res[:], rows_of(x3_dram, g)).then_inc(res_in, 16)
                turns(sp, GROUPS, group)
                sp.wait_ge(done, GROUPS * GN)
                r0 = (GROUPS - 1) * NODES
                sp.dma_start(out[r0:(NT - 1) * P, :].rearrange("(t p) c -> p t c", p=P), res[:, 0:GN - 1, :]
                             ).then_inc(stored, 16)
                sp.dma_start(out[(NT - 1) * P:N, :], res[0:LAST, GN - 1, :]).then_inc(stored, 16)
                sp.wait_ge(stored, 16 * (GROUPS + 1))

            @block.tensor
            def _(pe):
                def group(g):
                    pe.wait_ge(y_in, g * 16 + 16)
                    turn_group(pe, T, y, psT, turned, yT_in, lambda n: g * GN + n - 1 if n >= 2 else
                               (g * GN + n - 1 if later(g) else None))
                    pe.wait_ge(yT_in, g * GN + GN)
                    for f in range(FK):
                        fs = slice(f * P, (f + 1) * P)
                        if later(g) or f >= 2:
                            pe.wait_ge(silued, g * FK + f - 1)
                        for k in range(KC):
                            last = pe.matmul(psG[f % 2][:], wT[0][:, k, fs], yT[:, k, :], start=(k == 0),
                                             stop=(k == KC - 1))
                        last.then_inc(gated, 1)
                        if later(g) or f >= 2:
                            pe.wait_ge(hT_in, g * FK + f - 1)
                        for k in range(KC):
                            last = pe.matmul(psU[f % 2][:], wT[1][:, k, fs], yT[:, k, :], start=(k == 0),
                                             stop=(k == KC - 1))
                        last.then_inc(upped, 1)
                    pe.wait_ge(hT_in, g * FK + FK)
                    for n in range(GN):
                        if later(g) or n >= 2:
                            pe.wait_ge(done, g * GN + n - 1)
                        for f in range(FK):
                            last = pe.matmul(psO[n % 2][:], hT[:, f, n * P:(n + 1) * P], wT[2][:, f, :], start=(f == 0),
                                             stop=(f == FK - 1))
                        last.then_inc(out_done, 1)
                turns(pe, GROUPS, group)

            @block.scalar
            def _(act):
                def group(g):
                    for n in range(GN):
                        act.wait_ge(turned, g * GN + n + 1)
                        act.copy(yT[:, :, n * P:(n + 1) * P], psT[n % 2][:]).then_inc(yT_in, 1)
                    for f in range(FK):
                        act.wait_ge(gated, g * FK + f + 1)
                        if later(g) or f >= 2:
                            act.wait_ge(hT_in, g * FK + f - 1)
                        act.activation(silu[:, f % 2, :], psG[f % 2][:], ACT.Silu).then_inc(silued, 1)
                turns(act, GROUPS, group)

            @block.vector
            def _(vec):
                def group(g):
                    for f in range(FK):
                        vec.wait_ge(silued, g * FK + f + 1)
                        vec.wait_ge(upped, g * FK + f + 1)
                        vec.tensor_tensor(hT[:, f, :], psU[f % 2][:], silu[:, f % 2, :], ALU.mult).then_inc(hT_in, 1)
                    vec.wait_ge(res_in, g * 16 + 16)
                    for n in range(GN):
                        vec.wait_ge(out_done, g * GN + n + 1)
                        vec.tensor_tensor(res[:, n, :], psO[n % 2][:], res[:, n, :], ALU.add).then_inc(done, 1)
                turns(vec, GROUPS, group)


def gps_layer(nc, a, out):
    with ExitStack() as whole:
        kept = Memory(nc, whole, "kept")
        T = {}
        xn, k, v, base, x1, y1, gnn, x3, y3 = (nc.dram_tensor(n, (NP, C), F32).ap() for n in (
            "xn_rows", "k_rows", "v_rows", "base_rows", "x1_rows", "y1_rows", "gnn_rows", "x3_rows", "y3_rows"))
        make_constants(nc, kept, T)
        normalise_input(nc, a, xn)
        with ExitStack() as edges:
            share_edges(nc, Memory(nc, edges, "edges"), T)
            index_edges(nc, a, T)
            for layer in range(LAYERS):
                with ExitStack() as stack:
                    m = Memory(nc, stack, f"layer{layer}")
                    scores = m.sb("scores", [P, SLOTS * H])
                    weights = m.sb("weights", [P, SLOTS * H])
                    with ExitStack() as queries:
                        T["q_parts"] = Memory(nc, queries, f"layer{layer}").sb("q_parts", [P, 3, NT, C], BF16)
                        project_nodes(nc, a, T, layer, x1 if layer else xn, xn, k, v, base)
                        score_edges(nc, a, T, layer, k, scores)
                    soften(nc, T, layer, scores, weights)
                    agg = m.sb("agg", [P, NT, 2, HW])
                    aggregate(nc, a, T, layer, v, weights, agg)
                    combine(nc, a, T, layer, agg, base, y1 if layer == LAYERS - 1 else x1)
        node_mlp(nc, a, T, y1, xn, gnn)
        mix_slices(nc, a, T, xn, gnn, x3, y3)
        wT = (kept.sb("gateT", [P, KC, FFN]), kept.sb("upT", [P, KC, FFN]), kept.sb("downT", [P, FK, C]))
        quantise_weights(nc, a, T, wT)
        gated_ffn(nc, a, T, wT, x3, y3, out)


def kernel(**inputs):
    import numpy as np
    import concourse.bacc as bacc
    from concourse.bass_utils import run_bass_kernel_spmd

    nc = bacc.Bacc("TRN2", target_bir_lowering=False, num_devices=1)
    arrays, aps = {}, {}
    for name in inputs:
        if name in ("edge_type_10", "edge_weight"):
            continue
        arrays[name] = np.ascontiguousarray(inputs[name])
        aps[name] = nc.dram_tensor(name, arrays[name].shape, mybir.dt.from_np(arrays[name].dtype),
                                   kind="ExternalInput").ap()
    out = nc.dram_tensor("out", (N, C), F32, kind="ExternalOutput").ap()
    gps_layer(nc, aps, out)
    return run_bass_kernel_spmd(nc, [arrays], core_ids=[0]).results[0]["out"]
```

```python
from contextlib import ExitStack

import concourse.bass as bass
from concourse import mybir

P = 128
N = 2500
C = 512
KC = C // P
H = 8
D = C // H
E = 40000
LAYERS = 2
NT = -(-N // P)
NP = NT * P
LAST = N - (NT - 1) * P
ET = -(-E // P)
EK = -(-ET // P)
CH = 16
G = -(-(ET + NT - 1) // CH)
SLOTS = CH * G
RUN = G * P
U = 16
TURNS = SLOTS // U
GN = 4
GROUPS = NT // GN
NODES = GN * P
NEG = -1e30
EPS = 1e-5
F1 = 2 * C
FFN = 1408
FK = FFN // P
SL = 32
AW = C + H

F32 = mybir.dt.float32
BF16 = mybir.dt.bfloat16
F32R = mybir.dt.float32r
I32 = mybir.dt.int32
ALU = mybir.AluOpType
ACT = mybir.ActivationFunctionType
AX = mybir.AxisListType
ROUND = 1.5 * 2.0 ** 23


class Memory:

    def __init__(self, nc, stack, prefix):
        self.nc, self.stack, self.prefix, self.sems = nc, stack, prefix, []
        stack.callback(self.clear)

    def clear(self):
        if self.sems:
            self.nc.clear_and_free_semaphores(self.sems)
            self.nc.all_engine_barrier()

    def sb(self, name, shape, dt=F32):
        return self.stack.enter_context(self.nc.sbuf_tensor(f"{self.prefix}_{name}", shape, dt))

    def ps(self, name, shape, dt=F32):
        return self.stack.enter_context(self.nc.psum_tensor(f"{self.prefix}_{name}", shape, dt))

    def sem(self, name):
        self.sems.append(self.nc.alloc_semaphore(f"{self.prefix}_{name}"))
        return self.sems[-1]


class Chain:

    def __init__(self, engine, sem, base=0):
        self.engine, self.sem, self.base, self.n = engine, sem, base, 0

    def then(self, ins):
        ins.then_inc(self.sem, 1)
        self.n += 1

    def wait(self):
        self.engine.wait_ge(self.sem, self.base + self.n)


def one(ap):
    return ap.rearrange("p o c -> p (o c)")


def product(pe, out, left, right, start, stop):
    for n, (i, j) in enumerate(((0, 1), (1, 0), (0, 0))):
        last = pe.matmul(out, left[i], right[j], start=start and n == 0, stop=stop and n == 2)
    return last


def turns(engine, n, body):
    body(0)
    with engine.Fori(1, n) as t:
        body(t)


def turns_ahead(engine, n, body):
    body(0, False)
    with engine.Fori(1, n - 1) as t:
        body(t, False)
    body(n - 1, True)


def later(t):
    return not isinstance(t, int) or t > 0


def make_constants(nc, mem, T):
    T["ident"] = mem.sb("ident", [P, P])
    T["identb"] = mem.sb("identb", [P, P], BF16)
    T["lane"] = mem.sb("lane", [P, P])
    T["laneb"] = mem.sb("laneb", [P, P], BF16)
    T["head_of"] = mem.sb("head_of", [P, H])
    T["of_head"] = mem.sb("of_head", [H, P])
    T["chunk_of"] = mem.sb("chunk_of", [P, CH])
    ident, identb, lane, laneb = T["ident"], T["identb"], T["lane"], T["laneb"]
    with ExitStack() as stack:
        m = Memory(nc, stack, "const")
        flip = m.ps("flip", [H, P])
        zeroed, built, masks, flipped, done = (m.sem(x) for x in ("zeroed", "built", "masks", "flipped", "done"))
        with nc.Block() as block:
            @block.gpsimd
            def _(pool):
                pool.memset(ident[:], 0.0).then_inc(zeroed, 1)
                pool.iota(lane[:], [[1, P]], base=0, channel_multiplier=0,
                          allow_small_or_imprecise_dtypes=True).then_inc(built, 1)
                pool.wait_ge(zeroed, 1)
                pool.affine_select(out=ident[:], in_=ident[:], compare_op=ALU.not_equal, fill=1.0, base=0,
                                   pattern=[[-1, P]], channel_multiplier=1).then_inc(built, 1)

            @block.vector
            def _(vec):
                vec.wait_ge(built, 2)
                vec.tensor_copy(identb[:], ident[:]).then_inc(done, 1)
                vec.tensor_copy(laneb[:], lane[:]).then_inc(done, 1)
                vec.tensor_reduce(T["head_of"][:], ident[:].rearrange("p (c h) -> p h c", h=H), AX.X,
                                  ALU.add).then_inc(masks, 1)
                vec.tensor_reduce(T["chunk_of"][:], ident[:].rearrange("p (c h) -> p c h", h=H), AX.X,
                                  ALU.add).then_inc(masks, 1)
                vec.wait_ge(flipped, 1)
                vec.tensor_copy(T["of_head"][:], flip[:]).then_inc(done, 1)

            @block.tensor
            def _(pe):
                pe.wait_ge(masks, 2)
                pe.transpose(flip[:], T["head_of"][:], ident[:]).then_inc(flipped, 1)


def share_edges(nc, mem, T):
    T["full_at"] = mem.sb("full_at", [P, NT], I32)
    T["tile_of"] = mem.sb("tile_of", [P, SLOTS], I32)
    T["local"] = mem.sb("local", [P, SLOTS + U // 2])
    T["disorder"] = mem.sb("disorder", [P, 1], I32)
    T["src"] = mem.sb("src", [P, SLOTS], I32)
    T["same"] = mem.sb("same", [P, RUN + 1], BF16)
    T["first"] = mem.sb("first", [P, RUN], BF16)
    T["last"] = mem.sb("last", [P, RUN], BF16)
    T["linked"] = mem.sb("linked", [H, 2 * CH, 2 * CH])


def order_edges(nc, a, T, ordered):
    with ExitStack() as stack:
        m = Memory(nc, stack, "disorder")
        R, W = 125, E // 125
        here = m.sb("here", [R, W], I32)
        after = m.sb("after", [R, W], I32)
        down = m.sb("down", [R, W])
        count = m.sb("count", [P, 1])
        ones = m.sb("ones", [P, P])
        total = m.ps("total", [P, 1])
        landed, filled, steps, counted, summed = (m.sem(s) for s in ("landed", "filled", "steps", "counted", "summed"))
        with nc.Block() as block:
            @block.gpsimd
            def _(pool):
                pool.memset(ones[:], 1.0).then_inc(filled, 1)
                pool.memset(count[:], 0.0).then_inc(filled, 1)

            @block.sync
            def _(sp):
                sp.dma_start(here[:], a["dst"].rearrange("(r w) -> r w", w=W)).then_inc(landed, 16)
                sp.dma_start(after[0:R - 1, :], a["dst"][1:E - W + 1].rearrange("(r w) -> r w", w=W)
                             ).then_inc(landed, 16)
                sp.dma_start(after[R - 1:R, 0:W - 1], a["dst"][E - W + 1:E].rearrange("(r w) -> r w", r=1)
                             ).then_inc(landed, 16)
                sp.dma_start(after[R - 1:R, W - 1:W], a["dst"][E - 1:E].rearrange("(r w) -> r w", r=1)
                             ).then_inc(landed, 16)

            @block.vector
            def _(vec):
                vec.wait_ge(landed, 64)
                vec.tensor_tensor(down[:], here[:], after[:], ALU.is_gt).then_inc(steps, 1)
                vec.wait_ge(filled, 2)
                vec.wait_ge(steps, 1)
                vec.tensor_reduce(count[0:R, :], down[:], AX.X, ALU.add).then_inc(counted, 1)
                vec.wait_ge(summed, 1)
                vec.tensor_copy(T["disorder"][:], total[:]).then_inc(steps, 1)

            @block.tensor
            def _(pe):
                pe.wait_ge(filled, 2)
                pe.wait_ge(counted, 1)
                pe.matmul(total[:], ones[:], count[:], start=True, stop=True).then_inc(summed, 1)

    with ExitStack() as stack:
        m = Memory(nc, stack, "order")
        EP = ET * P
        CHUNK = E // 10
        wide = m.sb("wide", [P, CHUNK], I32)
        every = m.sb("every", [P, EP], mybir.dt.int16)
        less = m.sb("less", [P, EP], mybir.dt.uint8)
        tiles = m.sb("tiles", [P, 2, ET], I32)
        key = m.sb("key", [P, ET])
        before = m.sb("before", [P, P])
        ties = m.sb("ties", [P, P])
        place = m.sb("place", [P, 2])
        index = m.sb("index", [P, 1], I32)
        load = m.sb("load", [P, 2], I32)
        FAR = 2 * NP
        filled, chunk_in, tiles_in, widened, steps, placed, loads, going, sent, keyed, lower = (
            m.sem(s) for s in ("filled", "chunk_in", "tiles_in", "widened", "steps", "placed", "loads", "going",
                               "sent", "keyed", "lower"))

        def disordered(engine):
            return engine.value_load(T["disorder"][0:1, 0:1], min_val=0, max_val=E) > 0

        with nc.Block() as block:
            @block.gpsimd
            def _(pool):
                with pool.If(disordered(pool)):
                    pool.memset(before[:], 1.0).then_inc(lower, 1)
                    pool.memset(tiles[:, 0, ET - 1:ET], FAR).then_inc(filled, 1)
                    pool.memset(tiles[:, 1, ET - 1:ET], 0).then_inc(filled, 1)
                    pool.wait_ge(lower, 1)
                    pool.affine_select(out=before[:], in_=before[:], compare_op=ALU.is_gt, fill=0.0, base=0,
                                       pattern=[[-1, P]], channel_multiplier=1).then_inc(filled, 1)

                    def turn(t):
                        pool.wait_ge(placed, t + 1)
                        pool.sem_inc(going, 1)
                        for k in range(2):
                            pool.indirect_dma_start(ordered[k], bass.IndirectOffsetOnAxis(ap=index[:, 0:1], axis=0),
                                                    load[:, k:k + 1], None).then_inc(sent, 16)
                    turns(pool, ET, turn)
                    pool.wait_ge(sent, 32 * ET)

            @block.sync
            def _(sp):
                with sp.If(disordered(sp)):
                    sp.wait_ge(filled, 3)
                    for k, name in enumerate(("dst", "src")):
                        sp.dma_start(tiles[:, k, 0:ET - 1], a[name][0:(ET - 1) * P].rearrange("(t p) -> p t", p=P),
                                     allow_slow_non_contiguous=True).then_inc(tiles_in, 16)
                        sp.dma_start(tiles[0:E % P, k, ET - 1:ET],
                                     a[name][(ET - 1) * P:E].rearrange("(p o) -> p o", o=1)).then_inc(tiles_in, 16)
                    for n in range(E // CHUNK):
                        if n:
                            sp.wait_ge(widened, n)
                        sp.dma_start(wide[:], a["dst"][n * CHUNK:(n + 1) * CHUNK].partition_broadcast(P)
                                     ).then_inc(chunk_in, 16)

            @block.vector
            def _(vec):
                with vec.If(disordered(vec)):
                    for n in range(E // CHUNK):
                        vec.wait_ge(chunk_in, 16 * (n + 1))
                        vec.tensor_scalar(every[:, n * CHUNK:(n + 1) * CHUNK], wide[:], 2.0, None, ALU.mult
                                          ).then_inc(widened, 1)
                    vec.memset(every[:, E:EP], 2 * FAR).then_inc(widened, 1)
                    vec.wait_ge(tiles_in, 64)
                    vec.tensor_scalar(key[:], tiles[:, 0, :], 2.0, None, ALU.mult).then_inc(keyed, 1)
                    vec.wait_ge(keyed, 1)
                    vec.wait_ge(filled, 3)
                    vec.wait_ge(widened, E // CHUNK + 1)

                    def turn(t):
                        PER = 7
                        c = Chain(vec, steps, t * PER)
                        mine = every[:, bass.ds(t * P, P)]
                        c.then(vec.tensor_scalar(less[:], every[:], key[:, bass.ds(t, 1)], 0.0, ALU.is_lt, ALU.add,
                                                 accum_out=place[:, 0:1]))
                        c.then(vec.tensor_scalar(ties[:], mine, key[:, bass.ds(t, 1)], None, ALU.is_equal))
                        c.wait()
                        c.then(vec.tensor_tensor(ties[:], ties[:], before[:], ALU.mult))
                        c.then(vec.tensor_scalar(mine, mine, -1.0, None, ALU.add))
                        c.wait()
                        c.then(vec.tensor_reduce(place[:, 1:2], ties[:], AX.X, ALU.add))
                        c.wait()
                        if later(t):
                            vec.wait_ge(sent, t * 32)
                        c.then(vec.tensor_scalar(load[:], tiles[:, :, bass.ds(t, 1)].rearrange("p k o -> p (k o)"), 0.0,
                                                 None, ALU.add))
                        c.then(vec.tensor_tensor(index[:], place[:, 0:1], place[:, 1:2], ALU.add))
                        c.wait()
                        vec.sem_inc(placed, 1)
                    turns(vec, ET, turn)


def index_edges(nc, a, T, ordered):
    with ExitStack() as stack:
        m = Memory(nc, stack, "index")
        raw = m.sb("raw", [P, 2, EK, P], I32)
        rows = m.sb("rows", [P, 2, EK, P])
        low = m.sb("low", [P, NT])
        junk = m.sb("junk", [P, EK * P])
        ones = m.sb("ones", [P, P])
        bound = m.sb("bound", [P, NT + 1])
        up = m.sb("up", [P, NT])
        ints = m.sb("ints", [P, 2, NT], I32)
        shifted = m.sb("shifted", [P, 2, NT], I32)
        flo = m.sb("flo", [P, NT])
        cnt = m.sb("cnt", [P, NT])
        some = m.sb("some", [P, NT])
        cum = m.sb("cum", [P, NT + 1])
        shift = m.sb("shift", [P, NT])
        dshift = m.sb("dshift", [P, NT])
        slot = m.sb("slot", [P, SLOTS])
        part = m.sb("part", [P, 1])
        tile_of = m.sb("tile_of", [P, SLOTS])
        etile = m.sb("etile", [P, SLOTS])
        step = m.sb("step", [P, SLOTS])
        pick = m.sb("pick", [P, EK, SLOTS])
        dst = m.sb("dst", [P, SLOTS])
        okl = m.sb("okl", [P, SLOTS])
        okh = m.sb("okh", [P, SLOTS])
        spread = m.sb("spread", [P, RUN])
        seg = m.sb("seg", [P, RUN])
        diff = m.sb("diff", [P, RUN])
        ends = m.sb("ends", [P, 2, CH])
        endv = m.sb("endv", [H, 2 * CH])
        neq = m.sb("neq", [H, 2 * CH, 2 * CH])
        psb = m.ps("psb", [P, NT])
        psd = m.ps("psd", [P, SLOTS])
        pss = m.ps("pss", [P, SLOTS])
        pse = m.ps("pse", [H, 2 * CH])
        pst = [m.ps(f"pst{i}", [P, 4 * P]) for i in range(2)]
        landed, filled, built, step_done, counted, summed, picked, placed, spread_done, turned, ends_done, ends_sum \
            = (m.sem(x) for x in ("landed", "filled", "built", "steps", "counted", "summed", "picked", "placed",
                                  "spread", "turned", "ends", "ends_sum"))
        copied = m.sem("copied")
        full = E // P - (EK - 1) * P
        rest = E % P
        flip_groups = [(g, min(4, G - g)) for g in range(0, G, 4)]
        with nc.Block() as block:
            @block.gpsimd
            def _(pool):
                pool.memset(raw[:, 0, :, :], -1).then_inc(filled, 1)
                pool.memset(raw[:, 1, :, :], 0).then_inc(filled, 1)
                pool.memset(ones[:], 1.0).then_inc(built, 1)
                pool.iota(slot[:], [[1, SLOTS]], base=0, channel_multiplier=0,
                          allow_small_or_imprecise_dtypes=True).then_inc(built, 1)
                pool.iota(part[:], [[0, 1]], base=0, channel_multiplier=1,
                          allow_small_or_imprecise_dtypes=True).then_inc(built, 1)

            @block.sync
            def _(sp):
                sp.wait_ge(filled, 2)
                whole = (EK - 1) * P * P

                def load(k, edges):
                    sp.dma_start(raw[:, k, 0:EK - 1, :],
                                 edges[0:whole].rearrange("(k p e) -> p k e", p=P, e=P)).then_inc(landed, 16)
                    sp.dma_start(raw[0:full, k, EK - 1, :],
                                 edges[whole:whole + full * P].rearrange("(p e) -> p e", e=P)).then_inc(landed, 16)
                    sp.dma_start(raw[full:full + 1, k, EK - 1, 0:rest],
                                 edges[E - rest:E].rearrange("(p e) -> p e", p=1)).then_inc(landed, 16)

                disorder = sp.value_load(T["disorder"][0:1, 0:1], min_val=0, max_val=E)
                with sp.If(disorder > 0):
                    for k in range(2):
                        load(k, ordered[k].rearrange("e o -> (e o)"))
                with sp.Else():
                    for k, name in enumerate(("dst", "src")):
                        load(k, a[name])

            @block.vector
            def _(vec):
                c = Chain(vec, step_done)
                vec.wait_ge(landed, 96)
                c.then(vec.tensor_scalar(rows[:, 0], raw[:, 0], 1.0, None, ALU.add))
                c.then(vec.tensor_copy(rows[:, 1], raw[:, 1]))
                c.wait()
                for d in range(NT):
                    c.then(vec.tensor_scalar(junk[:], rows[:, 0].rearrange("p k e -> p (k e)"),
                                             float(P * (d + 1)), 0.0, ALU.is_le, ALU.add,
                                             accum_out=low[:, d:d + 1]))
                    c.wait()
                vec.nop().then_inc(counted, 1)
                vec.wait_ge(summed, 1)
                c.then(vec.memset(bound[:, 0:1], 0.0))
                c.then(vec.tensor_scalar(bound[:, 1:NT + 1], psb[:], -float(EK * P * P - E), None, ALU.add))
                c.wait()
                c.then(vec.tensor_scalar(up[:], bound[:, 1:NT + 1], float(P - 1), None, ALU.add))
                c.then(vec.tensor_copy(ints[:, 0, :], bound[:, 0:NT]))
                c.then(vec.tensor_tensor(some[:], bound[:, 1:NT + 1], bound[:, 0:NT], ALU.is_gt))
                c.wait()
                c.then(vec.tensor_copy(ints[:, 1, :], up[:]))
                c.wait()
                c.then(vec.tensor_scalar(shifted[:], ints[:], 7, None, ALU.logical_shift_right))
                c.wait()
                c.then(vec.tensor_copy(flo[:], shifted[:, 0, :]))
                c.then(vec.tensor_tensor(cnt[:], shifted[:, 1, :], shifted[:, 0, :], ALU.subtract))
                c.wait()
                c.then(vec.tensor_tensor(cnt[:], cnt[:], some[:], ALU.mult))
                c.then(vec.memset(cum[:, 0:1], 0.0))
                c.wait()
                c.then(vec.tensor_tensor_scan(cum[:, 1:NT + 1], ones[:, 0:NT], cnt[:], 0.0, ALU.mult, ALU.add))
                c.wait()
                c.then(vec.tensor_tensor(shift[:], flo[:], cum[:, 0:NT], ALU.subtract))
                vec.wait_ge(built, 3)
                c.then(vec.memset(tile_of[:], 0.0))
                c.then(vec.tensor_copy(etile[:], slot[:]))
                c.wait()
                c.then(vec.tensor_tensor(dshift[:, 1:NT], shift[:, 1:NT], shift[:, 0:NT - 1], ALU.subtract))
                c.wait()
                for d in range(1, NT):
                    c.then(vec.scalar_tensor_tensor(out=tile_of[:], in0=slot[:], scalar=cum[:, d:d + 1],
                                                    in1=tile_of[:], op0=ALU.is_ge, op1=ALU.add))
                    c.then(vec.tensor_scalar(step[:], slot[:], cum[:, d:d + 1], dshift[:, d:d + 1], ALU.is_ge,
                                             ALU.mult))
                    c.wait()
                    c.then(vec.tensor_tensor(etile[:], etile[:], step[:], ALU.add))
                    c.wait()
                c.then(vec.tensor_copy(T["tile_of"][:], tile_of[:]))
                c.then(vec.tensor_scalar(up[:], cum[:, 1:NT + 1], 1.0, None, ALU.add))
                c.wait()
                c.then(vec.tensor_copy(T["full_at"][:], up[:]))
                for k in range(EK):
                    c.then(vec.tensor_scalar(pick[:, k, :], etile[:], -float(P * k), part[:, 0:1], ALU.add,
                                             ALU.is_equal))
                c.wait()
                vec.nop().then_inc(picked, 1)
                vec.wait_ge(placed, 2)
                c.then(vec.memset(T["local"][:, SLOTS:], -1.0))
                c.then(vec.tensor_copy(T["src"][:], pss[:]))
                c.then(vec.tensor_scalar(dst[:], psd[:], -1.0, None, ALU.add))
                c.then(vec.tensor_scalar(step[:], tile_of[:], -float(P), None, ALU.mult))
                c.wait()
                c.then(vec.tensor_tensor(T["local"][:, 0:SLOTS], dst[:], step[:], ALU.add))
                c.wait()
                c.then(vec.tensor_scalar(okl[:], T["local"][:, 0:SLOTS], 0.0, None, ALU.is_ge))
                c.then(vec.tensor_scalar(okh[:], T["local"][:, 0:SLOTS], float(P), None, ALU.is_lt))
                c.then(vec.tensor_scalar(dst[:], dst[:], 1.0, None, ALU.add))
                c.wait()
                c.then(vec.tensor_tensor(okl[:], okl[:], okh[:], ALU.mult))
                c.wait()
                c.then(vec.tensor_tensor(dst[:], dst[:], okl[:], ALU.mult))
                c.wait()
                for cc in range(CH):
                    c.then(vec.tensor_copy(
                        spread[:].rearrange("p (g c h) -> p g c h", c=CH, h=H)[:, :, cc, :],
                        dst[:, cc * G:(cc + 1) * G].rearrange("p (g o) -> p g o", o=1).to_broadcast([P, G, H])))
                c.wait()
                vec.nop().then_inc(spread_done, 1)
                for n, (g, k) in enumerate(flip_groups):
                    vec.wait_ge(turned, n + 1)
                    vec.tensor_copy(seg[:, g * P:(g + k) * P], pst[n % 2][:, 0:k * P]).then_inc(copied, 1)
                vec.wait_ge(copied, len(flip_groups))
                same, first, last = T["same"], T["first"], T["last"]
                c.then(vec.memset(same[:, 0:1], NEG))
                c.then(vec.memset(same[:, RUN:RUN + 1], NEG))
                c.then(vec.tensor_tensor(diff[:, 1:RUN], seg[:, 1:RUN], seg[:, 0:RUN - 1], ALU.not_equal))
                c.then(vec.tensor_scalar(first[:], seg[:], seg[:, 0:1], NEG, ALU.not_equal, ALU.mult))
                c.then(vec.tensor_scalar(last[:], seg[:], seg[:, RUN - 1:RUN], NEG, ALU.not_equal, ALU.mult))
                c.then(vec.tensor_scalar(ends[:, 0, :], T["chunk_of"][:], seg[:, 0:1], None, ALU.mult))
                c.then(vec.tensor_scalar(ends[:, 1, :], T["chunk_of"][:], seg[:, RUN - 1:RUN], None, ALU.mult))
                c.wait()
                vec.nop().then_inc(ends_done, 1)
                c.then(vec.tensor_scalar(same[:, 1:RUN], diff[:, 1:RUN], NEG, None, ALU.mult))
                vec.wait_ge(ends_sum, 1)
                c.then(vec.tensor_copy(endv[:], pse[:]))
                c.wait()
                c.then(vec.tensor_tensor(neq[:], endv[:].unsqueeze(2).to_broadcast([H, 2 * CH, 2 * CH]),
                                         endv[:].unsqueeze(1).to_broadcast([H, 2 * CH, 2 * CH]), ALU.not_equal))
                c.wait()
                c.then(vec.tensor_scalar(T["linked"][:], neq[:], NEG, None, ALU.mult))
                c.wait()

            @block.tensor
            def _(pe):
                pe.wait_ge(built, 3)
                pe.wait_ge(counted, 1)
                pe.matmul(psb[:], ones[:], low[:], start=True, stop=True).then_inc(summed, 1)
                pe.wait_ge(picked, 1)
                for k, out in ((0, psd), (1, pss)):
                    for b in range(EK):
                        last = pe.matmul(out[:], rows[:, k, b, :], pick[:, b, :], start=(b == 0), stop=(b == EK - 1))
                    last.then_inc(placed, 1)
                pe.wait_ge(spread_done, 1)
                for n, (g, k) in enumerate(flip_groups):
                    if n >= 2:
                        pe.wait_ge(copied, n - 1)
                    for j in range(k):
                        last = pe.transpose(pst[n % 2][:, j * P:(j + 1) * P], spread[:, (g + j) * P:(g + j + 1) * P],
                                            T["ident"][:])
                    last.then_inc(turned, 1)
                pe.wait_ge(ends_done, 1)
                pe.matmul(pse[:], T["head_of"][:], ends[:].rearrange("p e c -> p (e c)"), start=True,
                          stop=True).then_inc(ends_sum, 1)


def normalise_input(nc, a, xn_dram):
    with ExitStack() as stack:
        m = Memory(nc, stack, "ln0")
        x = m.sb("x", [P, NT, C])
        stats = m.sb("stats", [P, NT, 6])
        mv = m.sb("mv", [P, NT, 2])
        eps = m.sb("eps", [P, 1])
        std = m.sb("std", [P, NT])
        rstd = m.sb("rstd", [P, NT])
        zeroed, landed, steps, have_mv, have_std, normed, stored = (
            m.sem(x_) for x_ in ("zeroed", "landed", "steps", "have_mv", "have_std", "normed", "stored"))
        with nc.Block() as block:
            @block.gpsimd
            def _(pool):
                pool.memset(x[:, NT - 1, :], 0.0).then_inc(zeroed, 1)
                pool.memset(eps[:], EPS).then_inc(zeroed, 1)

            @block.sync
            def _(sp):
                sp.wait_ge(zeroed, 1)
                sp.dma_start(x[:, 0:NT - 1, :],
                             a["x"][0:(NT - 1) * P, :].rearrange("(t p) c -> p t c", p=P)).then_inc(landed, 16)
                sp.dma_start(x[0:LAST, NT - 1, :], a["x"][(NT - 1) * P:N, :]).then_inc(landed, 16)
                sp.wait_ge(normed, NT)
                sp.dma_start(xn_dram.rearrange("(t p) c -> p t c", p=P), x[:]).then_inc(stored, 16)
                sp.wait_ge(stored, 16)

            @block.vector
            def _(vec):
                vec.wait_ge(landed, 32)
                for t in range(NT):
                    vec.bn_stats(stats[:, t, :], x[:, t, :]).then_inc(steps, 1)
                vec.wait_ge(steps, NT)
                for t in range(NT):
                    vec.bn_aggr(mv[:, t, :], stats[:, t, :]).then_inc(have_mv, 1)
                vec.wait_ge(have_std, 1)
                vec.reciprocal(rstd[:], std[:]).then_inc(steps, 1)
                vec.wait_ge(steps, NT + 1)
                vec.wait_ge(have_mv, NT)
                for t in range(NT):
                    vec.tensor_scalar(x[:, t, :], x[:, t, :], mv[:, t, 0:1], rstd[:, t:t + 1], ALU.subtract,
                                      ALU.mult).then_inc(normed, 1)

            @block.scalar
            def _(act):
                act.wait_ge(zeroed, 2)
                act.wait_ge(have_mv, NT)
                act.activation(std[:], mv[:, :, 1], ACT.Sqrt, bias=eps[:, 0:1]).then_inc(have_std, 1)


def project_nodes(nc, a, T, layer, x_dram, enc_dram, k_dram, v_dram, base_dram):
    with ExitStack() as stack:
        m = Memory(nc, stack, f"proj{layer}")
        names = ("s", "k", "v", "q")
        RAW = 4
        S_, K_, V_, Q_ = range(4)
        raw = m.sb("raw", [P, RAW, C])
        w = m.sb("w", [P, 2, 4 * KC, C], F32R)
        bias = m.sb("bias", [P, 4, C])
        x = m.sb("x", [P, 2, C])
        enc = m.sb("enc", [P, 2, C])
        xT = m.sb("xT", [P, 2, 2, KC, P], F32R)
        out = m.sb("out", [P, 2, 3, C])
        psT = [m.ps(f"psT{i}", [P, KC * P]) for i in range(2)]
        psP = [m.ps(f"psP{i}", [P, C]) for i in range(4)]
        w_in = [m.sem(f"w_in{i}") for i in range(RAW)]
        bias_in = m.sem("bias_in")
        w_highs, w_lows, xT_high = (m.sem(s) for s in ("w_highs", "w_lows", "xT_high"))
        x_in = [m.sem(f"x_in{b}") for b in range(2)]
        enc_in = [m.sem(f"enc_in{b}") for b in range(2)]
        kv_out = [m.sem(f"kv_out{b}") for b in range(2)]
        base_out = [m.sem(f"base_out{b}") for b in range(2)]
        turned, xT_ready, projected, ready, split, biased = (
            m.sem(s) for s in ("turned", "xT_ready", "projected", "ready", "split", "biased"))
        qp = T["q_parts"]
        T2 = NT // 2
        with nc.Block() as block:
            @block.sync
            def _(sp):
                for b in range(2):
                    sp.dma_start(x[:, b, :], x_dram[b * P:(b + 1) * P, :]).then_inc(x_in[b], 16)
                for j, n in enumerate(names):
                    for k in range(KC):
                        i = j * KC + k
                        if i >= RAW:
                            sp.wait_ge(w_lows, i + 1 - RAW)
                        sp.dma_start(raw[:, i % RAW, :], a[f"L0_gnn_W{n}"][layer, k * P:(k + 1) * P, :]
                                     ).then_inc(w_in[i % RAW], 16)
                    sp.dma_start(bias[:, j], a[f"L0_gnn_b{n}"][layer, :].partition_broadcast(P)).then_inc(bias_in, 16)

                def pair(t, end):
                    for b in range(2):
                        if not end:
                            sp.wait_ge(turned, t * 2 + b + 1)
                            sp.dma_start(x[:, b, :], x_dram[bass.ds((t * 2 + 2 + b) * P, P), :]).then_inc(x_in[b], 16)
                    for b in range(2):
                        if later(t):
                            sp.wait_ge(base_out[b], t * 16)
                        sp.dma_start(enc[:, b, :], enc_dram[bass.ds((t * 2 + b) * P, P), :]).then_inc(enc_in[b], 16)
                    for b in range(2):
                        sp.wait_ge(ready, t * 8 + b * 4 + S_ + 1)
                        sp.dma_start(base_dram[bass.ds((t * 2 + b) * P, P), :], enc[:, b, :]).then_inc(base_out[b], 16)
                turns_ahead(sp, T2, pair)
                for b in range(2):
                    sp.wait_ge(base_out[b], 16 * T2)

            @block.tensor
            def _(pe):
                def flip(t, b):
                    pe.wait_ge(x_in[b], t * 16 + 16)
                    for k in range(KC):
                        last = pe.transpose(psT[b][:, k * P:(k + 1) * P], x[:, b, k * P:(k + 1) * P], T["ident"][:])
                    last.then_inc(turned, 1)

                flip(0, 0)

                def pair(t, end):
                    for b in range(2):
                        if not (end and b):
                            flip(t + b, 1 - b)
                        pe.wait_ge(xT_ready, t * 2 + b + 1)
                        for j in range(4):
                            if later(t) or b:
                                pe.wait_ge(ready, t * 8 + b * 4 + j - 3)
                            else:
                                pe.wait_ge(w_lows, (j + 1) * KC)
                            for k in range(KC):
                                last = product(pe, psP[j][:], [xT[:, b, i, k, :] for i in range(2)],
                                               [w[:, i, j * KC + k, :] for i in range(2)],
                                               start=(k == 0), stop=(k == KC - 1))
                            last.then_inc(projected, 1)
                turns_ahead(pe, T2, pair)

            @block.scalar
            def _(act):
                def high(t, b):
                    act.wait_ge(turned, t * 2 + b + 1)
                    act.copy(xT[:, b, 0].rearrange("p k n -> p (k n)"), psT[b][:]).then_inc(xT_high, 1)

                for i in range(4 * KC):
                    act.wait_ge(w_in[i % RAW], i // RAW * 16 + 16)
                    act.copy(w[:, 0, i, :], raw[:, i % RAW, :]).then_inc(w_highs, 1)
                    if i == KC - 1:
                        high(0, 0)

                def pair(t, end):
                    for b in range(2):
                        if not (end and b):
                            high(t + b, 1 - b)
                        for j, dram in ((K_, k_dram), (V_, v_dram)):
                            act.wait_ge(ready, t * 8 + b * 4 + j + 1)
                            act.dma_start(dram[bass.ds((t * 2 + b) * P, P), :], out[:, b, j - 1, :]).then_inc(kv_out[b], 16)
                turns_ahead(act, T2, pair)
                for b in range(2):
                    act.wait_ge(kv_out[b], 32 * T2)

            @block.vector
            def _(vec):
                def low(t, b):
                    vec.wait_ge(xT_high, t * 2 + b + 1)
                    vec.tensor_tensor(xT[:, b, 1].rearrange("p k n -> p (k n)"), psT[b][:],
                                      xT[:, b, 0].rearrange("p k n -> p (k n)").bitcast(F32),
                                      ALU.subtract).then_inc(xT_ready, 1)

                for i in range(4 * KC):
                    vec.wait_ge(w_highs, i + 1)
                    vec.tensor_tensor(w[:, 1, i, :], raw[:, i % RAW, :], w[:, 0, i, :].bitcast(F32),
                                      ALU.subtract).then_inc(w_lows, 1)
                    if i == KC - 1:
                        low(0, 0)
                vec.wait_ge(bias_in, 16 * 4)

                def pair(t, end):
                    for b in range(2):
                        if not (end and b):
                            low(t + b, 1 - b)
                        i = t * 2 + b
                        for j in range(4):
                            vec.wait_ge(projected, t * 8 + b * 4 + j + 1)
                            if j == S_:
                                vec.wait_ge(biased, i + 1)
                                vec.tensor_tensor(enc[:, b, :], psP[j][:], enc[:, b, :], ALU.add).then_inc(ready, 1)
                                continue
                            if later(t) and j == K_:
                                vec.wait_ge(kv_out[b], t * 32)
                            vec.tensor_tensor(out[:, b, j - 1, :], psP[j][:], bias[:, j, :], ALU.add).then_inc(ready, 1)
                        c = Chain(vec, split, i * 5)
                        q = out[:, b, Q_ - 1, :]
                        part = [one(qp[:, k, bass.ds(i, 1), :]) for k in range(3)]
                        vec.wait_ge(ready, t * 8 + b * 4 + Q_ + 1)
                        for k in range(2):
                            c.then(vec.tensor_scalar(part[k], q, 1.0, None, ALU.mult))
                            c.wait()
                            c.then(vec.tensor_tensor(q, q, part[k], ALU.subtract))
                            c.wait()
                        c.then(vec.tensor_scalar(part[2], q, 1.0, None, ALU.mult))
                turns_ahead(vec, T2, pair)

            @block.gpsimd
            def _(pool):
                pool.wait_ge(bias_in, 16 * 4)

                def pair(t):
                    for b in range(2):
                        pool.wait_ge(enc_in[b], t * 16 + 16)
                        pool.tensor_tensor(enc[:, b, :], enc[:, b, :], bias[:, S_, :], ALU.add).then_inc(biased, 1)
                turns(pool, T2, pair)


def gather(pool, T, t, half, bufs, index, table, landed, copied, started, freed, later_):
    h = U // 2
    if later_:
        pool.wait_ge(freed, (t - 1) * U + half * h + h)
    pool.tensor_copy(index[:, half, :], T["src"][:, bass.ds(t * U + half * h, h)]).then_inc(copied, 1)
    pool.wait_ge(copied, t * 2 + half + 1)
    pool.sem_inc(started, 1)
    for u in range(half * h, half * h + h):
        pool.indirect_dma_start(bufs[:, u, :], None, table,
                                bass.IndirectOffsetOnAxis(ap=index[:, half, u - half * h:u - half * h + 1], axis=0)
                                ).then_inc(landed[u], 16)


def node_tiles(nc, engine, T, slot, n):
    return nc.values_load_multi_w_load_instructions(T["tile_of"][0:1, bass.ds(slot, n)], engines=[engine.engine],
                                                    min_val=0, max_val=NT - 1)[1]


def score_edges(nc, a, T, layer, k_dram, scores):
    with ExitStack() as stack:
        m = Memory(nc, stack, f"score{layer}")
        h, B = U // 2, 4
        kbuf = m.sb("kbuf", [P, U, C])
        index = m.sb("index", [P, 2, h], I32)
        hot = m.sb("hot", [P, U, P], BF16)
        hotT = m.sb("hotT", [P, 2, B, P], BF16)
        prod = m.sb("prod", [P, 2, B, C])
        found = m.sb("found", [P, U, H])
        psT = [m.ps(f"psT{i}", [P, B, P], BF16) for i in range(2)]
        psQ = [m.ps(f"psQ{i}", [P, C]) for i in range(B)]
        landed = [m.sem(f"landed{u}") for u in range(U)]
        copied, hots, turned, hotT_ready, queried, multiplied, reduced, kept = (
            m.sem(x) for x in ("copied", "hots", "turned", "hotT_ready", "queried", "multiplied", "reduced", "kept"))
        started = m.sem("started")
        qp, local = T["q_parts"], T["local"]
        with nc.Block() as block:
            @block.gpsimd
            def _(pool):
                def turn(t):
                    for half in range(2):
                        gather(pool, T, t, half, kbuf, index, k_dram, landed, copied, started, multiplied, later(t))
                turns(pool, TURNS, turn)

            @block.vector
            def _(vec):
                def one_hot(slot, u, sem_value=None):
                    if sem_value is not None:
                        vec.wait_ge(turned, sem_value)
                    vec.tensor_scalar(hot[:, u, :], T["laneb"][:], local[:, bass.ds(slot, 1)], None,
                                      ALU.is_equal).then_inc(hots, 1)

                for u in range(h):
                    one_hot(u, u)

                def turn(t):
                    for j in range(U // B):
                        for u in range(j * B + h, j * B + h + B):
                            before = t * (U // B) + j + 2 - U // B + 1
                            first = u % B == 0
                            one_hot(t * U + u, u % U, before if first and (later(t) or u >= U) else None)
                        pb = j % 2
                        for i in range(B):
                            u = j * B + i
                            vec.wait_ge(landed[u], t * 16 + 16)
                            vec.wait_ge(queried, t * U + u + 1)
                            vec.tensor_tensor(prod[:, pb, i, :], psQ[i][:], kbuf[:, u, :],
                                              ALU.mult).then_inc(multiplied, 1)
                        vec.wait_ge(multiplied, t * U + j * B + B)
                        if later(t) and j == 0:
                            vec.wait_ge(kept, t)
                        vec.tensor_reduce(found[:, j * B:(j + 1) * B, :],
                                          prod[:, pb].rearrange("p i (h d) -> p i h d", h=H), AX.X,
                                          ALU.add).then_inc(reduced, 1)
                    vec.wait_ge(reduced, t * (U // B) + U // B)
                    vec.tensor_scalar(scores[:, bass.ds(t * U * H, U * H)], found[:].rearrange("p u h -> p (u h)"),
                                      1.0, None, ALU.mult).then_inc(kept, 1)
                turns(vec, TURNS, turn)

            @block.tensor
            def _(pe):
                def flip(batch, j):
                    pe.wait_ge(hots, batch * B + B)
                    for i in range(B):
                        last = pe.transpose(psT[j % 2][:, i, :], hot[:, (j * B + i) % U, :], T["identb"][:])
                    last.then_inc(turned, 1)

                flip(0, 0)

                def turn(t):
                    for j in range(U // B):
                        batch = t * (U // B) + j
                        flip(batch + 1, j + 1)
                        tiles = node_tiles(nc, pe, T, t * U + j * B, B)
                        pe.wait_ge(hotT_ready, batch + 1)
                        for i in range(B):
                            u = j * B + i
                            d = tiles[i]
                            if later(t) or j:
                                pe.wait_ge(multiplied, t * U + u - B + 1)
                            for k in range(3):
                                last = pe.matmul(psQ[i][:], hotT[:, j % 2, i, :], one(qp[:, k, bass.ds(d, 1), :]),
                                                 start=(k == 0), stop=(k == 2))
                            last.then_inc(queried, 1)
                turns(pe, TURNS, turn)

            @block.scalar
            def _(act):
                def turn(t):
                    for j in range(U // B):
                        batch = t * (U // B) + j
                        act.wait_ge(turned, batch + 1)
                        if later(t) or j >= 2:
                            act.wait_ge(queried, batch * B - B)
                        act.copy(hotT[:, j % 2].rearrange("p i e -> p (i e)"),
                                 psT[j % 2][:].rearrange("p i e -> p (i e)")).then_inc(hotT_ready, 1)
                turns(act, TURNS, turn)


def soften(nc, T, layer, scores, weights):
    with ExitStack() as stack:
        m = Memory(nc, stack, f"soft{layer}")
        near = m.sb("near", [P, G, P])
        rows = m.sb("rows", [P, RUN])
        run = m.sb("run", [P, RUN])
        top = m.sb("top", [P, RUN])
        ends = m.sb("ends", [P, 2, CH])
        pair = m.sb("pair", [H, 2 * CH, 2 * CH])
        best = m.sb("best", [H, 2 * CH])
        back = m.sb("back", [P, 2, CH])
        shared = m.sb("shared", [P, 2])
        pst = [m.ps(f"pst{i}", [P, 4, P]) for i in range(2)]
        psw = [m.ps(f"psw{i}", [P, 4, P]) for i in range(2)]
        pse = m.ps("pse", [H, 2 * CH])
        psb = m.ps("psb", [P, 2 * CH])
        nearby = m.sem("nearby")
        turned, in_rows, steps, ends_done, ends_in, best_done, best_out, ready, exped, returned, stored = (
            m.sem(x) for x in ("turned", "in_rows", "steps", "ends_done", "ends_in", "best_done", "best_out", "ready",
                               "exped", "returned", "stored"))
        parts = [(g, min(4, G - g)) for g in range(0, G, 4)]
        by_g = scores[:].rearrange("p (c g h) -> p g c h", c=CH, g=G)
        w_by_g = weights[:].rearrange("p (c g h) -> p g c h", c=CH, g=G)
        with nc.Block() as block:
            @block.tensor
            def _(pe):
                for n, (g, k) in enumerate(parts):
                    pe.wait_ge(nearby, n + 1)
                    if n >= 2:
                        pe.wait_ge(in_rows, n - 1)
                    for j in range(k):
                        last = pe.transpose(pst[n % 2][:, j, :], near[:, g + j, :], T["ident"][:])
                    last.then_inc(turned, 1)
                pe.wait_ge(ends_done, 1)
                pe.matmul(pse[:], T["head_of"][:], ends[:].rearrange("p e c -> p (e c)"), start=True,
                          stop=True).then_inc(ends_in, 1)
                pe.wait_ge(best_done, 1)
                pe.matmul(psb[:], T["of_head"][:], best[:], start=True, stop=True).then_inc(best_out, 1)
                for n, (g, k) in enumerate(parts):
                    pe.wait_ge(exped, n + 1)
                    if n >= 2:
                        pe.wait_ge(stored, n - 1)
                    for j in range(k):
                        last = pe.transpose(psw[n % 2][:, j, :], rows[:, (g + j) * P:(g + j + 1) * P], T["ident"][:])
                    last.then_inc(returned, 1)

            @block.scalar
            def _(act):
                for n, (g, k) in enumerate(parts):
                    act.copy(near[:, g:g + k, :].rearrange("p k (c h) -> p k c h", c=CH), by_g[:, g:g + k]
                             ).then_inc(nearby, 1)
                for n, (g, k) in enumerate(parts):
                    act.wait_ge(ready, n + 1)
                    act.activation(rows[:, g * P:(g + k) * P], rows[:, g * P:(g + k) * P], ACT.Exp,
                                   scale=float(D) ** -0.5).then_inc(exped, 1)

            @block.vector
            def _(vec):
                c = Chain(vec, steps)
                same, first, last = T["same"], T["first"], T["last"]
                for n, (g, k) in enumerate(parts):
                    vec.wait_ge(turned, n + 1)
                    vec.tensor_copy(rows[:, g * P:(g + k) * P], pst[n % 2][:, 0:k, :].rearrange("p k e -> p (k e)")
                                    ).then_inc(in_rows, 1)
                vec.wait_ge(in_rows, len(parts))
                c.then(vec.tensor_tensor_scan(run[:], same[:, 0:RUN], rows[:], NEG, ALU.add, ALU.max))
                c.wait()
                c.then(vec.tensor_tensor_scan(top[:, RUN - 1::-1], same[:, RUN:0:-1], run[:, RUN - 1::-1], NEG,
                                              ALU.add, ALU.max))
                c.wait()
                c.then(vec.tensor_scalar(ends[:, 0, :], T["chunk_of"][:], top[:, 0:1], None, ALU.mult))
                c.then(vec.tensor_scalar(ends[:, 1, :], T["chunk_of"][:], top[:, RUN - 1:RUN], None, ALU.mult))
                c.wait()
                vec.nop().then_inc(ends_done, 1)
                vec.wait_ge(ends_in, 1)
                c.then(vec.tensor_tensor(pair[:], T["linked"][:],
                                         pse[:].unsqueeze(1).to_broadcast([H, 2 * CH, 2 * CH]), ALU.add))
                c.wait()
                vec.tensor_reduce(best[:], pair[:], AX.X, ALU.max).then_inc(best_done, 1)
                vec.wait_ge(best_out, 1)
                c.then(vec.tensor_tensor(back[:], psb[:].rearrange("p (e c) -> p e c", e=2),
                                         T["chunk_of"][:].unsqueeze(1).to_broadcast([P, 2, CH]), ALU.mult))
                c.wait()
                c.then(vec.tensor_reduce(shared[:], back[:], AX.X, ALU.add))
                c.wait()
                c.then(vec.scalar_tensor_tensor(out=top[:], in0=first[:], scalar=shared[:, 0:1], in1=top[:],
                                                op0=ALU.add, op1=ALU.max))
                c.wait()
                c.then(vec.scalar_tensor_tensor(out=top[:], in0=last[:], scalar=shared[:, 1:2], in1=top[:],
                                                op0=ALU.add, op1=ALU.max))
                c.wait()
                for n, (g, k) in enumerate(parts):
                    s = slice(g * P, (g + k) * P)
                    vec.tensor_tensor(rows[:, s], rows[:, s], top[:, s], ALU.subtract).then_inc(ready, 1)
                for n, (g, k) in enumerate(parts):
                    vec.wait_ge(returned, n + 1)
                    vec.tensor_copy(w_by_g[:, g:g + k], psw[n % 2][:, 0:k, :].rearrange("p k (c h) -> p k c h", c=CH)
                                    ).then_inc(stored, 1)


def aggregate(nc, a, T, layer, v_dram, weights, agg):
    with ExitStack() as stack:
        m = Memory(nc, stack, f"agg{layer}")
        h, B, R = U // 2, 4, 8
        vbuf = m.sb("vbuf", [P, U, C])
        index = m.sb("index", [P, 2, h], I32)
        hot = m.sb("hot", [P, U, P])
        wt = m.sb("wt", [P, 2, h, H])
        wv = m.sb("wv", [P, R, AW])
        zeros = m.sb("zeros", [P, 2, C // 2 + H])
        psA = m.ps("psA", [P, 2, 2, C])
        landed = [m.sem(f"landed{u}") for u in range(U)]
        copied, hots, staged, beside, weighted, summed, blank, evicted, kept, started = (
            m.sem(x) for x in ("copied", "hots", "staged", "beside", "weighted", "summed", "blank", "evicted",
                               "kept", "started"))
        local = T["local"]
        parts = ((0, C // 2), (C // 2, AW))
        with nc.Block() as block:
            @block.gpsimd
            def _(pool):
                def turn(t):
                    for half in range(2):
                        gather(pool, T, t, half, vbuf, index, v_dram, landed, copied, started, weighted, later(t))
                turns(pool, TURNS, turn)

            @block.vector
            def _(vec):
                vec.memset(zeros[:], 0.0).then_inc(blank, 1)

                def stage(t, half):
                    if later(t):
                        vec.wait_ge(weighted, (t - 1) * U + half * h + h)
                        vec.wait_ge(beside, (t - 1) * (U // B) + (half * h + h) // B)
                    vec.tensor_scalar(wt[:, half].rearrange("p u h -> p (u h)"),
                                      weights[:, bass.ds((t * U + half * h) * H, h * H)],
                                      1.0, None, ALU.mult).then_inc(staged, 1)
                    vec.wait_ge(staged, t * 2 + half + 1)

                def turn(t):
                    for u in range(U):
                        if u % h == 0:
                            stage(t, u // h)
                        if later(t):
                            vec.wait_ge(summed, t * U + u + 2 - U)
                        vec.tensor_scalar(hot[:, u, :], T["lane"][:], local[:, bass.ds(t * U + u, 1)], None,
                                          ALU.is_equal).then_inc(hots, 1)
                        if u % B == 0:
                            if later(t) or u >= R:
                                vec.wait_ge(summed, t * U + u + B + 1 - R)
                            vec.tensor_scalar(wv[:, u % R:u % R + B, C:AW], wt[:, u // h, u % h:u % h + B, :], 1.0, None,
                                              ALU.mult).then_inc(beside, 1)
                        vec.wait_ge(landed[u], t * 16 + 16)
                        vec.tensor_tensor(wv[:, u % R, 0:C].rearrange("p (h d) -> p h d", h=H),
                                          vbuf[:, u, :].rearrange("p (h d) -> p h d", h=H),
                                          wt[:, u // h, u % h, :].unsqueeze(2).to_broadcast([P, H, D]),
                                          ALU.mult).then_inc(weighted, 1)
                turns(vec, TURNS, turn)

            @block.scalar
            def _(act):
                act.wait_ge(blank, 1)
                act.sem_inc(evicted, 2)
                for d in range(NT):
                    full = act.value_load(T["full_at"][0:1, d:d + 1], min_val=1, max_val=SLOTS + 1)
                    act.wait_ge(summed, full if d < NT - 1 else SLOTS + 1)
                    for e, (lo, hi) in enumerate(parts):
                        act.copy(agg[:, d, lo:hi], psA[:, d % 2, e, 0:hi - lo]).then_inc(kept, 1)
                    act.wait_ge(kept, 2 * d + 2)
                    act.copy(psA[:, d % 2, :, 0:C // 2 + H], zeros[:]).then_inc(evicted, 1)

            @block.tensor
            def _(pe):
                pe.wait_ge(blank, 1)
                for bank in range(2):
                    for e in range(2):
                        last = pe.matmul(psA[:, bank, e, 0:C // 2 + H], T["ident"][:], zeros[:, e, :], start=True,
                                         stop=True)
                last.then_inc(summed, 1)

                def turn(t):
                    for u in range(U):
                        if u % B == 0:
                            tiles = node_tiles(nc, pe, T, t * U + u, B)
                        d = tiles[u % B]
                        pe.wait_ge(hots, t * U + u + 1)
                        pe.wait_ge(beside, t * (U // B) + u // B + 1)
                        pe.wait_ge(weighted, t * U + u + 1)
                        pe.wait_ge(evicted, d + 1)
                        for e, (lo, hi) in enumerate(parts):
                            last = pe.matmul(psA[:, bass.ds(d % 2, 1), e, 0:hi - lo].rearrange("p o w -> p (o w)"),
                                             hot[:, u, :], wv[:, u % R, lo:hi], start=False, stop=True,
                                             skip_group_check=True)
                        last.then_inc(summed, 1)
                turns(pe, TURNS, turn)



def combine(nc, a, T, layer, agg, base_dram, out_dram):
    final = layer == LAYERS - 1
    with ExitStack() as stack:
        m = Memory(nc, stack, f"comb{layer}")
        x = m.sb("x", [P, NT, C])
        den = m.sb("den", [P, NT, H])
        gb = m.sb("gb", [P, 2, C])
        landed, steps, done, stored = (m.sem(s) for s in ("landed", "steps", "done", "stored"))
        ln = LayerNorm(nc, m, NT) if final else None
        with nc.Block() as block:
            @block.sync
            def _(sp):
                sp.dma_start(x[:], base_dram.rearrange("(t p) c -> p t c", p=P)).then_inc(landed, 16)
                if final:
                    sp.dma_start(gb[:, 0], a["L0_gnn_ln_g"].partition_broadcast(P)).then_inc(landed, 16)
                    sp.dma_start(gb[:, 1], a["L0_gnn_ln_b"].partition_broadcast(P)).then_inc(landed, 16)
                for t in range(NT):
                    sp.wait_ge(done, t + 1)
                    sp.dma_start(out_dram[t * P:(t + 1) * P, :], x[:, t, :]).then_inc(stored, 16)
                sp.wait_ge(stored, 16 * NT)

            @block.vector
            def _(vec):
                c = Chain(vec, steps)
                c.then(vec.tensor_scalar(den[:], agg[:, :, C:AW], 1e-16, None, ALU.add))
                c.wait()
                c.then(vec.reciprocal(den[:], den[:]))
                c.wait()
                for t in range(NT):
                    at = agg[:, t, 0:C].rearrange("p (h d) -> p h d", h=H)
                    c.then(vec.tensor_tensor(at, at, den[:, t].unsqueeze(2).to_broadcast([P, H, D]), ALU.mult))
                vec.wait_ge(landed, 48 if final else 16)
                c.wait()
                for t in range(NT):
                    ins = vec.tensor_tensor(x[:, t, :], x[:, t, :], agg[:, t, 0:C], ALU.add)
                    if final:
                        c.then(ins)
                    else:
                        ins.then_inc(done, 1)
                if final:
                    c.wait()
                    ln.stats(vec, lambda t: x[:, t, :])
                    ln.scale(vec)
                    for t in range(NT):
                        c.then(ln.apply(vec, t, x[:, t, :], x[:, t, :]))
                    c.wait()
                    for t in range(NT):
                        c.then(vec.tensor_tensor(x[:, t, :], x[:, t, :], gb[:, 0], ALU.mult))
                    c.wait()
                    for t in range(NT):
                        vec.tensor_tensor(x[:, t, :], x[:, t, :], gb[:, 1], ALU.add).then_inc(done, 1)

            @block.gpsimd
            def _(pool):
                if final:
                    ln.set_eps(pool)

            @block.scalar
            def _(act):
                if final:
                    ln.root(act)


class LayerNorm:

    def __init__(self, nc, m, n):
        self.n = n
        self.st = m.sb("ln_stats", [P, n, 6])
        self.mv = m.sb("ln_mv", [P, n, 2])
        self.eps = m.sb("ln_eps", [P, 1])
        self.std = m.sb("ln_std", [P, n])
        self.rstd = m.sb("ln_rstd", [P, n])
        self.all_st = m.sem("ln_all_st")
        self.have_eps, self.have_st, self.have_mv, self.have_std, self.have_rstd = (
            m.sem(x) for x in ("ln_have_eps", "ln_have_st", "ln_have_mv", "ln_have_std", "ln_have_rstd"))

    def set_eps(self, engine):
        engine.memset(self.eps[:], EPS).then_inc(self.have_eps, 1)

    def stats(self, vec, row, turn=0):
        for t in range(self.n):
            vec.bn_stats(self.st[:, t, :], row(t)).then_inc(self.have_st, 1)
        vec.wait_ge(self.have_st, (turn + 1) * self.n)
        vec.sem_inc(self.all_st, 1)
        for t in range(self.n):
            vec.bn_aggr(self.mv[:, t, :], self.st[:, t, :]).then_inc(self.have_mv, 1)

    def root(self, act, turn=0):
        if isinstance(turn, int) and turn == 0:
            act.wait_ge(self.have_eps, 1)
        act.wait_ge(self.have_mv, (turn + 1) * self.n)
        act.activation(self.std[:], self.mv[:, :, 1], ACT.Sqrt, bias=self.eps[:, 0:1]).then_inc(self.have_std, 1)

    def scale(self, vec, turn=0):
        vec.wait_ge(self.have_std, turn + 1)
        vec.reciprocal(self.rstd[:], self.std[:]).then_inc(self.have_rstd, 1)
        vec.wait_ge(self.have_rstd, turn + 1)
        vec.wait_ge(self.have_mv, (turn + 1) * self.n)

    def apply(self, vec, t, out, in_):
        return vec.tensor_scalar(out, in_, self.mv[:, t, 0:1], self.rstd[:, t:t + 1], ALU.subtract, ALU.mult)


def turn_group(pe, T, tile, psT, turned, free, wait_free):
    for n in range(GN):
        if wait_free(n) is not None:
            pe.wait_ge(free, wait_free(n))
        for k in range(KC):
            last = pe.transpose(psT[n % 2][:, k, :], tile[:, n, k * P:(k + 1) * P], T["ident"][:])
        last.then_inc(turned, 1)


def node_mlp(nc, a, T, y_dram, enc_dram, out_dram):
    with ExitStack() as stack:
        m = Memory(nc, stack, "mlp")
        FC = F1 // P
        raw1 = m.sb("raw1", [P, KC, F1])
        raw2 = m.sb("raw2", [P, FC, C])
        w1 = m.sb("w1", [P, 2, KC, F1], F32R)
        w2 = m.sb("w2", [P, 2, FC, C], F32R)
        b1 = m.sb("b1", [P, FC])
        rowsb = m.sb("rowsb", [P, 3, C])
        y = m.sb("y", [P, GN, C])
        yres = m.sb("yres", [P, GN, C])
        enc = m.sb("enc", [P, GN, C])
        yT = m.sb("yT", [P, 2, KC, NODES], F32R)
        h = m.sb("h", [P, 2, NODES])
        hT = m.sb("hT", [P, 2, FC, NODES], F32R)
        z = m.sb("z", [P, GN, C])
        psT = [m.ps(f"psT{i}", [P, KC, P]) for i in range(2)]
        psH = [m.ps(f"psH{i}", [P, NODES]) for i in range(2)]
        psO = [m.ps(f"psO{i}", [P, C]) for i in range(2)]
        w1_in, w2_in, b_in, w_highs, w_lows = (m.sem(s) for s in ("w1_in", "w2_in", "b_in", "w_highs", "w_lows"))
        (y_in, yres_in, enc_in, turned, yT_high, yT_in, hidden, h_in, hT_high, hT_in, out_done, z_in, steps, done,
         stored) = (
            m.sem(s) for s in ("y_in", "yres_in", "enc_in", "turned", "yT_high", "yT_in", "hidden", "h_in", "hT_high",
                               "hT_in", "out_done", "z_in", "steps", "done", "stored"))
        ln = LayerNorm(nc, m, GN)

        def rows_of(dram, g):
            return dram[bass.ds(g * NODES, NODES), :].rearrange("(t p) c -> p t c", p=P)

        def over(j):
            return rowsb[:, j, :].unsqueeze(1).to_broadcast([P, GN, C])

        with nc.Block() as block:
            @block.sync
            def _(sp):
                sp.dma_start(y[:], rows_of(y_dram, 0)).then_inc(y_in, 16)
                sp.dma_start(raw1[:], a["L0_gnn_W1"].rearrange("(k p) n -> p k n", p=P)).then_inc(w1_in, 16)
                sp.dma_start(b1[:], a["L0_gnn_b1"].rearrange("(f p) -> p f", p=P), allow_slow_non_contiguous=True
                             ).then_inc(b_in, 16)
                sp.dma_start(raw2[:], a["L0_gnn_W2"].rearrange("(k p) n -> p k n", p=P)).then_inc(w2_in, 16)
                for j, n in enumerate(("b2", "ln_g", "ln_b")):
                    sp.dma_start(rowsb[:, j], a[f"L0_gnn_{n}"].partition_broadcast(P)).then_inc(b_in, 16)
                sp.dma_start(yres[:], rows_of(y_dram, 0)).then_inc(yres_in, 16)
                sp.dma_start(enc[:], rows_of(enc_dram, 0)).then_inc(enc_in, 16)

                def group(g, end):
                    if not end:
                        sp.wait_ge(turned, g * GN + GN)
                        sp.dma_start(y[:], rows_of(y_dram, g + 1)).then_inc(y_in, 16)
                        sp.wait_ge(z_in, g * GN + GN)
                        sp.dma_start(yres[:], rows_of(y_dram, g + 1)).then_inc(yres_in, 16)
                    sp.wait_ge(done, g + 1)
                    sp.dma_start(rows_of(out_dram, g), z[:]).then_inc(stored, 16)
                    if not end:
                        sp.dma_start(enc[:], rows_of(enc_dram, g + 1)).then_inc(enc_in, 16)
                turns_ahead(sp, GROUPS, group)
                sp.wait_ge(stored, 16 * GROUPS)

            @block.tensor
            def _(pe):
                def flip(g, n):
                    if n == 0:
                        pe.wait_ge(y_in, g * 16 + 16)
                    if later(g) or n >= 2:
                        pe.wait_ge(yT_in, g * GN + n - 1)
                    for k in range(KC):
                        last = pe.transpose(psT[n % 2][:, k, :], y[:, n, k * P:(k + 1) * P], T["ident"][:])
                    last.then_inc(turned, 1)

                for n in range(GN):
                    flip(0, n)

                def group(g, end):
                    if not later(g):
                        pe.wait_ge(w_lows, 1)
                    pe.wait_ge(yT_in, g * GN + GN)
                    for f in range(FC):
                        if later(g) or f >= 2:
                            pe.wait_ge(h_in, g * FC + f - 1)
                        fs = slice(f * P, (f + 1) * P)
                        for k in range(KC):
                            last = product(pe, psH[f % 2][:], [w1[:, i, k, fs] for i in range(2)],
                                           [yT[:, i, k, :] for i in range(2)], start=(k == 0), stop=(k == KC - 1))
                        last.then_inc(hidden, 1)
                    if not end:
                        flip(g + 1, 0)
                        flip(g + 1, 1)
                    if not later(g):
                        pe.wait_ge(w_lows, 2)
                    pe.wait_ge(hT_in, g * FC + FC)
                    for n in range(GN):
                        if later(g) or n >= 2:
                            pe.wait_ge(z_in, g * GN + n - 1)
                        for f in range(FC):
                            last = product(pe, psO[n % 2][:], [hT[:, i, f, n * P:(n + 1) * P] for i in range(2)],
                                           [w2[:, i, f, :] for i in range(2)], start=(f == 0),
                                           stop=(f == FC - 1))
                        last.then_inc(out_done, 1)
                        if not end and n + 2 < GN:
                            flip(g + 1, n + 2)
                turns_ahead(pe, GROUPS, group)

            @block.scalar
            def _(act):
                def high(g, n):
                    act.wait_ge(turned, g * GN + n + 1)
                    act.copy(yT[:, 0, :, n * P:(n + 1) * P], psT[n % 2][:]).then_inc(yT_high, 1)

                act.wait_ge(w1_in, 16)
                act.copy(w1[:, 0], raw1[:]).then_inc(w_highs, 1)
                for n in range(GN):
                    high(0, n)
                act.wait_ge(w2_in, 16)
                act.copy(w2[:, 0], raw2[:]).then_inc(w_highs, 1)
                act.wait_ge(b_in, 16 * 4)

                def group(g, end):
                    for f in range(FC):
                        act.wait_ge(hidden, g * FC + f + 1)
                        if later(g) or f >= 2:
                            act.wait_ge(hT_in, g * FC + f - 1)
                        act.activation(h[:, f % 2, :], psH[f % 2][:], ACT.Relu, bias=b1[:, f:f + 1]).then_inc(h_in, 1)
                        act.wait_ge(h_in, g * FC + f + 1)
                        act.copy(hT[:, 0, f, :], h[:, f % 2, :]).then_inc(hT_high, 1)
                    if not end:
                        for n in range(GN):
                            high(g + 1, n)
                    ln.root(act, g)
                turns_ahead(act, GROUPS, group)

            @block.gpsimd
            def _(pool):
                ln.set_eps(pool)

                def group(g):
                    for f in range(FC):
                        pool.wait_ge(hT_high, g * FC + f + 1)
                        pool.tensor_tensor(hT[:, 1, f, :], h[:, f % 2, :], hT[:, 0, f, :].bitcast(F32),
                                           ALU.subtract).then_inc(hT_in, 1)
                turns(pool, GROUPS, group)

            @block.vector
            def _(vec):
                def low(g, n):
                    vec.wait_ge(yT_high, g * GN + n + 1)
                    vec.tensor_tensor(yT[:, 1, :, n * P:(n + 1) * P], psT[n % 2][:],
                                      yT[:, 0, :, n * P:(n + 1) * P].bitcast(F32), ALU.subtract).then_inc(yT_in, 1)

                vec.wait_ge(w_highs, 1)
                vec.tensor_tensor(w1[:, 1], raw1[:], w1[:, 0].bitcast(F32), ALU.subtract).then_inc(w_lows, 1)
                for n in range(GN):
                    low(0, n)
                vec.wait_ge(w_highs, 2)
                vec.tensor_tensor(w2[:, 1], raw2[:], w2[:, 0].bitcast(F32), ALU.subtract).then_inc(w_lows, 1)
                vec.wait_ge(b_in, 16 * 4)

                def group(g, end):
                    c = Chain(vec, steps, g * (1 + GN + 2))
                    if not end:
                        low(g + 1, 0)
                        low(g + 1, 1)
                    vec.wait_ge(yres_in, g * 16 + 16)
                    if later(g):
                        vec.wait_ge(stored, g * 16)
                    for n in range(GN):
                        vec.wait_ge(out_done, g * GN + n + 1)
                        vec.tensor_tensor(z[:, n, :], psO[n % 2][:], yres[:, n, :], ALU.add).then_inc(z_in, 1)
                        if not end and n + 2 < GN:
                            low(g + 1, n + 2)
                    vec.wait_ge(z_in, g * GN + GN)
                    c.then(vec.tensor_tensor(z[:], z[:], over(0), ALU.add))
                    c.wait()
                    ln.stats(vec, lambda n: z[:, n, :], g)
                    ln.scale(vec, g)
                    for n in range(GN):
                        c.then(ln.apply(vec, n, z[:, n, :], z[:, n, :]))
                    c.wait()
                    c.then(vec.tensor_tensor(z[:], z[:], over(1), ALU.mult))
                    c.wait()
                    c.then(vec.tensor_tensor(z[:], z[:], over(2), ALU.add))
                    c.wait()
                    vec.wait_ge(enc_in, g * 16 + 16)
                    vec.tensor_tensor(z[:], z[:], enc[:], ALU.add).then_inc(done, 1)
                turns_ahead(vec, GROUPS, group)


def mix_slices(nc, a, T, xn_dram, gnn_dram, x3_dram, y3_dram):
    with ExitStack() as stack:
        m = Memory(nc, stack, "mix")
        qT = m.sb("qT", [P, 2, NP])
        folded = m.sb("folded", [P, 2, C])
        project_slices(nc, a, T, xn_dram, qT, folded)
        spread_slices(nc, a, T, qT, folded, gnn_dram, x3_dram, y3_dram)


def project_slices(nc, a, T, xn_dram, qT, folded):
    with ExitStack() as stack:
        m = Memory(nc, stack, "slice")
        HS = H * SL
        VW = 4 * D + 1
        w_in = m.sb("w_in", [P, KC, C])
        w_out = m.sb("w_out", [P, KC, C])
        b_in = m.sb("b_in", [P, KC])
        wqkv = m.sb("wqkv", [P, 2 * (2 * SL + D)])
        x = m.sb("x", [P, GN, C])
        xT = m.sb("xT", [P, KC, NODES])
        mid = m.sb("mid", [P, KC, NODES])
        q = m.sb("q", [P, GN, HS])
        qsum = m.sb("qsum", [P, GN * H])
        kall = m.sb("kall", [P, NT, HS])
        vall = m.sb("vall", [P, NT, 2, VW])
        kmax = m.sb("kmax", [P, HS])
        ktop = m.sb("ktop", [P, 2])
        kdiag = m.sb("kdiag", [P, 2, P])
        ones = m.sb("ones", [P, P])
        ksum = m.sb("ksum", [P, 2])
        kv = m.sb("kv", [P, 2, 4 * D])
        kvT = m.sb("kvT", [P, 2, 2, P])
        psT = [m.ps(f"psT{i}", [P, KC, P]) for i in range(2)]
        psM = [m.ps(f"psM{i}", [P, NODES]) for i in range(2)]
        psQ = [m.ps(f"psQ{i}", [P, KC, 4 * D]) for i in range(2)]
        names = ("zeroed", "w_landed", "x_in", "turned", "xT_in", "middled", "mid_in", "projected", "q_in", "kv_in",
                 "kmaxed", "steps", "shifted", "exped", "normed", "q_turned", "qT_in", "kflip", "ktopped", "kspread",
                 "kshifted", "kexped", "kv_done", "kv_in2", "kvflip", "kvT_in", "fold_done", "ones_in", "fixed")
        s = {n: m.sem(n) for n in names}
        W2 = 2 * SL
        with nc.Block() as block:
            @block.gpsimd
            def _(pool):
                pool.memset(wqkv[:], 0.0).then_inc(s["zeroed"], 1)
                pool.memset(ones[:], 1.0).then_inc(s["ones_in"], 1)
                pool.memset(vall[:, :, :, 4 * D:VW], 1.0).then_inc(s["ones_in"], 1)
                pool.memset(kmax[:], -3e38).then_inc(s["ones_in"], 1)
                pool.memset(kv[:], 0.0).then_inc(s["ones_in"], 1)

            @block.sync
            def _(sp):
                sp.dma_start(w_in[:], a["L0_mix_W_in"].rearrange("(k p) n -> p k n", p=P)).then_inc(s["w_landed"], 16)
                sp.dma_start(w_out[:], a["L0_mix_W_out"].rearrange("(k p) n -> p k n", p=P)).then_inc(s["w_landed"], 16)
                sp.dma_start(b_in[:], a["L0_mix_b_in"].rearrange("(k p) -> p k", p=P), allow_slow_non_contiguous=True).then_inc(s["w_landed"], 16)
                sp.wait_ge(s["zeroed"], 1)
                for j in range(2):
                    r = slice(j * D, (j + 1) * D)
                    sp.dma_start(wqkv[r, j * SL:(j + 1) * SL], a["L0_mix_Wq"]).then_inc(s["w_landed"], 16)
                    sp.dma_start(wqkv[r, W2 + j * SL:W2 + (j + 1) * SL], a["L0_mix_Wk"]).then_inc(s["w_landed"], 16)
                    sp.dma_start(wqkv[r, 2 * W2 + j * D:2 * W2 + (j + 1) * D], a["L0_mix_Wv"]).then_inc(s["w_landed"], 16)

                def group(g):
                    if later(g):
                        sp.wait_ge(s["turned"], g * GN)
                    sp.dma_start(x[:], xn_dram[bass.ds(g * NODES, NODES), :].rearrange("(t p) c -> p t c", p=P)
                                 ).then_inc(s["x_in"], 16)
                turns(sp, GROUPS, group)

            @block.tensor
            def _(pe):
                pe.wait_ge(s["w_landed"], 16 * 9)

                def group(g):
                    pe.wait_ge(s["x_in"], g * 16 + 16)
                    if later(g):
                        pe.wait_ge(s["qT_in"], g * 2)
                    turn_group(pe, T, x, psT, s["turned"], s["xT_in"], lambda n: g * GN + n - 1 if n >= 2 else None)
                    pe.wait_ge(s["xT_in"], g * GN + GN)
                    for c in range(KC):
                        if later(g) or c >= 2:
                            pe.wait_ge(s["mid_in"], g * KC + c - 1)
                        for k in range(KC):
                            last = pe.matmul(psM[c % 2][:], w_in[:, k, c * P:(c + 1) * P], xT[:, k, :], start=(k == 0),
                                             stop=(k == KC - 1))
                        last.then_inc(s["middled"], 1)
                    pe.wait_ge(s["mid_in"], g * KC + KC)
                    for n in range(GN):
                        if later(g) or n >= 2:
                            pe.wait_ge(s["kv_in"], g * GN + n - 1)
                            pe.wait_ge(s["kmaxed"], g * GN + n - 1)
                        for c in range(KC):
                            last = pe.matmul(psQ[n % 2][:, c, :], mid[:, c, n * P:(n + 1) * P], wqkv[:], start=True,
                                             stop=True)
                        last.then_inc(s["projected"], 1)
                    pe.wait_ge(s["normed"], g + 1)
                    for e in range(2):
                        for n in range(GN):
                            last = pe.transpose(psT[e][:, n, :], q[:, n, e * P:(e + 1) * P], T["ident"][:])
                        last.then_inc(s["q_turned"], 1)
                turns(pe, GROUPS, group)

                pe.wait_ge(s["qT_in"], 2 * GROUPS)
                pe.wait_ge(s["kmaxed"], NT)
                for e in range(2):
                    last = pe.transpose(psT[0][:, e, :], kmax[:, e * P:(e + 1) * P], T["ident"][:])
                last.then_inc(s["kflip"], 1)
                pe.wait_ge(s["ktopped"], 2)
                pe.wait_ge(s["ones_in"], 4)
                for e in range(2):
                    last = pe.matmul(psT[1][:, e, :], ones[:], kdiag[:, e, :], start=True, stop=True)
                last.then_inc(s["kspread"], 1)
                pe.wait_ge(s["kexped"], GROUPS)
                pe.wait_ge(s["kv_in"], NT)
                for e in range(2):
                    for t in range(NT):
                        r = P if t < NT - 1 else LAST
                        last = pe.matmul(psM[e][:, 0:VW], kall[0:r, t, e * P:(e + 1) * P], vall[0:r, t, e, :],
                                         start=(t == 0), stop=(t == NT - 1))
                    last.then_inc(s["kv_done"], 1)
                pe.wait_ge(s["kv_in2"], 2)
                for e in range(2):
                    for c in range(2):
                        last = pe.transpose(psT[0][:, 2 * e + c, :], kv[:, e, c * P:(c + 1) * P], T["ident"][:])
                last.then_inc(s["kvflip"], 1)
                pe.wait_ge(s["kvT_in"], 1)
                for e in range(2):
                    for c in range(2):
                        last = pe.matmul(psM[e][:], kvT[:, e, c, :], w_out[:, 2 * e + c, :], start=(c == 0), stop=(c == 1))
                    last.then_inc(s["fold_done"], 1)

            @block.scalar
            def _(act):
                act.wait_ge(s["ones_in"], 4)

                def group(g):
                    for n in range(GN):
                        act.wait_ge(s["turned"], g * GN + n + 1)
                        act.copy(xT[:, :, n * P:(n + 1) * P], psT[n % 2][:]).then_inc(s["xT_in"], 1)
                    for c in range(KC):
                        act.wait_ge(s["middled"], g * KC + c + 1)
                        act.activation(mid[:, c, :], psM[c % 2][:], ACT.Identity, bias=b_in[:, c:c + 1]
                                       ).then_inc(s["mid_in"], 1)
                    for n in range(GN):
                        act.wait_ge(s["projected"], g * GN + n + 1)
                        ps = psQ[n % 2]
                        if n == 0 and later(g):
                            act.wait_ge(s["q_turned"], g * 2)
                        act.copy(q[:, n, :].rearrange("p (c w) -> p c w", c=KC), ps[:, :, 0:W2]).then_inc(s["q_in"], 1)
                        act.copy(one(kall[:, bass.ds(g * GN + n, 1), :]).rearrange("p (c w) -> p c w", c=KC),
                                 ps[:, :, W2:2 * W2])
                        for e in range(2):
                            last = act.copy(vall[:, bass.ds(g * GN + n, 1), e, 0:4 * D].rearrange(
                                "p o (c w) -> p (o c) w", c=2), ps[:, 2 * e:2 * e + 2, 2 * W2:])
                        last.then_inc(s["kv_in"], 1)
                    act.wait_ge(s["shifted"], g + 1)
                    act.activation(q[:], q[:], ACT.Exp).then_inc(s["exped"], 1)
                turns(act, GROUPS, group)
                for t in range(GROUPS):
                    r = slice(t * GN, (t + 1) * GN)
                    act.wait_ge(s["kshifted"], t + 1)
                    act.activation(kall[:, r, :], kall[:, r, :], ACT.Exp).then_inc(s["kexped"], 1)

            @block.vector
            def _(vec):
                vec.wait_ge(s["ones_in"], 4)

                def k_top(g, n, rows):
                    km = kmax[0:rows, :].rearrange("p (c w) -> p c w", c=KC)
                    vec.wait_ge(s["kv_in"], g * GN + n + 1)
                    if later(g) or n:
                        vec.wait_ge(s["kmaxed"], g * GN + n)
                    vec.tensor_tensor(km, km, psQ[n % 2][0:rows, :, W2:2 * W2], ALU.max).then_inc(s["kmaxed"], 1)

                def group(g, rows_of_last=P):
                    c = Chain(vec, s["steps"], g * 3)
                    for n in range(GN):
                        k_top(g, n, P if n < GN - 1 else rows_of_last)
                    vec.wait_ge(s["q_in"], g * GN + GN)
                    by_head = q[:].rearrange("p n (h s) -> p (n h) s", s=SL)
                    c.then(vec.tensor_reduce(qsum[:], by_head, AX.X, ALU.max))
                    c.wait()
                    vec.tensor_tensor(by_head, by_head, qsum[:].unsqueeze(2).to_broadcast([P, GN * H, SL]),
                                      ALU.subtract).then_inc(s["shifted"], 1)
                    vec.wait_ge(s["exped"], g + 1)
                    c.then(vec.tensor_reduce(qsum[:], by_head, AX.X, ALU.add))
                    c.wait()
                    c.then(vec.reciprocal(qsum[:], qsum[:]))
                    c.wait()
                    vec.tensor_tensor(by_head, by_head, qsum[:].unsqueeze(2).to_broadcast([P, GN * H, SL]),
                                      ALU.mult).then_inc(s["normed"], 1)
                    for e in range(2):
                        vec.wait_ge(s["q_turned"], g * 2 + e + 1)
                        vec.tensor_scalar(qT[:, e, bass.ds(g * NODES, NODES)], psT[e][:].rearrange("p k n -> p (k n)"),
                                          1.0, None, ALU.mult).then_inc(s["qT_in"], 1)
                group(0)
                with vec.Fori(1, GROUPS - 1) as g:
                    group(g)
                group(GROUPS - 1, LAST)

                c = Chain(vec, s["fixed"])
                vec.wait_ge(s["kflip"], 1)
                c.then(vec.tensor_reduce(ktop[:], psT[0][:, 0:2, :], AX.X, ALU.max))
                c.wait()
                for e in range(2):
                    vec.tensor_scalar(kdiag[:, e, :], T["ident"][:], ktop[:, e:e + 1], None, ALU.mult
                                      ).then_inc(s["ktopped"], 1)
                vec.wait_ge(s["kspread"], 1)
                vec.wait_ge(s["kv_in"], NT)
                for t in range(GROUPS):
                    r = slice(t * GN, (t + 1) * GN)
                    vec.tensor_tensor(kall[:, r, :], kall[:, r, :], psT[1][:, 0:2, :].rearrange("p e w -> p (e w)")
                                      .unsqueeze(1).to_broadcast([P, GN, HS]), ALU.subtract).then_inc(s["kshifted"], 1)
                for e in range(2):
                    vec.wait_ge(s["kv_done"], e + 1)
                    c.then(vec.reciprocal(ksum[:, e:e + 1], psM[e][:, 4 * D:VW]))
                    c.wait()
                    for j in range(4):
                        r = slice(j * SL, (j + 1) * SL)
                        last = vec.tensor_scalar(kv[r, e, j * D:(j + 1) * D], psM[e][r, j * D:(j + 1) * D],
                                                 ksum[r, e:e + 1], None, ALU.mult)
                    last.then_inc(s["kv_in2"], 1)
                vec.wait_ge(s["kvflip"], 1)
                vec.tensor_copy(kvT[:].rearrange("p e c w -> p (e c w)"), psT[0][:].rearrange("p k n -> p (k n)")
                                ).then_inc(s["kvT_in"], 1)
                for e in range(2):
                    vec.wait_ge(s["fold_done"], e + 1)
                    c.then(vec.tensor_copy(folded[:, e, :], psM[e][:]))


def spread_slices(nc, a, T, qT, folded, gnn_dram, x3_dram, y3_dram):
    with ExitStack() as stack:
        m = Memory(nc, stack, "spread")
        x = m.sb("x", [P, NT, C])
        gnn = m.sb("gnn", [P, NT, C])
        bias = m.sb("bias", [P, C])
        psX = [m.ps(f"psX{i}", [P, C]) for i in range(4)]
        zeroed, landed, summed, mixed, mixed_in, biased, normed, stored = (
            m.sem(s) for s in ("zeroed", "landed", "summed", "mixed", "mixed_in", "biased", "normed", "stored"))
        ln = LayerNorm(nc, m, NT)
        with nc.Block() as block:
            @block.sync
            def _(sp):
                sp.dma_start(gnn[:], gnn_dram.rearrange("(t p) c -> p t c", p=P)).then_inc(landed, 16)
                sp.dma_start(bias[:], a["L0_mix_b_out"].partition_broadcast(P)).then_inc(landed, 16)
                sp.wait_ge(zeroed, 1)
                sp.dma_start(x[:, 0:NT - 1, :],
                             a["x"][0:(NT - 1) * P, :].rearrange("(t p) c -> p t c", p=P)).then_inc(landed, 16)
                sp.dma_start(x[0:LAST, NT - 1, :], a["x"][(NT - 1) * P:N, :]).then_inc(landed, 16)
                for t in range(NT):
                    sp.wait_ge(biased, t + 1)
                    sp.dma_start(x3_dram[t * P:(t + 1) * P, :], x[:, t, :]).then_inc(stored, 16)
                for t in range(NT):
                    sp.wait_ge(normed, t + 1)
                    sp.dma_start(y3_dram[t * P:(t + 1) * P, :], gnn[:, t, :]).then_inc(stored, 16)
                sp.wait_ge(stored, 32 * NT)

            @block.gpsimd
            def _(pool):
                pool.memset(x[:, NT - 1, :], 0.0).then_inc(zeroed, 1)
                ln.set_eps(pool)
                pool.wait_ge(landed, 64)
                for t in range(NT):
                    pool.tensor_tensor(x[:, t, :], x[:, t, :], gnn[:, t, :], ALU.add).then_inc(summed, 1)

            @block.tensor
            def _(pe):
                for t in range(NT):
                    if t >= 4:
                        pe.wait_ge(mixed_in, t - 3)
                    for e in range(2):
                        last = pe.matmul(psX[t % 4][:], qT[:, e, t * P:(t + 1) * P], folded[:, e, :], start=(e == 0),
                                         stop=(e == 1))
                    last.then_inc(mixed, 1)

            @block.vector
            def _(vec):
                for t in range(NT):
                    vec.wait_ge(mixed, t + 1)
                    vec.wait_ge(summed, t + 1)
                    vec.tensor_tensor(x[:, t, :], x[:, t, :], psX[t % 4][:], ALU.add).then_inc(mixed_in, 1)
                for t in range(NT):
                    vec.wait_ge(mixed_in, t + 1)
                    vec.tensor_tensor(x[:, t, :], x[:, t, :], bias[:], ALU.add).then_inc(biased, 1)
                vec.wait_ge(biased, NT)
                ln.stats(vec, lambda t: x[:, t, :])
                ln.scale(vec)
                for t in range(NT):
                    ln.apply(vec, t, gnn[:, t, :], x[:, t, :]).then_inc(normed, 1)

            @block.scalar
            def _(act):
                ln.root(act)


def quantise_weights(nc, a, T, W):
    with ExitStack() as stack:
        m = Memory(nc, stack, "quant")
        big = FK * C
        w = m.sb("w", [P, 2, big])
        mag = m.sb("mag", [P, big])
        n_groups = big // P
        scale = m.sb("scale", [P, n_groups])
        inv = m.sb("inv", [P, n_groups])
        psT = [m.ps(f"psT{i}", [P, 4, P]) for i in range(4)]
        landed = [m.sem(f"landed{i}") for i in range(3)]
        steps, ready, turned, taken, lows = (m.sem(s) for s in ("steps", "ready", "turned", "taken", "lows"))
        sources = [(a["L0_ffn_w_gate"].rearrange("(f p) c -> p f c", p=P), FK, KC, W["gateT"]),
                   (a["L0_ffn_w_up"].rearrange("(f p) c -> p f c", p=P), FK, KC, W["upT"]),
                   (a["L0_ffn_w_down"].rearrange("(k p) c -> p k c", p=P), KC, FK, W["downT"][:, 0])]
        batches = n_groups // 4
        with nc.Block() as block:
            @block.sync
            def _(sp):
                for i, (src, ro, co, _t) in enumerate(sources):
                    if i >= 2:
                        sp.wait_ge(turned, (i - 1) * batches)
                    sp.dma_start(w[:, i % 2, :].rearrange("p (r c) -> p r c", r=ro), src).then_inc(landed[i], 16)

            @block.vector
            def _(vec):
                c = Chain(vec, steps)
                for i in range(3):
                    wi = w[:, i % 2, :]
                    wg = wi.rearrange("p (g e) -> p g e", e=P)
                    mg = mag[:].rearrange("p (g e) -> p g e", e=P)

                    def over(x):
                        return x[:].unsqueeze(2).to_broadcast([P, n_groups, P])
                    vec.wait_ge(landed[i], 16)
                    c.then(vec.tensor_scalar(mag[:], wi, -1.0, None, ALU.mult))
                    c.wait()
                    c.then(vec.tensor_tensor(mag[:], mag[:], wi, ALU.max))
                    c.wait()
                    c.then(vec.tensor_reduce(scale[:], mg, AX.X, ALU.add))
                    c.wait()
                    c.then(vec.tensor_scalar(scale[:], scale[:], 1.0 / P, EPS, ALU.mult, ALU.add))
                    c.wait()
                    c.then(vec.reciprocal(inv[:], scale[:]))
                    c.wait()
                    c.then(vec.tensor_tensor(wg, wg, over(inv), ALU.mult))
                    c.wait()
                    c.then(vec.tensor_scalar(wi, wi, ROUND, ROUND, ALU.add, ALU.subtract))
                    c.wait()
                    ins = vec.tensor_scalar(wi, wi, 1.0, -1.0, ALU.min, ALU.max)
                    if i < 2:
                        ins.then_inc(ready, 1)
                        c.then(vec.tensor_copy(W["means"][:, i, :], scale[:]))
                    else:
                        c.then(ins)
                        c.wait()
                        vec.tensor_tensor(wg, wg, over(scale), ALU.mult).then_inc(ready, 1)
                flat = [W["downT"][:, part].rearrange("p c r -> p (c r)") for part in range(2)]
                for b in range(batches):
                    n = 2 * batches + b
                    at = slice(b * 4 * P, (b + 1) * 4 * P)
                    vec.wait_ge(taken, n + 1)
                    vec.tensor_tensor(flat[1][:, at], psT[n % 4][:].rearrange("p k e -> p (k e)"),
                                      flat[0][:, at].bitcast(F32), ALU.subtract).then_inc(lows, 1)

            @block.tensor
            def _(pe):
                for i, (_s, ro, co, _t) in enumerate(sources):
                    pe.wait_ge(ready, i + 1)
                    wv = w[:, i % 2, :].rearrange("p (r c e) -> p r c e", r=ro, e=P)
                    for b in range(batches):
                        n = i * batches + b
                        if n >= 4:
                            pe.wait_ge(taken, n - 3)
                        if n >= 2 * batches + 4:
                            pe.wait_ge(lows, n - 2 * batches - 3)
                        for j in range(4):
                            cc, rr = divmod(b * 4 + j, ro)
                            last = pe.transpose(psT[n % 4][:, j, :], wv[:, rr, cc, :], T["ident"][:])
                        last.then_inc(turned, 1)

            @block.scalar
            def _(act):
                for i, (_s, ro, co, t) in enumerate(sources):
                    flat = t[:].rearrange("p c r -> p (c r)")
                    for b in range(batches):
                        n = i * batches + b
                        act.wait_ge(turned, n + 1)
                        act.copy(flat[:, b * 4 * P:(b + 1) * 4 * P], psT[n % 4][:].rearrange("p k e -> p (k e)")
                                 ).then_inc(taken, 1)


def gated_ffn(nc, a, T, W, x3_dram, y3_dram, out):
    with ExitStack() as stack:
        m = Memory(nc, stack, "ffn")
        y = m.sb("y", [P, GN, C])
        res = m.sb("res", [P, GN, C])
        yT = m.sb("yT", [P, 2, KC, NODES], F32R)
        sums = m.sb("sums", [P, 2, 2, 2, NODES])
        silu = m.sb("silu", [P, 2, NODES])
        h = m.sb("h", [P, 2, NODES])
        hT = m.sb("hT", [P, 2, FK, NODES], F32R)
        psT = [m.ps(f"psT{i}", [P, KC, P]) for i in range(2)]
        psP = [m.ps(f"psP{i}", [P, NODES]) for i in range(KC)]
        psO = [m.ps(f"psO{i}", [P, C]) for i in range(2)]
        (y_in, res_in, turned, yT_high, yT_in, partial, scaled, added, summed, silued, multiplied, hT_high, low_vec,
         low_pool, out_done, done, stored) = (
            m.sem(s) for s in ("y_in", "res_in", "turned", "yT_high", "yT_in", "partial", "scaled", "added", "summed",
                               "silued", "multiplied", "hT_high", "low_vec", "low_pool", "out_done", "done", "stored"))
        ON_POOL = [f for f in range(FK) if f % 2 == 1]
        ON_VEC = [f for f in range(FK) if f % 2 == 0]

        def rows_of(dram, g):
            return dram[bass.ds(g * NODES, NODES), :].rearrange("(t p) c -> p t c", p=P)

        def before(g, f):
            return g * FK + (f - 1 if f else 0)

        with nc.Block() as block:
            @block.sync
            def _(sp):
                sp.dma_start(y[:], rows_of(y3_dram, 0)).then_inc(y_in, 16)

                def group(g, end):
                    if later(g):
                        sp.wait_ge(done, g * GN)
                        sp.dma_start(rows_of(out, g - 1), res[:]).then_inc(stored, 16)
                        sp.wait_ge(stored, g * 16)
                    sp.dma_start(res[:], rows_of(x3_dram, g)).then_inc(res_in, 16)
                    if not end:
                        sp.wait_ge(turned, g * GN + GN)
                        sp.dma_start(y[:], rows_of(y3_dram, g + 1)).then_inc(y_in, 16)
                turns_ahead(sp, GROUPS, group)
                sp.wait_ge(done, GROUPS * GN)
                r0 = (GROUPS - 1) * NODES
                sp.dma_start(out[r0:(NT - 1) * P, :].rearrange("(t p) c -> p t c", p=P), res[:, 0:GN - 1, :]
                             ).then_inc(stored, 16)
                sp.dma_start(out[(NT - 1) * P:N, :], res[0:LAST, GN - 1, :]).then_inc(stored, 16)
                sp.wait_ge(stored, 16 * (GROUPS + 1))

            @block.tensor
            def _(pe):
                def flip(g, n):
                    if n == 0:
                        pe.wait_ge(y_in, g * 16 + 16)
                    if later(g) or n >= 2:
                        pe.wait_ge(yT_in, g * GN + n - 1)
                    for k in range(KC):
                        last = pe.transpose(psT[n % 2][:, k, :], y[:, n, k * P:(k + 1) * P], T["ident"][:])
                    last.then_inc(turned, 1)

                for n in range(GN):
                    flip(0, n)

                def group(g, end):
                    pe.wait_ge(yT_in, g * GN + GN)
                    for f in range(FK):
                        for j, w in enumerate((W["gateT"], W["upT"])):
                            s = (g * FK + f) * 2 + j
                            for k in range(KC):
                                if later(g) or f or j:
                                    pe.wait_ge(scaled if k < 2 else added, 2 * s - 1 + k % 2)
                                for part in (1, 0):
                                    last = pe.matmul(psP[k][:], w[:, k, f * P:(f + 1) * P], yT[:, part, k, :],
                                                     start=(part == 1), stop=(part == 0))
                                last.then_inc(partial, 1)

                    def down(n):
                        if later(g) or n >= 2:
                            pe.wait_ge(done, g * GN + n - 1)
                        for f in range(FK):
                            last = product(pe, psO[n % 2][:], [hT[:, i, f, n * P:(n + 1) * P] for i in range(2)],
                                           [W["downT"][:, i, f, :] for i in range(2)], start=(f == 0),
                                           stop=(f == FK - 1))
                        last.then_inc(out_done, 1)

                    if not end:
                        flip(g + 1, 0)
                        flip(g + 1, 1)
                    pe.wait_ge(low_vec, (g + 1) * len(ON_VEC))
                    pe.wait_ge(low_pool, (g + 1) * len(ON_POOL))
                    for n in range(GN):
                        down(n)
                        if not end and n + 2 < GN:
                            flip(g + 1, n + 2)
                turns_ahead(pe, GROUPS, group)

            @block.scalar
            def _(act):
                def high(g, n):
                    act.wait_ge(turned, g * GN + n + 1)
                    act.copy(yT[:, 0, :, n * P:(n + 1) * P], psT[n % 2][:]).then_inc(yT_high, 1)

                for n in range(GN):
                    high(0, n)

                def scale(g, f, j):
                    if later(g) or f >= 2:
                        act.wait_ge(multiplied, before(g, f))
                    for k in range(2):
                        act.wait_ge(partial, ((g * FK + f) * 2 + j) * KC + k + 1)
                        act.activation(sums[:, f % 2, j, k, :], psP[k][:], ACT.Copy,
                                       scale=W["means"][:, j, f * KC + k:f * KC + k + 1]).then_inc(scaled, 1)

                def smooth(g, f):
                    act.wait_ge(summed, (g * FK + f) * 2 + 1)
                    act.activation(silu[:, f % 2, :], sums[:, f % 2, 0, 0, :], ACT.Silu).then_inc(silued, 1)

                def round_h(g, f):
                    act.wait_ge(multiplied, g * FK + f + 1)
                    act.copy(hT[:, 0, f, :], h[:, f % 2, :]).then_inc(hT_high, 1)

                def group(g, end):
                    for f in range(FK + 1):
                        if f < FK:
                            scale(g, f, 0)
                        if f:
                            smooth(g, f - 1)
                        if f < FK:
                            scale(g, f, 1)
                        if f:
                            round_h(g, f - 1)
                    if not end:
                        for n in range(GN):
                            high(g + 1, n)
                turns_ahead(act, GROUPS, group)

            @block.gpsimd
            def _(pool):
                def total(g, f, j):
                    pool.wait_ge(added, ((g * FK + f) * 2 + j) * 2 + 2)
                    pool.tensor_tensor(sums[:, f % 2, j, 0, :], sums[:, f % 2, j, 0, :], sums[:, f % 2, j, 1, :],
                                       ALU.add).then_inc(summed, 1)

                def group(g):
                    for f in range(FK + 1):
                        for j in range(2):
                            if f < FK:
                                total(g, f, j)
                        if f - 1 in ON_POOL:
                            pool.wait_ge(hT_high, g * FK + f)
                            pool.tensor_tensor(hT[:, 1, f - 1, :], h[:, (f - 1) % 2, :], hT[:, 0, f - 1, :].bitcast(F32),
                                               ALU.subtract).then_inc(low_pool, 1)
                turns(pool, GROUPS, group)

            @block.vector
            def _(vec):
                def low(g, n):
                    vec.wait_ge(yT_high, g * GN + n + 1)
                    vec.tensor_tensor(yT[:, 1, :, n * P:(n + 1) * P], psT[n % 2][:],
                                      yT[:, 0, :, n * P:(n + 1) * P].bitcast(F32), ALU.subtract).then_inc(yT_in, 1)

                for n in range(GN):
                    low(0, n)

                def add(g, f, j):
                    s = (g * FK + f) * 2 + j
                    for k in range(2, KC):
                        half = sums[:, f % 2, j, k - 2, :]
                        vec.wait_ge(partial, s * KC + k + 1)
                        vec.wait_ge(scaled, s * 2 + k - 1)
                        vec.scalar_tensor_tensor(out=half, in0=psP[k][:],
                                                 scalar=W["means"][:, j, f * KC + k:f * KC + k + 1],
                                                 in1=half, op0=ALU.mult, op1=ALU.add).then_inc(added, 1)

                def multiply(g, f):
                    vec.wait_ge(silued, g * FK + f + 1)
                    vec.wait_ge(summed, (g * FK + f) * 2 + 2)
                    if later(g) or f >= 2:
                        vec.wait_ge(hT_high, before(g, f))
                        user = f - 2 if f >= 2 else FK - 1 - f
                        if user in ON_POOL:
                            vec.wait_ge(low_pool, (g if f >= 2 else g - 1) * len(ON_POOL) + ON_POOL.index(user) + 1)
                        else:
                            vec.wait_ge(low_vec, (g if f >= 2 else g - 1) * len(ON_VEC) + ON_VEC.index(user) + 1)
                    vec.tensor_tensor(h[:, f % 2, :], silu[:, f % 2, :], sums[:, f % 2, 1, 0, :],
                                      ALU.mult).then_inc(multiplied, 1)

                def group(g, end):
                    for f in range(FK + 1):
                        if f < FK:
                            add(g, f, 0)
                        if f:
                            multiply(g, f - 1)
                        if f < FK:
                            add(g, f, 1)
                        if f - 1 in ON_VEC:
                            vec.wait_ge(hT_high, g * FK + f)
                            vec.tensor_tensor(hT[:, 1, f - 1, :], h[:, (f - 1) % 2, :], hT[:, 0, f - 1, :].bitcast(F32),
                                              ALU.subtract).then_inc(low_vec, 1)
                    if not end:
                        low(g + 1, 0)
                        low(g + 1, 1)
                    vec.wait_ge(res_in, g * 16 + 16)
                    for n in range(GN):
                        vec.wait_ge(out_done, g * GN + n + 1)
                        vec.tensor_tensor(res[:, n, :], psO[n % 2][:], res[:, n, :], ALU.add).then_inc(done, 1)
                        if not end and n + 2 < GN:
                            low(g + 1, n + 2)
                turns_ahead(vec, GROUPS, group)


def gps_layer(nc, a, out):
    with ExitStack() as whole:
        kept = Memory(nc, whole, "kept")
        T = {}
        xn, k, v, base, x1, y1, gnn, x3, y3 = (nc.dram_tensor(n, (NP, C), F32).ap() for n in (
            "xn_rows", "k_rows", "v_rows", "base_rows", "x1_rows", "y1_rows", "gnn_rows", "x3_rows", "y3_rows"))
        make_constants(nc, kept, T)
        normalise_input(nc, a, xn)
        with ExitStack() as edges:
            share_edges(nc, Memory(nc, edges, "edges"), T)
            ordered = [nc.dram_tensor(n, (ET * P, 1), I32).ap() for n in ("ordered_dst", "ordered_src")]
            order_edges(nc, a, T, ordered)
            index_edges(nc, a, T, ordered)
            for layer in range(LAYERS):
                with ExitStack() as stack:
                    m = Memory(nc, stack, f"layer{layer}")
                    scores = m.sb("scores", [P, SLOTS * H])
                    with ExitStack() as queries:
                        T["q_parts"] = Memory(nc, queries, f"layer{layer}").sb("q_parts", [P, 3, NT, C], BF16)
                        project_nodes(nc, a, T, layer, x1 if layer else xn, xn, k, v, base)
                        score_edges(nc, a, T, layer, k, scores)
                    weights = m.sb("weights", [P, SLOTS * H])
                    soften(nc, T, layer, scores, weights)
                    agg = m.sb("agg", [P, NT, AW])
                    aggregate(nc, a, T, layer, v, weights, agg)
                    combine(nc, a, T, layer, agg, base, y1 if layer == LAYERS - 1 else x1)
        node_mlp(nc, a, T, y1, xn, gnn)
        mix_slices(nc, a, T, xn, gnn, x3, y3)
        W = {"gateT": kept.sb("gateT", [P, KC, FFN], F32R), "upT": kept.sb("upT", [P, KC, FFN], F32R),
             "downT": kept.sb("downT", [P, 2, FK, C], F32R), "means": kept.sb("means", [P, 2, FK * KC])}
        quantise_weights(nc, a, T, W)
        gated_ffn(nc, a, T, W, x3, y3, out)


def kernel(**inputs):
    import numpy as np
    import concourse.bacc as bacc
    from concourse.bass_utils import run_bass_kernel_spmd

    nc = bacc.Bacc("TRN2", target_bir_lowering=False, num_devices=1)
    arrays, aps = {}, {}
    for name in inputs:
        if name in ("edge_type_10", "edge_weight"):
            continue
        arrays[name] = np.ascontiguousarray(inputs[name])
        aps[name] = nc.dram_tensor(name, arrays[name].shape, mybir.dt.from_np(arrays[name].dtype),
                                   kind="ExternalInput").ap()
    out = nc.dram_tensor("out", (N, C), F32, kind="ExternalOutput").ap()
    gps_layer(nc, aps, out)
    return run_bass_kernel_spmd(nc, [arrays], core_ids=[0]).results[0]["out"]
```

```python
from contextlib import ExitStack

import concourse.bass as bass
from concourse import mybir

P = 128
N = 2500
C = 512
KC = C // P
H = 8
D = C // H
E = 40000
LAYERS = 2
NT = -(-N // P)
NP = NT * P
LAST = N - (NT - 1) * P
ET = -(-E // P)
EK = -(-ET // P)
CH = 16
G = -(-(ET + NT - 1) // CH)
SLOTS = CH * G
RUN = G * P
U = 16
TURNS = SLOTS // U
GN = 4
GROUPS = NT // GN
NODES = GN * P
NEG = -1e30
EPS = 1e-5
F1 = 2 * C
FFN = 1408
FK = FFN // P
SL = 32
AW = C + H

F32 = mybir.dt.float32
BF16 = mybir.dt.bfloat16
F32R = mybir.dt.float32r
I32 = mybir.dt.int32
ALU = mybir.AluOpType
ACT = mybir.ActivationFunctionType
AX = mybir.AxisListType


class Memory:

    def __init__(self, nc, stack, prefix):
        self.nc, self.stack, self.prefix, self.sems = nc, stack, prefix, []
        stack.callback(self.clear)

    def clear(self):
        if self.sems:
            self.nc.clear_and_free_semaphores(self.sems)
            self.nc.all_engine_barrier()

    def sb(self, name, shape, dt=F32):
        return self.stack.enter_context(self.nc.sbuf_tensor(f"{self.prefix}_{name}", shape, dt))

    def ps(self, name, shape, dt=F32):
        return self.stack.enter_context(self.nc.psum_tensor(f"{self.prefix}_{name}", shape, dt))

    def sem(self, name):
        self.sems.append(self.nc.alloc_semaphore(f"{self.prefix}_{name}"))
        return self.sems[-1]


class Chain:

    def __init__(self, engine, sem, base=0):
        self.engine, self.sem, self.base, self.n = engine, sem, base, 0

    def then(self, ins):
        ins.then_inc(self.sem, 1)
        self.n += 1

    def wait(self):
        self.engine.wait_ge(self.sem, self.base + self.n)


def one(ap):
    return ap.rearrange("p o c -> p (o c)")


def product(pe, out, left, right, start, stop):
    for n, (i, j) in enumerate(((0, 1), (1, 0), (0, 0))):
        last = pe.matmul(out, left[i], right[j], start=start and n == 0, stop=stop and n == 2)
    return last


def turns(engine, n, body):
    body(0)
    with engine.Fori(1, n) as t:
        body(t)


def turns_ahead(engine, n, body):
    body(0, False)
    with engine.Fori(1, n - 1) as t:
        body(t, False)
    body(n - 1, True)


def later(t):
    return not isinstance(t, int) or t > 0


def make_constants(nc, mem, T):
    T["ident"] = mem.sb("ident", [P, P])
    T["identb"] = mem.sb("identb", [P, P], BF16)
    T["lane"] = mem.sb("lane", [P, P])
    T["laneb"] = mem.sb("laneb", [P, P], BF16)
    T["head_of"] = mem.sb("head_of", [P, H])
    T["of_head"] = mem.sb("of_head", [H, P])
    T["chunk_of"] = mem.sb("chunk_of", [P, CH])
    ident, identb, lane, laneb = T["ident"], T["identb"], T["lane"], T["laneb"]
    with ExitStack() as stack:
        m = Memory(nc, stack, "const")
        flip = m.ps("flip", [H, P])
        zeroed, built, masks, flipped, done = (m.sem(x) for x in ("zeroed", "built", "masks", "flipped", "done"))
        with nc.Block() as block:
            @block.gpsimd
            def _(pool):
                pool.memset(ident[:], 0.0).then_inc(zeroed, 1)
                pool.iota(lane[:], [[1, P]], base=0, channel_multiplier=0,
                          allow_small_or_imprecise_dtypes=True).then_inc(built, 1)
                pool.wait_ge(zeroed, 1)
                pool.affine_select(out=ident[:], in_=ident[:], compare_op=ALU.not_equal, fill=1.0, base=0,
                                   pattern=[[-1, P]], channel_multiplier=1).then_inc(built, 1)

            @block.vector
            def _(vec):
                vec.wait_ge(built, 2)
                vec.tensor_copy(identb[:], ident[:]).then_inc(done, 1)
                vec.tensor_copy(laneb[:], lane[:]).then_inc(done, 1)
                vec.tensor_reduce(T["head_of"][:], ident[:].rearrange("p (c h) -> p h c", h=H), AX.X,
                                  ALU.add).then_inc(masks, 1)
                vec.tensor_reduce(T["chunk_of"][:], ident[:].rearrange("p (c h) -> p c h", h=H), AX.X,
                                  ALU.add).then_inc(masks, 1)
                vec.wait_ge(flipped, 1)
                vec.tensor_copy(T["of_head"][:], flip[:]).then_inc(done, 1)

            @block.tensor
            def _(pe):
                pe.wait_ge(masks, 2)
                pe.transpose(flip[:], T["head_of"][:], ident[:]).then_inc(flipped, 1)


def share_edges(nc, mem, T):
    T["full_at"] = mem.sb("full_at", [P, NT], I32)
    T["tile_of"] = mem.sb("tile_of", [P, SLOTS], I32)
    T["local"] = mem.sb("local", [P, SLOTS + U // 2])
    T["disorder"] = mem.sb("disorder", [P, 1], I32)
    T["src"] = mem.sb("src", [P, SLOTS], I32)
    T["same"] = mem.sb("same", [P, RUN + 1], BF16)
    T["first"] = mem.sb("first", [P, RUN], BF16)
    T["last"] = mem.sb("last", [P, RUN], BF16)
    T["linked"] = mem.sb("linked", [H, 2 * CH, 2 * CH])


def order_edges(nc, a, T, ordered):
    with ExitStack() as stack:
        m = Memory(nc, stack, "disorder")
        R, W = 125, E // 125
        here = m.sb("here", [R, W], I32)
        after = m.sb("after", [R, W], I32)
        down = m.sb("down", [R, W])
        count = m.sb("count", [P, 1])
        ones = m.sb("ones", [P, P])
        total = m.ps("total", [P, 1])
        landed, filled, steps, counted, summed = (m.sem(s) for s in ("landed", "filled", "steps", "counted", "summed"))
        with nc.Block() as block:
            @block.gpsimd
            def _(pool):
                pool.memset(ones[:], 1.0).then_inc(filled, 1)
                pool.memset(count[:], 0.0).then_inc(filled, 1)

            @block.sync
            def _(sp):
                sp.dma_start(here[:], a["dst"].rearrange("(r w) -> r w", w=W)).then_inc(landed, 16)
                sp.dma_start(after[0:R - 1, :], a["dst"][1:E - W + 1].rearrange("(r w) -> r w", w=W)
                             ).then_inc(landed, 16)
                sp.dma_start(after[R - 1:R, 0:W - 1], a["dst"][E - W + 1:E].rearrange("(r w) -> r w", r=1)
                             ).then_inc(landed, 16)
                sp.dma_start(after[R - 1:R, W - 1:W], a["dst"][E - 1:E].rearrange("(r w) -> r w", r=1)
                             ).then_inc(landed, 16)

            @block.vector
            def _(vec):
                vec.wait_ge(landed, 64)
                vec.tensor_tensor(down[:], here[:], after[:], ALU.is_gt).then_inc(steps, 1)
                vec.wait_ge(filled, 2)
                vec.wait_ge(steps, 1)
                vec.tensor_reduce(count[0:R, :], down[:], AX.X, ALU.add).then_inc(counted, 1)
                vec.wait_ge(summed, 1)
                vec.tensor_copy(T["disorder"][:], total[:]).then_inc(steps, 1)

            @block.tensor
            def _(pe):
                pe.wait_ge(filled, 2)
                pe.wait_ge(counted, 1)
                pe.matmul(total[:], ones[:], count[:], start=True, stop=True).then_inc(summed, 1)

    with ExitStack() as stack:
        m = Memory(nc, stack, "order")
        EP = ET * P
        CHUNK = E // 10
        wide = m.sb("wide", [P, CHUNK], I32)
        every = m.sb("every", [P, EP], mybir.dt.int16)
        less = m.sb("less", [P, EP], mybir.dt.uint8)
        tiles = m.sb("tiles", [P, 2, ET], I32)
        key = m.sb("key", [P, ET])
        before = m.sb("before", [P, P])
        ties = m.sb("ties", [P, P])
        place = m.sb("place", [P, 2])
        index = m.sb("index", [P, 1], I32)
        load = m.sb("load", [P, 2], I32)
        FAR = 2 * NP
        filled, chunk_in, tiles_in, widened, steps, placed, loads, going, sent, keyed, lower = (
            m.sem(s) for s in ("filled", "chunk_in", "tiles_in", "widened", "steps", "placed", "loads", "going",
                               "sent", "keyed", "lower"))

        def disordered(engine):
            return engine.value_load(T["disorder"][0:1, 0:1], min_val=0, max_val=E) > 0

        with nc.Block() as block:
            @block.gpsimd
            def _(pool):
                with pool.If(disordered(pool)):
                    pool.memset(before[:], 1.0).then_inc(lower, 1)
                    pool.memset(tiles[:, 0, ET - 1:ET], FAR).then_inc(filled, 1)
                    pool.memset(tiles[:, 1, ET - 1:ET], 0).then_inc(filled, 1)
                    pool.wait_ge(lower, 1)
                    pool.affine_select(out=before[:], in_=before[:], compare_op=ALU.is_gt, fill=0.0, base=0,
                                       pattern=[[-1, P]], channel_multiplier=1).then_inc(filled, 1)

                    def turn(t):
                        pool.wait_ge(placed, t + 1)
                        pool.sem_inc(going, 1)
                        for k in range(2):
                            pool.indirect_dma_start(ordered[k], bass.IndirectOffsetOnAxis(ap=index[:, 0:1], axis=0),
                                                    load[:, k:k + 1], None).then_inc(sent, 16)
                    turns(pool, ET, turn)
                    pool.wait_ge(sent, 32 * ET)

            @block.sync
            def _(sp):
                with sp.If(disordered(sp)):
                    sp.wait_ge(filled, 3)
                    for k, name in enumerate(("dst", "src")):
                        sp.dma_start(tiles[:, k, 0:ET - 1], a[name][0:(ET - 1) * P].rearrange("(t p) -> p t", p=P),
                                     allow_slow_non_contiguous=True).then_inc(tiles_in, 16)
                        sp.dma_start(tiles[0:E % P, k, ET - 1:ET],
                                     a[name][(ET - 1) * P:E].rearrange("(p o) -> p o", o=1)).then_inc(tiles_in, 16)
                    for n in range(E // CHUNK):
                        if n:
                            sp.wait_ge(widened, n)
                        sp.dma_start(wide[:], a["dst"][n * CHUNK:(n + 1) * CHUNK].partition_broadcast(P)
                                     ).then_inc(chunk_in, 16)

            @block.vector
            def _(vec):
                with vec.If(disordered(vec)):
                    for n in range(E // CHUNK):
                        vec.wait_ge(chunk_in, 16 * (n + 1))
                        vec.tensor_scalar(every[:, n * CHUNK:(n + 1) * CHUNK], wide[:], 2.0, None, ALU.mult
                                          ).then_inc(widened, 1)
                    vec.memset(every[:, E:EP], 2 * FAR).then_inc(widened, 1)
                    vec.wait_ge(tiles_in, 64)
                    vec.tensor_scalar(key[:], tiles[:, 0, :], 2.0, None, ALU.mult).then_inc(keyed, 1)
                    vec.wait_ge(keyed, 1)
                    vec.wait_ge(filled, 3)
                    vec.wait_ge(widened, E // CHUNK + 1)

                    def turn(t):
                        PER = 7
                        c = Chain(vec, steps, t * PER)
                        mine = every[:, bass.ds(t * P, P)]
                        c.then(vec.tensor_scalar(less[:], every[:], key[:, bass.ds(t, 1)], 0.0, ALU.is_lt, ALU.add,
                                                 accum_out=place[:, 0:1]))
                        c.then(vec.tensor_scalar(ties[:], mine, key[:, bass.ds(t, 1)], None, ALU.is_equal))
                        c.wait()
                        c.then(vec.tensor_tensor(ties[:], ties[:], before[:], ALU.mult))
                        c.then(vec.tensor_scalar(mine, mine, -1.0, None, ALU.add))
                        c.wait()
                        c.then(vec.tensor_reduce(place[:, 1:2], ties[:], AX.X, ALU.add))
                        c.wait()
                        if later(t):
                            vec.wait_ge(sent, t * 32)
                        c.then(vec.tensor_scalar(load[:], tiles[:, :, bass.ds(t, 1)].rearrange("p k o -> p (k o)"), 0.0,
                                                 None, ALU.add))
                        c.then(vec.tensor_tensor(index[:], place[:, 0:1], place[:, 1:2], ALU.add))
                        c.wait()
                        vec.sem_inc(placed, 1)
                    turns(vec, ET, turn)


def index_edges(nc, a, T, ordered, xn_dram):
    with ExitStack() as stack:
        m = Memory(nc, stack, "index")
        raw = m.sb("raw", [P, 2, EK, P], I32)
        rows = m.sb("rows", [P, 2, EK, P])
        low = m.sb("low", [P, NT])
        junk = m.sb("junk", [P, EK * P])
        ones = m.sb("ones", [P, P])
        bound = m.sb("bound", [P, NT + 1])
        up = m.sb("up", [P, NT])
        ints = m.sb("ints", [P, 2, NT], I32)
        shifted = m.sb("shifted", [P, 2, NT], I32)
        flo = m.sb("flo", [P, NT])
        cnt = m.sb("cnt", [P, NT])
        some = m.sb("some", [P, NT])
        cum = m.sb("cum", [P, NT + 1])
        shift = m.sb("shift", [P, NT])
        dshift = m.sb("dshift", [P, NT])
        slot = m.sb("slot", [P, SLOTS])
        part = m.sb("part", [P, 1])
        tile_of = m.sb("tile_of", [P, SLOTS])
        etile = m.sb("etile", [P, SLOTS])
        diag = m.sb("diag", [NT, 2, NT])
        begins = m.sb("begins", [NT, 2])
        begun = m.sb("begun", [NT, SLOTS])
        step_up = m.sb("step_up", [NT, P])
        step = m.sb("step", [P, SLOTS])
        pick = m.sb("pick", [P, EK, SLOTS])
        dst = m.sb("dst", [P, SLOTS])
        okl = m.sb("okl", [P, SLOTS])
        okh = m.sb("okh", [P, SLOTS])
        spread = m.sb("spread", [P, RUN])
        seg = m.sb("seg", [P, RUN])
        diff = m.sb("diff", [P, RUN])
        ends = m.sb("ends", [P, 2, CH])
        endv = m.sb("endv", [H, 2 * CH])
        neq = m.sb("neq", [H, 2 * CH, 2 * CH])
        psb = m.ps("psb", [P, NT])
        psd = m.ps("psd", [P, SLOTS])
        pss = m.ps("pss", [P, SLOTS])
        pse = m.ps("pse", [H, 2 * CH])
        pst = [m.ps(f"pst{i}", [P, 4 * P]) for i in range(2)]
        landed, filled, built, step_done, counted, summed, picked, placed, spread_done, turned, ends_done, ends_sum \
            = (m.sem(x) for x in ("landed", "filled", "built", "steps", "counted", "summed", "picked", "placed",
                                  "spread", "turned", "ends", "ends_sum"))
        copied, begun_done, stepped = m.sem("copied"), m.sem("begun"), m.sem("stepped")
        full = E // P - (EK - 1) * P
        rest = E % P
        flip_groups = [(g, min(4, G - g)) for g in range(0, G, 4)]
        x = m.sb("x", [P, NT, C])
        ln = LayerNorm(nc, m, GN)
        x_in = [m.sem(f"x_in{g}") for g in range(GROUPS)]
        padded, normed, stored = (m.sem(n) for n in ("padded", "normed", "stored"))
        with nc.Block() as block:
            @block.gpsimd
            def _(pool):
                ln.set_eps(pool)
                pool.memset(x[:, NT - 1, :], 0.0).then_inc(padded, 1)
                pool.memset(raw[:, 0, :, :], -1).then_inc(filled, 1)
                pool.memset(raw[:, 1, :, :], 0).then_inc(filled, 1)
                pool.memset(ones[:], 1.0).then_inc(built, 1)
                pool.iota(slot[:], [[1, SLOTS]], base=0, channel_multiplier=0,
                          allow_small_or_imprecise_dtypes=True).then_inc(built, 1)
                pool.iota(part[:], [[0, 1]], base=0, channel_multiplier=1,
                          allow_small_or_imprecise_dtypes=True).then_inc(built, 1)

            @block.sync
            def _(sp):
                sp.wait_ge(filled, 2)
                whole = (EK - 1) * P * P

                def load(k, edges):
                    sp.dma_start(raw[:, k, 0:EK - 1, :],
                                 edges[0:whole].rearrange("(k p e) -> p k e", p=P, e=P)).then_inc(landed, 16)
                    sp.dma_start(raw[0:full, k, EK - 1, :],
                                 edges[whole:whole + full * P].rearrange("(p e) -> p e", e=P)).then_inc(landed, 16)
                    sp.dma_start(raw[full:full + 1, k, EK - 1, 0:rest],
                                 edges[E - rest:E].rearrange("(p e) -> p e", p=1)).then_inc(landed, 16)

                disorder = sp.value_load(T["disorder"][0:1, 0:1], min_val=0, max_val=E)
                with sp.If(disorder > 0):
                    for k in range(2):
                        load(k, ordered[k].rearrange("e o -> (e o)"))
                with sp.Else():
                    for k, name in enumerate(("dst", "src")):
                        load(k, a[name])

                def rows_of(dram, g, n):
                    return dram[g * NODES:g * NODES + n * P, :].rearrange("(t p) c -> p t c", p=P)

                for g in range(GROUPS):
                    n = GN if g < GROUPS - 1 else GN - 1
                    sp.dma_start(x[:, g * GN:g * GN + n, :], rows_of(a["x"], g, n)).then_inc(x_in[g], 16)
                sp.wait_ge(padded, 1)
                sp.dma_start(x[0:LAST, NT - 1, :], a["x"][(NT - 1) * P:N, :]).then_inc(x_in[GROUPS - 1], 16)
                for g in range(GROUPS):
                    sp.wait_ge(normed, (g + 1) * GN)
                    sp.dma_start(rows_of(xn_dram, g, GN), x[:, g * GN:(g + 1) * GN, :]).then_inc(stored, 16)
                sp.wait_ge(stored, 16 * GROUPS)

            @block.scalar
            def _(act):
                for g in range(GROUPS):
                    ln.root(act, g)

            @block.vector
            def _(vec):
                c = Chain(vec, step_done)

                def normalise(g):
                    vec.wait_ge(x_in[g], 16 if g < GROUPS - 1 else 32)
                    ln.stats(vec, lambda n: x[:, g * GN + n, :], g)
                    ln.scale(vec, g)
                    for n in range(GN):
                        at = x[:, g * GN + n, :]
                        ln.apply(vec, n, at, at).then_inc(normed, 1)

                vec.wait_ge(landed, 96)
                c.then(vec.tensor_scalar(rows[:, 0], raw[:, 0], 1.0, None, ALU.add))
                c.then(vec.tensor_copy(rows[:, 1], raw[:, 1]))
                c.wait()
                for d in range(NT):
                    c.then(vec.tensor_scalar(junk[:], rows[:, 0].rearrange("p k e -> p (k e)"),
                                             float(P * (d + 1)), 0.0, ALU.is_le, ALU.add,
                                             accum_out=low[:, d:d + 1]))
                    c.wait()
                vec.nop().then_inc(counted, 1)
                normalise(0)
                vec.wait_ge(summed, 1)
                c.then(vec.memset(bound[:, 0:1], 0.0))
                c.then(vec.tensor_scalar(bound[:, 1:NT + 1], psb[:], -float(EK * P * P - E), None, ALU.add))
                c.wait()
                c.then(vec.tensor_scalar(up[:], bound[:, 1:NT + 1], float(P - 1), None, ALU.add))
                c.then(vec.tensor_copy(ints[:, 0, :], bound[:, 0:NT]))
                c.then(vec.tensor_tensor(some[:], bound[:, 1:NT + 1], bound[:, 0:NT], ALU.is_gt))
                c.wait()
                c.then(vec.tensor_copy(ints[:, 1, :], up[:]))
                c.wait()
                c.then(vec.tensor_scalar(shifted[:], ints[:], 7, None, ALU.logical_shift_right))
                c.wait()
                c.then(vec.tensor_copy(flo[:], shifted[:, 0, :]))
                c.then(vec.tensor_tensor(cnt[:], shifted[:, 1, :], shifted[:, 0, :], ALU.subtract))
                c.wait()
                c.then(vec.tensor_tensor(cnt[:], cnt[:], some[:], ALU.mult))
                c.then(vec.memset(cum[:, 0:1], 0.0))
                c.wait()
                c.then(vec.tensor_tensor_scan(cum[:, 1:NT + 1], ones[:, 0:NT], cnt[:], 0.0, ALU.mult, ALU.add))
                c.wait()
                c.then(vec.tensor_tensor(shift[:], flo[:], cum[:, 0:NT], ALU.subtract))
                vec.wait_ge(built, 3)
                c.then(vec.memset(dshift[:, 0:1], 0.0))
                c.wait()
                c.then(vec.tensor_tensor(dshift[:, 1:NT], shift[:, 1:NT], shift[:, 0:NT - 1], ALU.subtract))
                c.wait()
                ident = T["ident"][0:NT, 0:NT]
                c.then(vec.tensor_tensor(diag[:, 0, :], cum[0:NT, 0:NT], ident, ALU.mult))
                c.then(vec.tensor_tensor(diag[:, 1, :], dshift[0:NT, :], ident, ALU.mult))
                c.wait()
                c.then(vec.tensor_reduce(begins[:], diag[:], AX.X, ALU.add))
                c.wait()
                c.then(vec.tensor_scalar(begun[:], slot[0:NT, :], begins[:, 0:1], None, ALU.is_ge))
                c.then(vec.tensor_scalar(step_up[:], ones[0:NT, :], begins[:, 1:2], None, ALU.mult))
                c.wait()
                vec.nop().then_inc(begun_done, 1)
                vec.wait_ge(stepped, 2)
                c.then(vec.tensor_scalar(tile_of[:], psd[:], -1.0, None, ALU.add))
                c.then(vec.tensor_tensor(etile[:], slot[:], pss[:], ALU.add))
                c.wait()
                c.then(vec.tensor_copy(T["tile_of"][:], tile_of[:]))
                c.then(vec.tensor_scalar(up[:], cum[:, 1:NT + 1], 1.0, None, ALU.add))
                c.wait()
                c.then(vec.tensor_copy(T["full_at"][:], up[:]))
                for k in range(EK):
                    c.then(vec.tensor_scalar(pick[:, k, :], etile[:], -float(P * k), part[:, 0:1], ALU.add,
                                             ALU.is_equal))
                c.wait()
                vec.nop().then_inc(picked, 1)
                normalise(1)
                normalise(2)
                vec.wait_ge(placed, 2)
                c.then(vec.memset(T["local"][:, SLOTS:], -1.0))
                c.then(vec.tensor_copy(T["src"][:], pss[:]))
                c.then(vec.tensor_scalar(dst[:], psd[:], -1.0, None, ALU.add))
                c.then(vec.tensor_scalar(step[:], tile_of[:], -float(P), None, ALU.mult))
                c.wait()
                c.then(vec.tensor_tensor(T["local"][:, 0:SLOTS], dst[:], step[:], ALU.add))
                c.wait()
                c.then(vec.tensor_scalar(okl[:], T["local"][:, 0:SLOTS], 0.0, None, ALU.is_ge))
                c.then(vec.tensor_scalar(okh[:], T["local"][:, 0:SLOTS], float(P), None, ALU.is_lt))
                c.then(vec.tensor_scalar(dst[:], dst[:], 1.0, None, ALU.add))
                c.wait()
                c.then(vec.tensor_tensor(okl[:], okl[:], okh[:], ALU.mult))
                c.wait()
                c.then(vec.tensor_tensor(dst[:], dst[:], okl[:], ALU.mult))
                c.wait()
                for cc in range(CH):
                    c.then(vec.tensor_copy(
                        spread[:].rearrange("p (g c h) -> p g c h", c=CH, h=H)[:, :, cc, :],
                        dst[:, cc * G:(cc + 1) * G].rearrange("p (g o) -> p g o", o=1).to_broadcast([P, G, H])))
                c.wait()
                vec.nop().then_inc(spread_done, 1)
                normalise(3)
                for n, (g, k) in enumerate(flip_groups):
                    vec.wait_ge(turned, n + 1)
                    vec.tensor_copy(seg[:, g * P:(g + k) * P], pst[n % 2][:, 0:k * P]).then_inc(copied, 1)
                vec.wait_ge(copied, len(flip_groups))
                same, first, last = T["same"], T["first"], T["last"]
                c.then(vec.memset(same[:, 0:1], NEG))
                c.then(vec.memset(same[:, RUN:RUN + 1], NEG))
                c.then(vec.tensor_tensor(diff[:, 1:RUN], seg[:, 1:RUN], seg[:, 0:RUN - 1], ALU.not_equal))
                c.then(vec.tensor_scalar(first[:], seg[:], seg[:, 0:1], NEG, ALU.not_equal, ALU.mult))
                c.then(vec.tensor_scalar(last[:], seg[:], seg[:, RUN - 1:RUN], NEG, ALU.not_equal, ALU.mult))
                c.then(vec.tensor_scalar(ends[:, 0, :], T["chunk_of"][:], seg[:, 0:1], None, ALU.mult))
                c.then(vec.tensor_scalar(ends[:, 1, :], T["chunk_of"][:], seg[:, RUN - 1:RUN], None, ALU.mult))
                c.wait()
                vec.nop().then_inc(ends_done, 1)
                normalise(4)
                c.then(vec.tensor_scalar(same[:, 1:RUN], diff[:, 1:RUN], NEG, None, ALU.mult))
                vec.wait_ge(ends_sum, 1)
                c.then(vec.tensor_copy(endv[:], pse[:]))
                c.wait()
                c.then(vec.tensor_tensor(neq[:], endv[:].unsqueeze(2).to_broadcast([H, 2 * CH, 2 * CH]),
                                         endv[:].unsqueeze(1).to_broadcast([H, 2 * CH, 2 * CH]), ALU.not_equal))
                c.wait()
                c.then(vec.tensor_scalar(T["linked"][:], neq[:], NEG, None, ALU.mult))
                c.wait()

            @block.tensor
            def _(pe):
                pe.wait_ge(built, 3)
                pe.wait_ge(counted, 1)
                pe.matmul(psb[:], ones[:], low[:], start=True, stop=True).then_inc(summed, 1)
                pe.wait_ge(begun_done, 1)
                pe.matmul(psd[:], ones[0:NT, :], begun[:], start=True, stop=True).then_inc(stepped, 1)
                pe.matmul(pss[:], step_up[:], begun[:], start=True, stop=True).then_inc(stepped, 1)
                pe.wait_ge(picked, 1)
                for k, out in ((0, psd), (1, pss)):
                    for b in range(EK):
                        last = pe.matmul(out[:], rows[:, k, b, :], pick[:, b, :], start=(b == 0), stop=(b == EK - 1))
                    last.then_inc(placed, 1)
                pe.wait_ge(spread_done, 1)
                for n, (g, k) in enumerate(flip_groups):
                    if n >= 2:
                        pe.wait_ge(copied, n - 1)
                    for j in range(k):
                        last = pe.transpose(pst[n % 2][:, j * P:(j + 1) * P], spread[:, (g + j) * P:(g + j + 1) * P],
                                            T["ident"][:])
                    last.then_inc(turned, 1)
                pe.wait_ge(ends_done, 1)
                pe.matmul(pse[:], T["head_of"][:], ends[:].rearrange("p e c -> p (e c)"), start=True,
                          stop=True).then_inc(ends_sum, 1)


def project_nodes(nc, a, T, layer, x_dram, enc_dram, k_dram, v_dram, base_dram):
    with ExitStack() as stack:
        m = Memory(nc, stack, f"proj{layer}")
        names = ("s", "k", "v", "q")
        RAW = 4
        S_, K_, V_, Q_ = range(4)
        raw = m.sb("raw", [P, RAW, C])
        w = m.sb("w", [P, 2, 4 * KC, C], F32R)
        bias = m.sb("bias", [P, 4, C])
        x = m.sb("x", [P, 2, C])
        enc = m.sb("enc", [P, 2, C])
        xT = m.sb("xT", [P, 2, 2, KC, P], F32R)
        out = m.sb("out", [P, 2, 3, C])
        psT = [m.ps(f"psT{i}", [P, KC * P]) for i in range(2)]
        psP = [m.ps(f"psP{i}", [P, C]) for i in range(4)]
        w_in = [m.sem(f"w_in{i}") for i in range(RAW)]
        bias_in = m.sem("bias_in")
        w_highs, w_lows, xT_high = (m.sem(s) for s in ("w_highs", "w_lows", "xT_high"))
        x_in = [m.sem(f"x_in{b}") for b in range(2)]
        enc_in = [m.sem(f"enc_in{b}") for b in range(2)]
        kv_out = [m.sem(f"kv_out{b}") for b in range(2)]
        base_out = [m.sem(f"base_out{b}") for b in range(2)]
        turned, xT_ready, projected, ready, split, biased = (
            m.sem(s) for s in ("turned", "xT_ready", "projected", "ready", "split", "biased"))
        qp = T["q_parts"]
        T2 = NT // 2
        with nc.Block() as block:
            @block.sync
            def _(sp):
                for b in range(2):
                    sp.dma_start(x[:, b, :], x_dram[b * P:(b + 1) * P, :]).then_inc(x_in[b], 16)
                for j, n in enumerate(names):
                    for k in range(KC):
                        i = j * KC + k
                        if i >= RAW:
                            sp.wait_ge(w_lows, i + 1 - RAW)
                        sp.dma_start(raw[:, i % RAW, :], a[f"L0_gnn_W{n}"][layer, k * P:(k + 1) * P, :]
                                     ).then_inc(w_in[i % RAW], 16)
                    sp.dma_start(bias[:, j], a[f"L0_gnn_b{n}"][layer, :].partition_broadcast(P)).then_inc(bias_in, 16)

                def pair(t, end):
                    for b in range(2):
                        if not end:
                            sp.wait_ge(turned, t * 2 + b + 1)
                            sp.dma_start(x[:, b, :], x_dram[bass.ds((t * 2 + 2 + b) * P, P), :]).then_inc(x_in[b], 16)
                    for b in range(2):
                        if later(t):
                            sp.wait_ge(base_out[b], t * 16)
                        sp.dma_start(enc[:, b, :], enc_dram[bass.ds((t * 2 + b) * P, P), :]).then_inc(enc_in[b], 16)
                    for b in range(2):
                        sp.wait_ge(ready, t * 8 + b * 4 + S_ + 1)
                        sp.dma_start(base_dram[bass.ds((t * 2 + b) * P, P), :], enc[:, b, :]).then_inc(base_out[b], 16)
                turns_ahead(sp, T2, pair)
                for b in range(2):
                    sp.wait_ge(base_out[b], 16 * T2)

            @block.tensor
            def _(pe):
                def flip(t, b):
                    pe.wait_ge(x_in[b], t * 16 + 16)
                    for k in range(KC):
                        last = pe.transpose(psT[b][:, k * P:(k + 1) * P], x[:, b, k * P:(k + 1) * P], T["ident"][:])
                    last.then_inc(turned, 1)

                flip(0, 0)

                def pair(t, end):
                    for b in range(2):
                        if not (end and b):
                            flip(t + b, 1 - b)
                        pe.wait_ge(xT_ready, t * 2 + b + 1)
                        for j in range(4):
                            if later(t) or b:
                                pe.wait_ge(ready, t * 8 + b * 4 + j - 3)
                            else:
                                pe.wait_ge(w_lows, (j + 1) * KC)
                            for k in range(KC):
                                last = product(pe, psP[j][:], [xT[:, b, i, k, :] for i in range(2)],
                                               [w[:, i, j * KC + k, :] for i in range(2)],
                                               start=(k == 0), stop=(k == KC - 1))
                            last.then_inc(projected, 1)
                turns_ahead(pe, T2, pair)

            @block.scalar
            def _(act):
                def high(t, b):
                    act.wait_ge(turned, t * 2 + b + 1)
                    act.copy(xT[:, b, 0].rearrange("p k n -> p (k n)"), psT[b][:]).then_inc(xT_high, 1)

                for i in range(4 * KC):
                    act.wait_ge(w_in[i % RAW], i // RAW * 16 + 16)
                    act.copy(w[:, 0, i, :], raw[:, i % RAW, :]).then_inc(w_highs, 1)
                    if i == KC - 1:
                        high(0, 0)

                def pair(t, end):
                    for b in range(2):
                        if not (end and b):
                            high(t + b, 1 - b)
                        for j, dram in ((K_, k_dram), (V_, v_dram)):
                            act.wait_ge(ready, t * 8 + b * 4 + j + 1)
                            act.dma_start(dram[bass.ds((t * 2 + b) * P, P), :], out[:, b, j - 1, :]).then_inc(kv_out[b], 16)
                turns_ahead(act, T2, pair)
                for b in range(2):
                    act.wait_ge(kv_out[b], 32 * T2)

            @block.vector
            def _(vec):
                def low(t, b):
                    vec.wait_ge(xT_high, t * 2 + b + 1)
                    vec.tensor_tensor(xT[:, b, 1].rearrange("p k n -> p (k n)"), psT[b][:],
                                      xT[:, b, 0].rearrange("p k n -> p (k n)").bitcast(F32),
                                      ALU.subtract).then_inc(xT_ready, 1)

                for i in range(4 * KC):
                    vec.wait_ge(w_highs, i + 1)
                    vec.tensor_tensor(w[:, 1, i, :], raw[:, i % RAW, :], w[:, 0, i, :].bitcast(F32),
                                      ALU.subtract).then_inc(w_lows, 1)
                    if i == KC - 1:
                        low(0, 0)
                vec.wait_ge(bias_in, 16 * 4)

                def pair(t, end):
                    for b in range(2):
                        if not (end and b):
                            low(t + b, 1 - b)
                        i = t * 2 + b
                        for j in range(4):
                            vec.wait_ge(projected, t * 8 + b * 4 + j + 1)
                            if j == S_:
                                vec.wait_ge(biased, i + 1)
                                vec.tensor_tensor(enc[:, b, :], psP[j][:], enc[:, b, :], ALU.add).then_inc(ready, 1)
                                continue
                            if later(t) and j == K_:
                                vec.wait_ge(kv_out[b], t * 32)
                            vec.tensor_tensor(out[:, b, j - 1, :], psP[j][:], bias[:, j, :], ALU.add).then_inc(ready, 1)
                        c = Chain(vec, split, i * 5)
                        q = out[:, b, Q_ - 1, :]
                        part = [one(qp[:, k, bass.ds(i, 1), :]) for k in range(3)]
                        vec.wait_ge(ready, t * 8 + b * 4 + Q_ + 1)
                        for k in range(2):
                            c.then(vec.tensor_scalar(part[k], q, 1.0, None, ALU.mult))
                            c.wait()
                            c.then(vec.tensor_tensor(q, q, part[k], ALU.subtract))
                            c.wait()
                        c.then(vec.tensor_scalar(part[2], q, 1.0, None, ALU.mult))
                turns_ahead(vec, T2, pair)

            @block.gpsimd
            def _(pool):
                pool.wait_ge(bias_in, 16 * 4)

                def pair(t):
                    for b in range(2):
                        pool.wait_ge(enc_in[b], t * 16 + 16)
                        pool.tensor_tensor(enc[:, b, :], enc[:, b, :], bias[:, S_, :], ALU.add).then_inc(biased, 1)
                turns(pool, T2, pair)


def gather(pool, T, t, half, bufs, index, table, landed, copied, started, freed, later_):
    h = U // 2
    if later_:
        pool.wait_ge(freed, (t - 1) * U + half * h + h)
    pool.tensor_copy(index[:, half, :], T["src"][:, bass.ds(t * U + half * h, h)]).then_inc(copied, 1)
    pool.wait_ge(copied, t * 2 + half + 1)
    pool.sem_inc(started, 1)
    for u in range(half * h, half * h + h):
        pool.indirect_dma_start(bufs[:, u, :], None, table,
                                bass.IndirectOffsetOnAxis(ap=index[:, half, u - half * h:u - half * h + 1], axis=0)
                                ).then_inc(landed[u], 16)


def node_tiles(nc, engine, T, slot, n):
    return nc.values_load_multi_w_load_instructions(T["tile_of"][0:1, bass.ds(slot, n)], engines=[engine.engine],
                                                    min_val=0, max_val=NT - 1)[1]


def score_edges(nc, a, T, layer, k_dram, scores):
    with ExitStack() as stack:
        m = Memory(nc, stack, f"score{layer}")
        h, B = U // 2, 4
        V = 2
        kbuf = m.sb("kbuf", [P, U, C])
        index = m.sb("index", [P, 2, h], I32)
        hot = m.sb("hot", [P, U, P], BF16)
        hotT = m.sb("hotT", [P, 2, B, P], BF16)
        prod = m.sb("prod", [P, U // B, B, C])
        found = m.sb("found", [P, U // B, V, H])
        found_act = m.sb("found_act", [P, U // B, B - V, H])
        psT = [m.ps(f"psT{i}", [P, B, P], BF16) for i in range(2)]
        psQ = [m.ps(f"psQ{i}", [P, C]) for i in range(B)]
        landed = [m.sem(f"landed{u}") for u in range(U)]
        copied, hots, turned, hotT_ready, queried, multiplied, reduced, kept = (
            m.sem(x) for x in ("copied", "hots", "turned", "hotT_ready", "queried", "multiplied", "reduced", "kept"))
        started, reduced_act, kept_act, looked, looked_act = (
            m.sem(x) for x in ("started", "reduced_act", "kept_act", "looked", "looked_act"))
        qp, local = T["q_parts"], T["local"]
        ACT_SUMS = U // B * (B - V) * H

        def of_turn(t):
            return scores[:, bass.ds(t * U * H, U * H)].rearrange("p (j w) -> p j w", j=U // B)

        with nc.Block() as block:
            @block.gpsimd
            def _(pool):
                def turn(t):
                    for half in range(2):
                        gather(pool, T, t, half, kbuf, index, k_dram, landed, copied, started, multiplied, later(t))
                turns(pool, TURNS, turn)

            @block.vector
            def _(vec):
                def one_hot(slot, u, sem_value=None):
                    if sem_value is not None:
                        vec.wait_ge(turned, sem_value)
                    vec.tensor_scalar(hot[:, u, :], T["laneb"][:], local[:, bass.ds(slot, 1)], None,
                                      ALU.is_equal).then_inc(hots, 1)

                for u in range(h):
                    one_hot(u, u)

                def turn(t):
                    for j in range(U // B):
                        for u in range(j * B + h, j * B + h + B):
                            before = t * (U // B) + j + 2 - U // B + 1
                            first = u % B == 0
                            one_hot(t * U + u, u % U, before if first and (later(t) or u >= U) else None)
                        if later(t):
                            vec.wait_ge(reduced_act, (t - 1) * ACT_SUMS + (j + 1) * (B - V) * H)
                            vec.sem_inc(looked, 1)
                        for i in range(B):
                            u = j * B + i
                            vec.wait_ge(landed[u], t * 16 + 16)
                            vec.wait_ge(queried, t * U + u + 1)
                            vec.tensor_tensor(prod[:, j, i, :], psQ[i][:], kbuf[:, u, :],
                                              ALU.mult).then_inc(multiplied, 1)
                        vec.wait_ge(multiplied, t * U + j * B + V)
                        if later(t) and j == 0:
                            vec.wait_ge(kept, t)
                        vec.tensor_reduce(found[:, j], prod[:, j, 0:V].rearrange("p i (h d) -> p i h d", h=H), AX.X,
                                          ALU.add).then_inc(reduced, 1)
                    vec.wait_ge(reduced, t * (U // B) + U // B)
                    vec.tensor_scalar(of_turn(t)[:, :, 0:V * H], found[:].rearrange("p j i h -> p j (i h)"),
                                      1.0, None, ALU.mult).then_inc(kept, 1)
                turns(vec, TURNS, turn)

            @block.tensor
            def _(pe):
                def flip(batch, j):
                    pe.wait_ge(hots, batch * B + B)
                    for i in range(B):
                        last = pe.transpose(psT[j % 2][:, i, :], hot[:, (j * B + i) % U, :], T["identb"][:])
                    last.then_inc(turned, 1)

                flip(0, 0)

                def turn(t):
                    for j in range(U // B):
                        batch = t * (U // B) + j
                        flip(batch + 1, j + 1)
                        tiles = node_tiles(nc, pe, T, t * U + j * B, B)
                        pe.wait_ge(hotT_ready, batch + 1)
                        for i in range(B):
                            u = j * B + i
                            d = tiles[i]
                            if later(t) or j:
                                pe.wait_ge(multiplied, t * U + u - B + 1)
                            for k in range(3):
                                last = pe.matmul(psQ[i][:], hotT[:, j % 2, i, :], one(qp[:, k, bass.ds(d, 1), :]),
                                                 start=(k == 0), stop=(k == 2))
                            last.then_inc(queried, 1)
                turns(pe, TURNS, turn)

            @block.scalar
            def _(act):
                def keep(t):
                    act.wait_ge(reduced_act, t * ACT_SUMS + ACT_SUMS)
                    act.sem_inc(looked_act, 1)
                    act.copy(of_turn(t)[:, :, V * H:B * H], found_act[:].rearrange("p j i h -> p j (i h)")
                             ).then_inc(kept_act, 1)

                def add_up(t, j):
                    if later(t) and j == 0:
                        act.wait_ge(kept_act, t)
                    for i in range(V, B):
                        act.wait_ge(multiplied, t * U + j * B + i + 1)
                        for head in range(H):
                            at = prod[:, j, i, head * D:(head + 1) * D]
                            act.activation(at, at, ACT.Copy, accum_out=found_act[:, j, i - V, head:head + 1]
                                           ).then_inc(reduced_act, 1)

                def turn(t):
                    for j in range(U // B):
                        batch = t * (U // B) + j
                        act.wait_ge(turned, batch + 1)
                        if later(t) or j >= 2:
                            act.wait_ge(queried, batch * B - B)
                        act.copy(hotT[:, j % 2].rearrange("p i e -> p (i e)"),
                                 psT[j % 2][:].rearrange("p i e -> p (i e)")).then_inc(hotT_ready, 1)
                        if j >= 2:
                            add_up(t, j - 2)
                        elif later(t):
                            add_up(t - 1, U // B - 2 + j)
                            if j == 1:
                                keep(t - 1)
                turns(act, TURNS, turn)
                for j in range(U // B - 2, U // B):
                    add_up(TURNS - 1, j)
                keep(TURNS - 1)


def soften(nc, T, layer, scores, weights):
    with ExitStack() as stack:
        m = Memory(nc, stack, f"soft{layer}")
        near = m.sb("near", [P, G, P])
        rows = m.sb("rows", [P, RUN])
        run = m.sb("run", [P, RUN])
        top = m.sb("top", [P, RUN])
        ends = m.sb("ends", [P, 2, CH])
        pair = m.sb("pair", [H, 2 * CH, 2 * CH])
        best = m.sb("best", [H, 2 * CH])
        back = m.sb("back", [P, 2, CH])
        shared = m.sb("shared", [P, 2])
        pst = [m.ps(f"pst{i}", [P, 4, P]) for i in range(2)]
        psw = [m.ps(f"psw{i}", [P, 4, P]) for i in range(2)]
        pse = m.ps("pse", [H, 2 * CH])
        psb = m.ps("psb", [P, 2 * CH])
        nearby = m.sem("nearby")
        turned, in_rows, steps, ends_done, ends_in, best_done, best_out, ready, exped, returned, stored = (
            m.sem(x) for x in ("turned", "in_rows", "steps", "ends_done", "ends_in", "best_done", "best_out", "ready",
                               "exped", "returned", "stored"))
        parts = [(g, min(4, G - g)) for g in range(0, G, 4)]
        by_g = scores[:].rearrange("p (c g h) -> p g c h", c=CH, g=G)
        w_by_g = weights[:].rearrange("p (c g h) -> p g c h", c=CH, g=G)
        with nc.Block() as block:
            @block.tensor
            def _(pe):
                for n, (g, k) in enumerate(parts):
                    pe.wait_ge(nearby, n + 1)
                    if n >= 2:
                        pe.wait_ge(in_rows, n - 1)
                    for j in range(k):
                        last = pe.transpose(pst[n % 2][:, j, :], near[:, g + j, :], T["ident"][:])
                    last.then_inc(turned, 1)
                pe.wait_ge(ends_done, 1)
                pe.matmul(pse[:], T["head_of"][:], ends[:].rearrange("p e c -> p (e c)"), start=True,
                          stop=True).then_inc(ends_in, 1)
                pe.wait_ge(best_done, 1)
                pe.matmul(psb[:], T["of_head"][:], best[:], start=True, stop=True).then_inc(best_out, 1)
                for n, (g, k) in enumerate(parts):
                    pe.wait_ge(exped, n + 1)
                    if n >= 2:
                        pe.wait_ge(stored, n - 1)
                    for j in range(k):
                        last = pe.transpose(psw[n % 2][:, j, :], rows[:, (g + j) * P:(g + j + 1) * P], T["ident"][:])
                    last.then_inc(returned, 1)

            @block.scalar
            def _(act):
                for n, (g, k) in enumerate(parts):
                    act.copy(near[:, g:g + k, :].rearrange("p k (c h) -> p k c h", c=CH), by_g[:, g:g + k]
                             ).then_inc(nearby, 1)
                for n, (g, k) in enumerate(parts):
                    act.wait_ge(ready, n + 1)
                    act.activation(rows[:, g * P:(g + k) * P], rows[:, g * P:(g + k) * P], ACT.Exp,
                                   scale=float(D) ** -0.5).then_inc(exped, 1)

            @block.vector
            def _(vec):
                c = Chain(vec, steps)
                same, first, last = T["same"], T["first"], T["last"]
                for n, (g, k) in enumerate(parts):
                    vec.wait_ge(turned, n + 1)
                    vec.tensor_copy(rows[:, g * P:(g + k) * P], pst[n % 2][:, 0:k, :].rearrange("p k e -> p (k e)")
                                    ).then_inc(in_rows, 1)
                vec.wait_ge(in_rows, len(parts))
                c.then(vec.tensor_tensor_scan(run[:], same[:, 0:RUN], rows[:], NEG, ALU.add, ALU.max))
                c.wait()
                c.then(vec.tensor_tensor_scan(top[:, RUN - 1::-1], same[:, RUN:0:-1], run[:, RUN - 1::-1], NEG,
                                              ALU.add, ALU.max))
                c.wait()
                c.then(vec.tensor_scalar(ends[:, 0, :], T["chunk_of"][:], top[:, 0:1], None, ALU.mult))
                c.then(vec.tensor_scalar(ends[:, 1, :], T["chunk_of"][:], top[:, RUN - 1:RUN], None, ALU.mult))
                c.wait()
                vec.nop().then_inc(ends_done, 1)
                vec.wait_ge(ends_in, 1)
                c.then(vec.tensor_tensor(pair[:], T["linked"][:],
                                         pse[:].unsqueeze(1).to_broadcast([H, 2 * CH, 2 * CH]), ALU.add))
                c.wait()
                vec.tensor_reduce(best[:], pair[:], AX.X, ALU.max).then_inc(best_done, 1)
                vec.wait_ge(best_out, 1)
                c.then(vec.tensor_tensor(back[:], psb[:].rearrange("p (e c) -> p e c", e=2),
                                         T["chunk_of"][:].unsqueeze(1).to_broadcast([P, 2, CH]), ALU.mult))
                c.wait()
                c.then(vec.tensor_reduce(shared[:], back[:], AX.X, ALU.add))
                c.wait()
                c.then(vec.scalar_tensor_tensor(out=top[:], in0=first[:], scalar=shared[:, 0:1], in1=top[:],
                                                op0=ALU.add, op1=ALU.max))
                c.wait()
                c.then(vec.scalar_tensor_tensor(out=top[:], in0=last[:], scalar=shared[:, 1:2], in1=top[:],
                                                op0=ALU.add, op1=ALU.max))
                c.wait()
                for n, (g, k) in enumerate(parts):
                    s = slice(g * P, (g + k) * P)
                    vec.tensor_tensor(rows[:, s], rows[:, s], top[:, s], ALU.subtract).then_inc(ready, 1)
                for n, (g, k) in enumerate(parts):
                    vec.wait_ge(returned, n + 1)
                    vec.tensor_copy(w_by_g[:, g:g + k], psw[n % 2][:, 0:k, :].rearrange("p k (c h) -> p k c h", c=CH)
                                    ).then_inc(stored, 1)


def aggregate(nc, a, T, layer, v_dram, weights, agg, base_dram, x):
    with ExitStack() as stack:
        m = Memory(nc, stack, f"agg{layer}")
        h, B, R = U // 2, 4, 8
        vbuf = m.sb("vbuf", [P, U, C])
        index = m.sb("index", [P, 2, h], I32)
        hot = m.sb("hot", [P, U, P])
        wt = m.sb("wt", [P, 2, h, H])
        wv = m.sb("wv", [P, R, AW])
        zeros = m.sb("zeros", [P, 2, C // 2 + H])
        psA = m.ps("psA", [P, 2, 2, C])
        landed = [m.sem(f"landed{u}") for u in range(U)]
        copied, hots, staged, beside, weighted, summed, blank, evicted, kept, started = (
            m.sem(x) for x in ("copied", "hots", "staged", "beside", "weighted", "summed", "blank", "evicted",
                               "kept", "started"))
        base_in = m.sem("base_in")
        local = T["local"]
        parts = ((0, C // 2), (C // 2, AW))
        with nc.Block() as block:
            @block.sync
            def _(sp):
                def tile(t):
                    if later(t):
                        sp.wait_ge(weighted, t * U)
                    sp.dma_start(one(x[:, bass.ds(t, 1), :]), base_dram[bass.ds(t * P, P), :]).then_inc(base_in, 16)
                turns(sp, NT, tile)
                sp.wait_ge(base_in, 16 * NT)

            @block.gpsimd
            def _(pool):
                def turn(t):
                    for half in range(2):
                        gather(pool, T, t, half, vbuf, index, v_dram, landed, copied, started, weighted, later(t))
                turns(pool, TURNS, turn)

            @block.vector
            def _(vec):
                vec.memset(zeros[:], 0.0).then_inc(blank, 1)

                def stage(t, half):
                    if later(t):
                        vec.wait_ge(weighted, (t - 1) * U + half * h + h)
                        vec.wait_ge(beside, (t - 1) * (U // B) + (half * h + h) // B)
                    vec.tensor_scalar(wt[:, half].rearrange("p u h -> p (u h)"),
                                      weights[:, bass.ds((t * U + half * h) * H, h * H)],
                                      1.0, None, ALU.mult).then_inc(staged, 1)
                    vec.wait_ge(staged, t * 2 + half + 1)

                def turn(t):
                    for u in range(U):
                        if u % h == 0:
                            stage(t, u // h)
                        if later(t):
                            vec.wait_ge(summed, t * U + u + 2 - U)
                        vec.tensor_scalar(hot[:, u, :], T["lane"][:], local[:, bass.ds(t * U + u, 1)], None,
                                          ALU.is_equal).then_inc(hots, 1)
                        if u % B == 0:
                            if later(t) or u >= R:
                                vec.wait_ge(summed, t * U + u + B + 1 - R)
                            vec.tensor_scalar(wv[:, u % R:u % R + B, C:AW], wt[:, u // h, u % h:u % h + B, :], 1.0, None,
                                              ALU.mult).then_inc(beside, 1)
                        vec.wait_ge(landed[u], t * 16 + 16)
                        vec.tensor_tensor(wv[:, u % R, 0:C].rearrange("p (h d) -> p h d", h=H),
                                          vbuf[:, u, :].rearrange("p (h d) -> p h d", h=H),
                                          wt[:, u // h, u % h, :].unsqueeze(2).to_broadcast([P, H, D]),
                                          ALU.mult).then_inc(weighted, 1)
                turns(vec, TURNS, turn)

            @block.scalar
            def _(act):
                act.wait_ge(blank, 1)
                act.sem_inc(evicted, 2)
                for d in range(NT):
                    full = act.value_load(T["full_at"][0:1, d:d + 1], min_val=1, max_val=SLOTS + 1)
                    act.wait_ge(summed, full if d < NT - 1 else SLOTS + 1)
                    for e, (lo, hi) in enumerate(parts):
                        act.copy(agg[:, d, lo:hi], psA[:, d % 2, e, 0:hi - lo]).then_inc(kept, 1)
                    act.wait_ge(kept, 2 * d + 2)
                    act.copy(psA[:, d % 2, :, 0:C // 2 + H], zeros[:]).then_inc(evicted, 1)

            @block.tensor
            def _(pe):
                pe.wait_ge(blank, 1)
                for bank in range(2):
                    for e in range(2):
                        last = pe.matmul(psA[:, bank, e, 0:C // 2 + H], T["ident"][:], zeros[:, e, :], start=True,
                                         stop=True)
                last.then_inc(summed, 1)

                def turn(t):
                    for u in range(U):
                        if u % B == 0:
                            tiles = node_tiles(nc, pe, T, t * U + u, B)
                        d = tiles[u % B]
                        pe.wait_ge(hots, t * U + u + 1)
                        pe.wait_ge(beside, t * (U // B) + u // B + 1)
                        pe.wait_ge(weighted, t * U + u + 1)
                        pe.wait_ge(evicted, d + 1)
                        for e, (lo, hi) in enumerate(parts):
                            last = pe.matmul(psA[:, bass.ds(d % 2, 1), e, 0:hi - lo].rearrange("p o w -> p (o w)"),
                                             hot[:, u, :], wv[:, u % R, lo:hi], start=False, stop=True,
                                             skip_group_check=True)
                        last.then_inc(summed, 1)
                turns(pe, TURNS, turn)



def combine(nc, a, T, layer, agg, x, out_dram):
    final = layer == LAYERS - 1
    with ExitStack() as stack:
        m = Memory(nc, stack, f"comb{layer}")
        den = m.sb("den", [P, NT, H])
        gb = m.sb("gb", [P, 2, C])
        shift = m.sb("shift", [P, GROUPS, GN])
        ON_POOL = 3 * GN
        scaled_vec, done_vec = m.sem("scaled_vec"), m.sem("done_vec")
        gb_in, steps, summed, shifted, normed, scaled, done, stored = (
            m.sem(s) for s in ("gb_in", "steps", "summed", "shifted", "normed", "scaled", "done", "stored"))
        ln = LayerNorm(nc, m, GN) if final else None

        def rows_of(dram, g):
            return dram[g * NODES:(g + 1) * NODES, :].rearrange("(t p) c -> p t c", p=P)

        def tiles(g):
            return range(g * GN, (g + 1) * GN)

        with nc.Block() as block:
            @block.sync
            def _(sp):
                if final:
                    sp.dma_start(gb[:, 0], a["L0_gnn_ln_g"].partition_broadcast(P)).then_inc(gb_in, 16)
                    sp.dma_start(gb[:, 1], a["L0_gnn_ln_b"].partition_broadcast(P)).then_inc(gb_in, 16)
                for g in range(GROUPS):
                    if not final:
                        sp.wait_ge(summed, (g + 1) * GN)
                    elif (g + 1) * GN <= ON_POOL:
                        sp.wait_ge(done, (g + 1) * GN)
                    else:
                        sp.wait_ge(done_vec, (g + 1) * GN - ON_POOL)
                    sp.dma_start(rows_of(out_dram, g), x[:, g * GN:(g + 1) * GN, :]).then_inc(stored, 16)
                sp.wait_ge(stored, 16 * GROUPS)

            @block.vector
            def _(vec):
                c = Chain(vec, steps)
                c.then(vec.tensor_scalar(den[:], agg[:, :, C:AW], 1e-16, None, ALU.add))
                c.wait()
                c.then(vec.reciprocal(den[:], den[:]))
                c.wait()

                def add(g):
                    for t in tiles(g):
                        at = agg[:, t, 0:C].rearrange("p (h d) -> p h d", h=H)
                        c.then(vec.tensor_tensor(at, at, den[:, t].unsqueeze(2).to_broadcast([P, H, D]), ALU.mult))
                    c.wait()
                    for t in tiles(g):
                        vec.tensor_tensor(x[:, t, :], x[:, t, :], agg[:, t, 0:C], ALU.add).then_inc(summed, 1)

                def norm_shift(g):
                    vec.wait_ge(summed, (g + 1) * GN)
                    if g:
                        vec.wait_ge(normed, g * GN)
                    ln.stats(vec, lambda n: x[:, g * GN + n, :], g)
                    ln.scale(vec, g)
                    vec.scalar_tensor_tensor(out=shift[:, g, :], in0=ln.mv[:, :, 0], scalar=-1.0, in1=ln.rstd[:],
                                             op0=ALU.mult, op1=ALU.mult).then_inc(shifted, 1)

                for g in range(GROUPS):
                    add(g)
                    if final:
                        norm_shift(g)
                if final:
                    vec.wait_ge(gb_in, 32)
                    for t in range(ON_POOL, NT):
                        vec.wait_ge(normed, t + 1)
                        vec.tensor_tensor(x[:, t, :], x[:, t, :], gb[:, 0], ALU.mult).then_inc(scaled_vec, 1)
                    for t in range(ON_POOL, NT):
                        vec.wait_ge(scaled_vec, t + 1 - ON_POOL)
                        vec.tensor_tensor(x[:, t, :], x[:, t, :], gb[:, 1], ALU.add).then_inc(done_vec, 1)

            @block.scalar
            def _(act):
                for g in range(GROUPS):
                    if final:
                        ln.root(act, g)
                        act.wait_ge(shifted, g + 1)
                        for n, t in enumerate(tiles(g)):
                            act.activation(x[:, t, :], x[:, t, :], ACT.Identity, bias=shift[:, g, n:n + 1],
                                           scale=ln.rstd[:, n:n + 1]).then_inc(normed, 1)

            @block.gpsimd
            def _(pool):
                if final:
                    ln.set_eps(pool)
                    pool.wait_ge(gb_in, 32)
                    for t in range(ON_POOL):
                        pool.wait_ge(normed, t + 1)
                        pool.tensor_tensor(x[:, t, :], x[:, t, :], gb[:, 0], ALU.mult).then_inc(scaled, 1)
                        pool.wait_ge(scaled, t + 1)
                        pool.tensor_tensor(x[:, t, :], x[:, t, :], gb[:, 1], ALU.add).then_inc(done, 1)


class LayerNorm:

    def __init__(self, nc, m, n, prefix="ln"):
        self.n = n
        self.st = m.sb(f"{prefix}_stats", [P, n, 6])
        self.mv = m.sb(f"{prefix}_mv", [P, n, 2])
        self.eps = m.sb(f"{prefix}_eps", [P, 1])
        self.std = m.sb(f"{prefix}_std", [P, n])
        self.rstd = m.sb(f"{prefix}_rstd", [P, n])
        self.all_st = m.sem(f"{prefix}_all_st")
        self.have_eps, self.have_st, self.have_mv, self.have_std, self.have_rstd = (
            m.sem(x) for x in (f"{prefix}_have_eps", f"{prefix}_have_st", f"{prefix}_have_mv", f"{prefix}_have_std", f"{prefix}_have_rstd"))

    def set_eps(self, engine):
        engine.memset(self.eps[:], EPS).then_inc(self.have_eps, 1)

    def stats(self, vec, row, turn=0):
        for t in range(self.n):
            vec.bn_stats(self.st[:, t, :], row(t)).then_inc(self.have_st, 1)
        vec.wait_ge(self.have_st, (turn + 1) * self.n)
        vec.sem_inc(self.all_st, 1)
        for t in range(self.n):
            vec.bn_aggr(self.mv[:, t, :], self.st[:, t, :]).then_inc(self.have_mv, 1)

    def root(self, act, turn=0):
        if isinstance(turn, int) and turn == 0:
            act.wait_ge(self.have_eps, 1)
        act.wait_ge(self.have_mv, (turn + 1) * self.n)
        act.activation(self.std[:], self.mv[:, :, 1], ACT.Sqrt, bias=self.eps[:, 0:1]).then_inc(self.have_std, 1)

    def scale(self, vec, turn=0):
        vec.wait_ge(self.have_std, turn + 1)
        vec.reciprocal(self.rstd[:], self.std[:]).then_inc(self.have_rstd, 1)
        vec.wait_ge(self.have_rstd, turn + 1)
        vec.wait_ge(self.have_mv, (turn + 1) * self.n)

    def apply(self, vec, t, out, in_):
        return vec.tensor_scalar(out, in_, self.mv[:, t, 0:1], self.rstd[:, t:t + 1], ALU.subtract, ALU.mult)


def turn_group(pe, T, tile, psT, turned, free, wait_free):
    for n in range(GN):
        if wait_free(n) is not None:
            pe.wait_ge(free, wait_free(n))
        for k in range(KC):
            last = pe.transpose(psT[n % 2][:, k, :], tile[:, n, k * P:(k + 1) * P], T["ident"][:])
        last.then_inc(turned, 1)


def node_mlp(nc, a, T, y_dram, enc_dram, qT, folded, x3_dram, y3_dram):
    with ExitStack() as stack:
        m = Memory(nc, stack, "mlp")
        FC = F1 // P
        RAW = 4
        raw = m.sb("raw", [P, RAW, C])
        w1 = m.sb("w1", [P, 2, KC, F1], F32R)
        w2 = m.sb("w2", [P, 2, FC, C], F32R)
        b1 = m.sb("b1", [P, FC])
        rowsb = m.sb("rowsb", [P, 4, C])
        y = m.sb("y", [P, GN, C])
        enc = m.sb("enc", [P, GN, C])
        x = m.sb("x", [P, GN, C])
        yT = m.sb("yT", [P, 2, KC, NODES], F32R)
        h = m.sb("h", [P, 2, NODES])
        hT = m.sb("hT", [P, 2, FC, NODES], F32R)
        yres = m.sb("yres", [P, GN, C])
        z = m.sb("z", [P, GN, C])
        q = m.sb("q", [P, 2, NODES])
        psT = [m.ps(f"psT{i}", [P, KC, P]) for i in range(2)]
        psH = [m.ps(f"psH{i}", [P, NODES]) for i in range(2)]
        psO = [m.ps(f"psO{i}", [P, C]) for i in range(2)]
        psX = [m.ps(f"psX{i}", [P, C]) for i in range(2)]
        w_in = [m.sem(f"w_in{i}") for i in range(RAW)]
        b_in, w_highs, w_lows, x_in, x_biased, mixed, enc_mixed, x3_out, y3_out, enc_used = (
            m.sem(s) for s in ("b_in", "w_highs", "w_lows", "x_in", "x_biased", "mixed", "enc_mixed", "x3_out", "y3_out",
                               "enc_used"))
        q_in, q_free, b1_in, b_sum, yres_biased = (m.sem(s) for s in ("q_in", "q_free", "b1_in", "b_sum", "yres_biased"))
        (y_in, yres_in, enc_in, turned, yT_high, yT_in, hidden, h_in, hT_high, hT_in, out_done, z_in, steps, x3_done,
         y3_done) = (
            m.sem(s) for s in ("y_in", "yres_in", "enc_in", "turned", "yT_high", "yT_in", "hidden", "h_in", "hT_high",
                               "hT_in", "out_done", "z_in", "steps", "x3_done", "y3_done"))
        ln, ln3 = LayerNorm(nc, m, GN), LayerNorm(nc, m, GN, "ln3")
        halves = F1 // C
        pieces = [(a["L0_gnn_W1"][k * P:(k + 1) * P, e * C:(e + 1) * C], lambda i, k=k, e=e: w1[:, i, k, e * C:(e + 1) * C])
                  for k in range(KC) for e in range(halves)]
        W1_PIECES = len(pieces)
        pieces += [(a["L0_gnn_W2"][f * P:(f + 1) * P, :], lambda i, f=f: w2[:, i, f, :]) for f in range(FC)]

        def rows_of(dram, g):
            return dram[bass.ds(g * NODES, NODES), :].rearrange("(t p) c -> p t c", p=P)

        def over(j):
            return rowsb[:, j, :].unsqueeze(1).to_broadcast([P, GN, C])

        with nc.Block() as block:
            @block.sync
            def _(sp):
                sp.dma_start(y[:], rows_of(y_dram, 0)).then_inc(y_in, 16)
                sp.dma_start(b1[:], a["L0_gnn_b1"].rearrange("(f p) -> p f", p=P), allow_slow_non_contiguous=True
                             ).then_inc(b1_in, 16)
                for i, (rows, _part) in enumerate(pieces):
                    if i == W1_PIECES + RAW:
                        sp.wait_ge(turned, GN)
                        sp.dma_start(y[:], rows_of(y_dram, 1)).then_inc(y_in, 16)
                    if i >= RAW:
                        sp.wait_ge(w_lows, i + 1 - RAW)
                    sp.dma_start(raw[:, i % RAW, :], rows).then_inc(w_in[i % RAW], 16)
                sp.dma_start(yres[:], rows_of(y_dram, 0)).then_inc(yres_in, 16)
                sp.dma_start(enc[:], rows_of(enc_dram, 0)).then_inc(enc_in, 16)
                sp.dma_start(x[:], rows_of(a["x"], 0)).then_inc(x_in, 16)
                for j, n in enumerate(("L0_gnn_b2", "L0_gnn_ln_g", "L0_gnn_ln_b", "L0_mix_b_out")):
                    sp.dma_start(rowsb[:, j], a[n].partition_broadcast(P)).then_inc(b_in, 16)

                def leave(g):
                    sp.wait_ge(x3_done, g + 1)
                    sp.dma_start(rows_of(x3_dram, g), z[:]).then_inc(x3_out, 16)
                    sp.wait_ge(y3_done, (g + 1) * GN)
                    sp.dma_start(rows_of(y3_dram, g), x[:]).then_inc(y3_out, 16)

                def group(g, end):
                    if later(g) and not end:
                        sp.wait_ge(turned, g * GN + GN)
                        sp.dma_start(y[:], rows_of(y_dram, g + 1)).then_inc(y_in, 16)
                    if later(g):
                        sp.wait_ge(enc_used, g)
                        sp.dma_start(enc[:], rows_of(enc_dram, g)).then_inc(enc_in, 16)
                        leave(g - 1)
                        sp.wait_ge(y3_out, g * 16)
                        if end:
                            r0 = (GROUPS - 1) * NODES
                            sp.dma_start(x[:, 0:GN - 1, :], a["x"][r0:(NT - 1) * P, :].rearrange("(t p) c -> p t c", p=P)
                                         ).then_inc(x_in, 16)
                            sp.dma_start(x[0:LAST, GN - 1, :], a["x"][(NT - 1) * P:N, :]).then_inc(x_in, 16)
                        else:
                            sp.dma_start(x[:], rows_of(a["x"], g)).then_inc(x_in, 16)
                    if not end:
                        sp.wait_ge(z_in, g * GN + GN)
                        sp.dma_start(yres[:], rows_of(y_dram, g + 1)).then_inc(yres_in, 16)
                turns_ahead(sp, GROUPS, group)
                leave(GROUPS - 1)
                sp.wait_ge(x3_out, 16 * GROUPS)
                sp.wait_ge(y3_out, 16 * GROUPS)

            @block.tensor
            def _(pe):
                def flip(g, n):
                    if n == 0:
                        pe.wait_ge(y_in, g * 16 + 16)
                    if later(g) or n >= 2:
                        pe.wait_ge(yT_in, g * GN + n - 1)
                    for k in range(KC):
                        last = pe.transpose(psT[n % 2][:, k, :], y[:, n, k * P:(k + 1) * P], T["ident"][:])
                    last.then_inc(turned, 1)

                for n in range(GN):
                    flip(0, n)

                def group(g, end):
                    if not later(g):
                        pe.wait_ge(w_lows, W1_PIECES)
                    pe.wait_ge(yT_in, g * GN + GN)
                    for f in range(FC):
                        if later(g) or f >= 2:
                            pe.wait_ge(h_in, g * FC + f - 1)
                        fs = slice(f * P, (f + 1) * P)
                        for k in range(KC):
                            last = product(pe, psH[f % 2][:], [w1[:, i, k, fs] for i in range(2)],
                                           [yT[:, i, k, :] for i in range(2)], start=(k == 0), stop=(k == KC - 1))
                        last.then_inc(hidden, 1)
                    if not end:
                        flip(g + 1, 0)
                        flip(g + 1, 1)
                    pe.wait_ge(q_in, g + 1)
                    for n in range(GN):
                        if later(g) or n >= 2:
                            pe.wait_ge(enc_mixed, g * GN + n - 1)
                        for e in range(2):
                            last = pe.matmul(psX[n % 2][:], q[:, e, n * P:(n + 1) * P], folded[:, e, :],
                                             start=(e == 0), stop=(e == 1))
                        last.then_inc(mixed, 1)
                    if not later(g):
                        pe.wait_ge(w_lows, len(pieces))
                    pe.wait_ge(hT_in, g * FC + FC)
                    for n in range(GN):
                        if later(g) or n >= 2:
                            pe.wait_ge(z_in, g * GN + n - 1)
                        for f in range(FC):
                            last = product(pe, psO[n % 2][:], [hT[:, i, f, n * P:(n + 1) * P] for i in range(2)],
                                           [w2[:, i, f, :] for i in range(2)], start=(f == 0),
                                           stop=(f == FC - 1))
                        last.then_inc(out_done, 1)
                        if not end and n + 2 < GN:
                            flip(g + 1, n + 2)
                turns_ahead(pe, GROUPS, group)

            @block.scalar
            def _(act):
                def high(g, n):
                    act.wait_ge(turned, g * GN + n + 1)
                    act.copy(yT[:, 0, :, n * P:(n + 1) * P], psT[n % 2][:]).then_inc(yT_high, 1)

                def stage_q(g):
                    act.copy(q[:], qT[:, :, bass.ds(g * NODES, NODES)]).then_inc(q_in, 1)

                def part_high(i):
                    act.wait_ge(w_in[i % RAW], i // RAW * 16 + 16)
                    act.copy(pieces[i][1](0), raw[:, i % RAW, :]).then_inc(w_highs, 1)

                for i in range(W1_PIECES):
                    if i in (2, 3, 4, 5):
                        high(0, i - 2)
                    part_high(i)
                stage_q(0)
                act.wait_ge(b1_in, 16)
                act.wait_ge(ln.have_eps, 1)
                act.wait_ge(ln3.have_eps, 1)

                def group(g, end):
                    for f in range(FC):
                        act.wait_ge(hidden, g * FC + f + 1)
                        if later(g) or f >= 2:
                            act.wait_ge(hT_in, g * FC + f - 1)
                        act.activation(h[:, f % 2, :], psH[f % 2][:], ACT.Relu, bias=b1[:, f:f + 1]).then_inc(h_in, 1)
                        act.wait_ge(h_in, g * FC + f + 1)
                        act.copy(hT[:, 0, f, :], h[:, f % 2, :]).then_inc(hT_high, 1)
                        if not later(g):
                            part_high(W1_PIECES + f)
                        if later(g) and f == 2:
                            ln.root(act, g - 1)
                        if later(g) and f == 6:
                            ln3.root(act, g - 1)
                    if not end:
                        for n in range(GN):
                            high(g + 1, n)
                        act.wait_ge(mixed, g * GN + GN)
                        act.sem_inc(q_free, 1)
                        stage_q(g + 1)
                turns_ahead(act, GROUPS, group)
                ln.root(act, GROUPS - 1)
                ln3.root(act, GROUPS - 1)

            @block.gpsimd
            def _(pool):
                ln.set_eps(pool)
                ln3.set_eps(pool)

                def y_biased(g, n):
                    pool.wait_ge(yres_in, g * 16 + 16)
                    pool.tensor_tensor(yres[:, n, :], yres[:, n, :], rowsb[:, 0, :], ALU.add).then_inc(yres_biased, 1)

                def group(g, end):
                    for f in range(FC):
                        pool.wait_ge(hT_high, g * FC + f + 1)
                        pool.tensor_tensor(hT[:, 1, f, :], h[:, f % 2, :], hT[:, 0, f, :].bitcast(F32),
                                           ALU.subtract).then_inc(hT_in, 1)
                        if later(g) and f >= FC - GN:
                            y_biased(g, f - (FC - GN))
                    if not later(g):
                        pool.wait_ge(b_in, 16 * 4)
                        for n in range(GN):
                            y_biased(0, n)
                        pool.tensor_tensor(rowsb[:, 3, :], rowsb[:, 3, :], rowsb[:, 2, :], ALU.add).then_inc(b_sum, 1)
                        pool.wait_ge(b_sum, 1)
                    pool.wait_ge(x_in, g * 16 + (32 if end else 16))
                    pool.tensor_tensor(x[:], x[:], over(3), ALU.add).then_inc(x_biased, 1)
                turns_ahead(pool, GROUPS, group)

            @block.vector
            def _(vec):
                def low(g, n):
                    vec.wait_ge(yT_high, g * GN + n + 1)
                    vec.tensor_tensor(yT[:, 1, :, n * P:(n + 1) * P], psT[n % 2][:],
                                      yT[:, 0, :, n * P:(n + 1) * P].bitcast(F32), ALU.subtract).then_inc(yT_in, 1)

                for i, (_rows, part) in enumerate(pieces):
                    if i in (2, 3, 4, 5):
                        low(0, i - 2)
                    vec.wait_ge(w_highs, i + 1)
                    vec.tensor_tensor(part(1), raw[:, i % RAW, :], part(0).bitcast(F32), ALU.subtract
                                      ).then_inc(w_lows, 1)
                vec.wait_ge(b_in, 16 * 4)

                def group(g, end):
                    c = Chain(vec, steps, g * (GN + 1))
                    if not end:
                        low(g + 1, 0)
                        low(g + 1, 1)
                    vec.wait_ge(enc_in, g * 16 + 16)
                    for n in range(GN):
                        vec.wait_ge(mixed, g * GN + n + 1)
                        vec.tensor_tensor(enc[:, n, :], psX[n % 2][:], enc[:, n, :], ALU.add).then_inc(enc_mixed, 1)
                    vec.wait_ge(yres_biased, g * GN + GN)
                    if later(g):
                        vec.wait_ge(x3_out, g * 16)
                    for n in range(GN):
                        vec.wait_ge(out_done, g * GN + n + 1)
                        vec.tensor_tensor(z[:, n, :], psO[n % 2][:], yres[:, n, :], ALU.add).then_inc(z_in, 1)
                        if not end and n + 2 < GN:
                            low(g + 1, n + 2)
                    vec.wait_ge(z_in, g * GN + GN)
                    ln.stats(vec, lambda n: z[:, n, :], g)
                    ln.scale(vec, g)
                    for n in range(GN):
                        c.then(ln.apply(vec, n, z[:, n, :], z[:, n, :]))
                    c.wait()
                    c.then(vec.tensor_tensor(z[:], z[:], over(1), ALU.mult))
                    c.wait()
                    vec.wait_ge(enc_mixed, g * GN + GN)
                    vec.tensor_tensor(z[:], z[:], enc[:], ALU.add).then_inc(enc_used, 1)
                    vec.wait_ge(enc_used, g + 1)
                    vec.wait_ge(x_biased, g + 1)
                    vec.tensor_tensor(z[:], z[:], x[:], ALU.add).then_inc(x3_done, 1)
                    vec.wait_ge(x3_done, g + 1)
                    ln3.stats(vec, lambda n: z[:, n, :], g)
                    ln3.scale(vec, g)
                    for n in range(GN):
                        ln3.apply(vec, n, x[:, n, :], z[:, n, :]).then_inc(y3_done, 1)
                turns_ahead(vec, GROUPS, group)


def project_slices(nc, a, T, xn_dram, qT, folded):
    with ExitStack() as stack:
        m = Memory(nc, stack, "slice")
        HS = H * SL
        VW = 4 * D + 1
        raw = m.sb("raw", [P, KC, C])
        w_in = m.sb("w_in", [P, 2, KC, C], F32R)
        w_out = m.sb("w_out", [P, KC, C])
        b_in = m.sb("b_in", [P, KC])
        wqkv = m.sb("wqkv", [P, 2 * (2 * SL + D)])
        x = m.sb("x", [P, GN, C])
        xT = m.sb("xT", [P, 2, KC, NODES], F32R)
        mid = m.sb("mid", [P, KC, NODES])
        q = m.sb("q", [P, GN, HS])
        qsum = m.sb("qsum", [P, GN * H])
        kall = m.sb("kall", [P, NT, HS])
        vall = m.sb("vall", [P, NT, 2, VW])
        kmax = m.sb("kmax", [P, HS])
        ktop = m.sb("ktop", [P, 2])
        kdiag = m.sb("kdiag", [P, 2, P])
        ones = m.sb("ones", [P, P])
        ksum = m.sb("ksum", [P, 2])
        kv = m.sb("kv", [P, 2, 4 * D])
        kvT = m.sb("kvT", [P, 2, 2, P])
        psT = [m.ps(f"psT{i}", [P, KC, P]) for i in range(2)]
        psM = [m.ps(f"psM{i}", [P, NODES]) for i in range(2)]
        psQ = [m.ps(f"psQ{i}", [P, KC, 4 * D]) for i in range(2)]
        names = ("zeroed", "w_landed", "x_in", "turned", "xT_in", "middled", "mid_in", "projected", "q_in", "kv_in",
                 "kmaxed", "steps", "shifted", "exped", "normed", "q_turned", "qT_in", "kflip", "ktopped", "kspread",
                 "kshifted", "kexped", "kv_done", "kv_in2", "kvflip", "kvT_in", "fold_done", "ones_in", "fixed",
                 "w_in_landed", "out_landed", "w_high", "w_low", "xT_high")
        s = {n: m.sem(n) for n in names}
        W2 = 2 * SL
        with nc.Block() as block:
            @block.gpsimd
            def _(pool):
                pool.memset(wqkv[:], 0.0).then_inc(s["zeroed"], 1)
                pool.memset(ones[:], 1.0).then_inc(s["ones_in"], 1)
                pool.memset(vall[:, :, :, 4 * D:VW], 1.0).then_inc(s["ones_in"], 1)
                pool.memset(kmax[:], -3e38).then_inc(s["ones_in"], 1)
                pool.memset(kv[:], 0.0).then_inc(s["ones_in"], 1)

            @block.sync
            def _(sp):
                def load(g):
                    sp.dma_start(x[:], xn_dram[bass.ds(g * NODES, NODES), :].rearrange("(t p) c -> p t c", p=P)
                                 ).then_inc(s["x_in"], 16)

                load(0)
                sp.dma_start(raw[:], a["L0_mix_W_in"].rearrange("(k p) n -> p k n", p=P)).then_inc(s["w_in_landed"], 16)
                sp.dma_start(b_in[:], a["L0_mix_b_in"].rearrange("(k p) -> p k", p=P), allow_slow_non_contiguous=True
                             ).then_inc(s["w_landed"], 16)
                sp.wait_ge(s["zeroed"], 1)
                for j in range(2):
                    r = slice(j * D, (j + 1) * D)
                    sp.dma_start(wqkv[r, j * SL:(j + 1) * SL], a["L0_mix_Wq"]).then_inc(s["w_landed"], 16)
                    sp.dma_start(wqkv[r, W2 + j * SL:W2 + (j + 1) * SL], a["L0_mix_Wk"]).then_inc(s["w_landed"], 16)
                    sp.dma_start(wqkv[r, 2 * W2 + j * D:2 * W2 + (j + 1) * D], a["L0_mix_Wv"]).then_inc(s["w_landed"], 16)

                sp.dma_start(w_out[:], a["L0_mix_W_out"].rearrange("(k p) n -> p k n", p=P)).then_inc(s["out_landed"], 16)

                def group(g, end):
                    if not end:
                        sp.wait_ge(s["turned"], g * GN + GN)
                        load(g + 1)
                turns_ahead(sp, GROUPS, group)

            @block.tensor
            def _(pe):
                def flip(g):
                    pe.wait_ge(s["x_in"], g * 16 + 16)
                    turn_group(pe, T, x, psT, s["turned"], s["xT_in"], lambda n: g * GN + n - 1 if n >= 2 else None)

                def flip_q(g):
                    pe.wait_ge(s["normed"], g + 1)
                    for e in range(2):
                        for n in range(GN):
                            last = pe.transpose(psT[e][:, n, :], q[:, n, e * P:(e + 1) * P], T["ident"][:])
                        last.then_inc(s["q_turned"], 1)

                flip(0)

                def group(g, end):
                    if not later(g):
                        pe.wait_ge(s["w_low"], 1)
                    pe.wait_ge(s["xT_in"], g * GN + GN)
                    for c in range(KC):
                        if later(g) or c >= 2:
                            pe.wait_ge(s["mid_in"], g * KC + c - 1)
                        for k in range(KC):
                            last = product(pe, psM[c % 2][:], [w_in[:, i, k, c * P:(c + 1) * P] for i in range(2)],
                                           [xT[:, i, k, :] for i in range(2)], start=(k == 0), stop=(k == KC - 1))
                        last.then_inc(s["middled"], 1)
                    if not end:
                        flip(g + 1)
                    if later(g):
                        if not end:
                            pe.wait_ge(s["xT_in"], (g + 2) * GN)
                        flip_q(g - 1)
                    if not later(g):
                        pe.wait_ge(s["w_landed"], 16 * 7)
                    pe.wait_ge(s["mid_in"], g * KC + KC)
                    for n in range(GN):
                        if later(g) or n >= 2:
                            pe.wait_ge(s["kv_in"], g * GN + n - 1)
                            pe.wait_ge(s["kmaxed"], g * GN + n - 1)
                        for c in range(KC):
                            last = pe.matmul(psQ[n % 2][:, c, :], mid[:, c, n * P:(n + 1) * P], wqkv[:], start=True,
                                             stop=True)
                        last.then_inc(s["projected"], 1)
                    if later(g):
                        pe.wait_ge(s["qT_in"], g * 2)
                turns_ahead(pe, GROUPS, group)
                flip_q(GROUPS - 1)
                pe.wait_ge(s["out_landed"], 16)

                pe.wait_ge(s["qT_in"], 2 * GROUPS)
                pe.wait_ge(s["kmaxed"], NT)
                for e in range(2):
                    last = pe.transpose(psT[0][:, e, :], kmax[:, e * P:(e + 1) * P], T["ident"][:])
                last.then_inc(s["kflip"], 1)
                pe.wait_ge(s["ktopped"], 2)
                pe.wait_ge(s["ones_in"], 4)
                for e in range(2):
                    last = pe.matmul(psT[1][:, e, :], ones[:], kdiag[:, e, :], start=True, stop=True)
                last.then_inc(s["kspread"], 1)
                pe.wait_ge(s["kv_in"], NT)
                for e in range(2):
                    for t in range(NT):
                        if e == 0 and t % GN == 0:
                            pe.wait_ge(s["kexped"], t // GN + 1)
                        r = P if t < NT - 1 else LAST
                        last = pe.matmul(psM[e][:, 0:VW], kall[0:r, t, e * P:(e + 1) * P], vall[0:r, t, e, :],
                                         start=(t == 0), stop=(t == NT - 1))
                    last.then_inc(s["kv_done"], 1)
                pe.wait_ge(s["kv_in2"], 2)
                for e in range(2):
                    for c in range(2):
                        last = pe.transpose(psT[0][:, 2 * e + c, :], kv[:, e, c * P:(c + 1) * P], T["ident"][:])
                last.then_inc(s["kvflip"], 1)
                pe.wait_ge(s["kvT_in"], 1)
                for e in range(2):
                    for c in range(2):
                        last = pe.matmul(psM[e][:], kvT[:, e, c, :], w_out[:, 2 * e + c, :], start=(c == 0), stop=(c == 1))
                    last.then_inc(s["fold_done"], 1)

            @block.scalar
            def _(act):
                act.wait_ge(s["ones_in"], 4)

                def high(g):
                    for n in range(GN):
                        act.wait_ge(s["turned"], g * GN + n + 1)
                        act.copy(xT[:, 0, :, n * P:(n + 1) * P], psT[n % 2][:]).then_inc(s["xT_high"], 1)

                high(0)
                act.wait_ge(s["w_in_landed"], 16)
                act.copy(w_in[:, 0], raw[:]).then_inc(s["w_high"], 1)
                act.wait_ge(s["w_landed"], 16 * 7)

                def group(g, end):
                    for c in range(KC):
                        act.wait_ge(s["middled"], g * KC + c + 1)
                        act.activation(mid[:, c, :], psM[c % 2][:], ACT.Identity, bias=b_in[:, c:c + 1]
                                       ).then_inc(s["mid_in"], 1)
                    if not end:
                        high(g + 1)
                    for n in range(GN):
                        act.wait_ge(s["projected"], g * GN + n + 1)
                        ps = psQ[n % 2]
                        if n == 0 and later(g):
                            act.wait_ge(s["q_turned"], g * 2)
                        act.copy(q[:, n, :].rearrange("p (c w) -> p c w", c=KC), ps[:, :, 0:W2]).then_inc(s["q_in"], 1)
                        act.copy(one(kall[:, bass.ds(g * GN + n, 1), :]).rearrange("p (c w) -> p c w", c=KC),
                                 ps[:, :, W2:2 * W2])
                        for e in range(2):
                            last = act.copy(vall[:, bass.ds(g * GN + n, 1), e, 0:4 * D].rearrange(
                                "p o (c w) -> p (o c) w", c=2), ps[:, 2 * e:2 * e + 2, 2 * W2:])
                        last.then_inc(s["kv_in"], 1)
                    act.wait_ge(s["shifted"], g + 1)
                    act.activation(q[:], q[:], ACT.Exp).then_inc(s["exped"], 1)
                turns_ahead(act, GROUPS, group)
                for t in range(GROUPS):
                    r = slice(t * GN, (t + 1) * GN)
                    act.wait_ge(s["kshifted"], t + 1)
                    act.activation(kall[:, r, :], kall[:, r, :], ACT.Exp).then_inc(s["kexped"], 1)

            @block.vector
            def _(vec):
                vec.wait_ge(s["ones_in"], 4)

                def k_top(g, n, rows):
                    km = kmax[0:rows, :].rearrange("p (c w) -> p c w", c=KC)
                    vec.wait_ge(s["kv_in"], g * GN + n + 1)
                    if later(g) or n:
                        vec.wait_ge(s["kmaxed"], g * GN + n)
                    vec.tensor_tensor(km, km, psQ[n % 2][0:rows, :, W2:2 * W2], ALU.max).then_inc(s["kmaxed"], 1)

                def low(g):
                    for n in range(GN):
                        vec.wait_ge(s["xT_high"], g * GN + n + 1)
                        vec.tensor_tensor(xT[:, 1, :, n * P:(n + 1) * P], psT[n % 2][:],
                                          xT[:, 0, :, n * P:(n + 1) * P].bitcast(F32), ALU.subtract
                                          ).then_inc(s["xT_in"], 1)

                def take_q(g):
                    for e in range(2):
                        vec.wait_ge(s["q_turned"], g * 2 + e + 1)
                        vec.tensor_scalar(qT[:, e, bass.ds(g * NODES, NODES)], psT[e][:].rearrange("p k n -> p (k n)"),
                                          1.0, None, ALU.mult).then_inc(s["qT_in"], 1)

                low(0)
                vec.wait_ge(s["w_high"], 1)
                vec.tensor_tensor(w_in[:, 1], raw[:], w_in[:, 0].bitcast(F32), ALU.subtract).then_inc(s["w_low"], 1)

                def group(g, end, rows_of_last=P):
                    if not end:
                        low(g + 1)
                    if later(g):
                        take_q(g - 1)
                    c = Chain(vec, s["steps"], g * 3)
                    for n in range(GN):
                        k_top(g, n, P if n < GN - 1 else rows_of_last)
                    vec.wait_ge(s["q_in"], g * GN + GN)
                    by_head = q[:].rearrange("p n (h s) -> p (n h) s", s=SL)
                    c.then(vec.tensor_reduce(qsum[:], by_head, AX.X, ALU.max))
                    c.wait()
                    vec.tensor_tensor(by_head, by_head, qsum[:].unsqueeze(2).to_broadcast([P, GN * H, SL]),
                                      ALU.subtract).then_inc(s["shifted"], 1)
                    vec.wait_ge(s["exped"], g + 1)
                    c.then(vec.tensor_reduce(qsum[:], by_head, AX.X, ALU.add))
                    c.wait()
                    c.then(vec.reciprocal(qsum[:], qsum[:]))
                    c.wait()
                    vec.tensor_tensor(by_head, by_head, qsum[:].unsqueeze(2).to_broadcast([P, GN * H, SL]),
                                      ALU.mult).then_inc(s["normed"], 1)
                group(0, False)
                with vec.Fori(1, GROUPS - 1) as g:
                    group(g, False)
                group(GROUPS - 1, True, LAST)
                take_q(GROUPS - 1)

                c = Chain(vec, s["fixed"])
                vec.wait_ge(s["kflip"], 1)
                c.then(vec.tensor_reduce(ktop[:], psT[0][:, 0:2, :], AX.X, ALU.max))
                c.wait()
                for e in range(2):
                    vec.tensor_scalar(kdiag[:, e, :], T["ident"][:], ktop[:, e:e + 1], None, ALU.mult
                                      ).then_inc(s["ktopped"], 1)
                vec.wait_ge(s["kspread"], 1)
                vec.wait_ge(s["kv_in"], NT)
                for t in range(GROUPS):
                    r = slice(t * GN, (t + 1) * GN)
                    vec.tensor_tensor(kall[:, r, :], kall[:, r, :], psT[1][:, 0:2, :].rearrange("p e w -> p (e w)")
                                      .unsqueeze(1).to_broadcast([P, GN, HS]), ALU.subtract).then_inc(s["kshifted"], 1)
                for e in range(2):
                    vec.wait_ge(s["kv_done"], e + 1)
                    c.then(vec.reciprocal(ksum[:, e:e + 1], psM[e][:, 4 * D:VW]))
                    c.wait()
                    for j in range(4):
                        r = slice(j * SL, (j + 1) * SL)
                        last = vec.tensor_scalar(kv[r, e, j * D:(j + 1) * D], psM[e][r, j * D:(j + 1) * D],
                                                 ksum[r, e:e + 1], None, ALU.mult)
                    last.then_inc(s["kv_in2"], 1)
                vec.wait_ge(s["kvflip"], 1)
                vec.tensor_copy(kvT[:].rearrange("p e c w -> p (e c w)"), psT[0][:].rearrange("p k n -> p (k n)")
                                ).then_inc(s["kvT_in"], 1)
                for e in range(2):
                    vec.wait_ge(s["fold_done"], e + 1)
                    c.then(vec.tensor_copy(folded[:, e, :], psM[e][:]))


def quantise_weights(nc, a, T, W):
    with ExitStack() as stack:
        m = Memory(nc, stack, "quant")
        n_groups = FK * KC
        pieces = 4
        batches = n_groups // 4
        w = m.sb("w", [P, 2, n_groups, P])
        mag = m.sb("mag", [P, 2, n_groups, P])
        scale = m.sb("scale", [P, 3, n_groups])
        half = m.sb("half", [P, 3, n_groups])
        psT = [m.ps(f"psT{i}", [P, 4, P]) for i in range(4)]
        landed = [[m.sem(f"landed{i}_{q}") for q in range(pieces)] for i in range(3)]
        steps, sized, signed, chosen, ready, turned, taken, lows = (
            m.sem(s) for s in ("steps", "sized", "signed", "chosen", "ready", "turned", "taken", "lows"))
        sources = [(a["L0_ffn_w_gate"].rearrange("(f p) (c e) -> p f c e", p=P, e=P), FK, KC, W["gateT"]),
                   (a["L0_ffn_w_up"].rearrange("(f p) (c e) -> p f c e", p=P, e=P), FK, KC, W["upT"]),
                   (a["L0_ffn_w_down"].rearrange("(k p) (c e) -> p k c e", p=P, e=P), KC, FK, W["downT"][:, 0])]
        cuts = [[(ro * q + pieces - 1) // pieces for q in range(pieces + 1)] for _s, ro, _c, _t in sources]
        piece = [[slice(cut[q] * src[2], cut[q + 1] * src[2]) for q in range(pieces)] for cut, src in zip(cuts, sources)]
        with nc.Block() as block:
            @block.sync
            def _(sp):
                for i, (src, ro, co, _t) in enumerate(sources):
                    if i >= 2:
                        sp.wait_ge(turned, (i - 1) * batches)
                    for q in range(pieces):
                        sp.dma_start(w[:, i % 2].rearrange("p (r c) e -> p r c e", r=ro)[:, cuts[i][q]:cuts[i][q + 1]],
                                     src[:, cuts[i][q]:cuts[i][q + 1]]).then_inc(landed[i][q], 16)

            @block.scalar
            def _(act):
                def sizes_and_signs(i):
                    if i >= 2:
                        act.wait_ge(ready, (i - 1) * pieces)
                    for q, at in enumerate(piece[i]):
                        act.wait_ge(landed[i][q], 16)
                        act.activation(mag[:, i % 2, at], w[:, i % 2, at], ACT.Abs).then_inc(sized, 1)
                        act.wait_ge(sized, i * pieces + q + 1)
                        act.activation(w[:, i % 2, at], w[:, i % 2, at], ACT.Sign).then_inc(signed, 1)

                def take(i):
                    flat = sources[i][3][:].rearrange("p c r -> p (c r)")
                    for b in range(batches):
                        n = i * batches + b
                        act.wait_ge(turned, n + 1)
                        act.copy(flat[:, b * 4 * P:(b + 1) * 4 * P], psT[n % 4][:].rearrange("p k e -> p (k e)")
                                 ).then_inc(taken, 1)

                sizes_and_signs(0)
                sizes_and_signs(1)
                take(0)
                sizes_and_signs(2)
                take(1)
                take(2)

            @block.vector
            def _(vec):
                c = Chain(vec, steps)
                for i in range(3):
                    for q, at in enumerate(piece[i]):
                        def over(x):
                            return x[:, i, at].unsqueeze(2).to_broadcast([P, at.stop - at.start, P])
                        vec.wait_ge(sized, i * pieces + q + 1)
                        c.then(vec.tensor_reduce(scale[:, i, at], mag[:, i % 2, at], AX.X, ALU.add))
                        c.wait()
                        c.then(vec.tensor_scalar(scale[:, i, at], scale[:, i, at], 1.0 / P, EPS, ALU.mult, ALU.add))
                        c.wait()
                        c.then(vec.tensor_scalar(half[:, i, at], scale[:, i, at], 0.5, None, ALU.mult))
                        c.wait()
                        ins = vec.tensor_tensor(mag[:, i % 2, at], mag[:, i % 2, at], over(half), ALU.is_gt)
                        if i < 2:
                            ins.then_inc(chosen, 1)
                            c.then(vec.tensor_copy(W["means"][:, i, at], scale[:, i, at]))
                        else:
                            c.then(ins)
                            c.wait()
                            vec.tensor_tensor(mag[:, i % 2, at], mag[:, i % 2, at], over(scale),
                                              ALU.mult).then_inc(chosen, 1)
                flat = [W["downT"][:, part].rearrange("p c r -> p (c r)") for part in range(2)]
                for b in range(batches):
                    n = 2 * batches + b
                    at = slice(b * 4 * P, (b + 1) * 4 * P)
                    vec.wait_ge(taken, n + 1)
                    vec.tensor_tensor(flat[1][:, at], psT[n % 4][:].rearrange("p k e -> p (k e)"),
                                      flat[0][:, at].bitcast(F32), ALU.subtract).then_inc(lows, 1)

            @block.gpsimd
            def _(pool):
                for i in range(3):
                    for q, at in enumerate(piece[i]):
                        pool.wait_ge(signed, i * pieces + q + 1)
                        pool.wait_ge(chosen, i * pieces + q + 1)
                        pool.tensor_tensor(w[:, i % 2, at], w[:, i % 2, at], mag[:, i % 2, at],
                                           ALU.mult).then_inc(ready, 1)

            @block.tensor
            def _(pe):
                for i, (_s, ro, co, _t) in enumerate(sources):
                    pe.wait_ge(ready, (i + 1) * pieces)
                    wv = w[:, i % 2].rearrange("p (r c) e -> p r c e", r=ro)
                    for b in range(batches):
                        n = i * batches + b
                        if n >= 4:
                            pe.wait_ge(taken, n - 3)
                        if n >= 2 * batches + 4:
                            pe.wait_ge(lows, n - 2 * batches - 3)
                        for j in range(4):
                            cc, rr = divmod(b * 4 + j, ro)
                            last = pe.transpose(psT[n % 4][:, j, :], wv[:, rr, cc, :], T["ident"][:])
                        last.then_inc(turned, 1)


def gated_ffn(nc, a, T, W, x3_dram, y3_dram, out):
    with ExitStack() as stack:
        m = Memory(nc, stack, "ffn")
        y = m.sb("y", [P, GN, C])
        res = m.sb("res", [P, GN, C])
        yT = m.sb("yT", [P, 2, KC, NODES], F32R)
        sums = m.sb("sums", [P, 2, 2, 2, NODES])
        silu = m.sb("silu", [P, 2, NODES])
        h = m.sb("h", [P, 2, NODES])
        hT = m.sb("hT", [P, 2, FK, NODES], F32R)
        psT = [m.ps(f"psT{i}", [P, KC, P]) for i in range(2)]
        psP = [m.ps(f"psP{i}", [P, NODES]) for i in range(KC)]
        psO = [m.ps(f"psO{i}", [P, C]) for i in range(2)]
        (y_in, res_in, turned, yT_high, yT_in, partial, scaled, added, summed, silued, multiplied, hT_high, low_vec,
         low_pool, out_done, done, stored) = (
            m.sem(s) for s in ("y_in", "res_in", "turned", "yT_high", "yT_in", "partial", "scaled", "added", "summed",
                               "silued", "multiplied", "hT_high", "low_vec", "low_pool", "out_done", "done", "stored"))
        ON_POOL = [f for f in range(FK) if f % 2 == 1]
        ON_VEC = [f for f in range(FK) if f % 2 == 0]

        def rows_of(dram, g):
            return dram[bass.ds(g * NODES, NODES), :].rearrange("(t p) c -> p t c", p=P)

        def before(g, f):
            return g * FK + (f - 1 if f else 0)

        with nc.Block() as block:
            @block.sync
            def _(sp):
                sp.dma_start(y[:], rows_of(y3_dram, 0)).then_inc(y_in, 16)

                def group(g, end):
                    if later(g):
                        sp.wait_ge(done, g * GN)
                        sp.dma_start(rows_of(out, g - 1), res[:]).then_inc(stored, 16)
                        sp.wait_ge(stored, g * 16)
                    sp.dma_start(res[:], rows_of(x3_dram, g)).then_inc(res_in, 16)
                    if not end:
                        sp.wait_ge(turned, g * GN + GN)
                        sp.dma_start(y[:], rows_of(y3_dram, g + 1)).then_inc(y_in, 16)
                turns_ahead(sp, GROUPS, group)
                sp.wait_ge(done, GROUPS * GN)
                r0 = (GROUPS - 1) * NODES
                sp.dma_start(out[r0:(NT - 1) * P, :].rearrange("(t p) c -> p t c", p=P), res[:, 0:GN - 1, :]
                             ).then_inc(stored, 16)
                sp.dma_start(out[(NT - 1) * P:N, :], res[0:LAST, GN - 1, :]).then_inc(stored, 16)
                sp.wait_ge(stored, 16 * (GROUPS + 1))

            @block.tensor
            def _(pe):
                def flip(g, n):
                    if n == 0:
                        pe.wait_ge(y_in, g * 16 + 16)
                    if later(g) or n >= 2:
                        pe.wait_ge(yT_in, g * GN + n - 1)
                    for k in range(KC):
                        last = pe.transpose(psT[n % 2][:, k, :], y[:, n, k * P:(k + 1) * P], T["ident"][:])
                    last.then_inc(turned, 1)

                for n in range(GN):
                    flip(0, n)

                def group(g, end):
                    pe.wait_ge(yT_in, g * GN + GN)
                    for f in range(FK):
                        for j, w in enumerate((W["gateT"], W["upT"])):
                            s = (g * FK + f) * 2 + j
                            for k in range(KC):
                                if later(g) or f or j:
                                    pe.wait_ge(scaled if k < 2 else added, 2 * s - 1 + k % 2)
                                for part in (1, 0):
                                    last = pe.matmul(psP[k][:], w[:, k, f * P:(f + 1) * P], yT[:, part, k, :],
                                                     start=(part == 1), stop=(part == 0))
                                last.then_inc(partial, 1)

                    def down(n):
                        if later(g) or n >= 2:
                            pe.wait_ge(done, g * GN + n - 1)
                        for f in range(FK):
                            last = product(pe, psO[n % 2][:], [hT[:, i, f, n * P:(n + 1) * P] for i in range(2)],
                                           [W["downT"][:, i, f, :] for i in range(2)], start=(f == 0),
                                           stop=(f == FK - 1))
                        last.then_inc(out_done, 1)

                    if not end:
                        flip(g + 1, 0)
                        flip(g + 1, 1)
                    pe.wait_ge(low_vec, (g + 1) * len(ON_VEC))
                    pe.wait_ge(low_pool, (g + 1) * len(ON_POOL))
                    for n in range(GN):
                        down(n)
                        if not end and n + 2 < GN:
                            flip(g + 1, n + 2)
                turns_ahead(pe, GROUPS, group)

            @block.scalar
            def _(act):
                def high(g, n):
                    act.wait_ge(turned, g * GN + n + 1)
                    act.copy(yT[:, 0, :, n * P:(n + 1) * P], psT[n % 2][:]).then_inc(yT_high, 1)

                for n in range(GN):
                    high(0, n)

                def scale(g, f, j):
                    if later(g) or f >= 2:
                        act.wait_ge(multiplied, before(g, f))
                    for k in range(2):
                        act.wait_ge(partial, ((g * FK + f) * 2 + j) * KC + k + 1)
                        act.activation(sums[:, f % 2, j, k, :], psP[k][:], ACT.Copy,
                                       scale=W["means"][:, j, f * KC + k:f * KC + k + 1]).then_inc(scaled, 1)

                def smooth(g, f):
                    act.wait_ge(summed, (g * FK + f) * 2 + 1)
                    act.activation(silu[:, f % 2, :], sums[:, f % 2, 0, 0, :], ACT.Silu).then_inc(silued, 1)

                def round_h(g, f):
                    act.wait_ge(multiplied, g * FK + f + 1)
                    act.copy(hT[:, 0, f, :], h[:, f % 2, :]).then_inc(hT_high, 1)

                def group(g, end):
                    for f in range(FK + 1):
                        if f < FK:
                            scale(g, f, 0)
                        if f:
                            smooth(g, f - 1)
                        if f < FK:
                            scale(g, f, 1)
                        if f:
                            round_h(g, f - 1)
                    if not end:
                        for n in range(GN):
                            high(g + 1, n)
                turns_ahead(act, GROUPS, group)

            @block.gpsimd
            def _(pool):
                def total(g, f, j):
                    pool.wait_ge(added, ((g * FK + f) * 2 + j) * 2 + 2)
                    pool.tensor_tensor(sums[:, f % 2, j, 0, :], sums[:, f % 2, j, 0, :], sums[:, f % 2, j, 1, :],
                                       ALU.add).then_inc(summed, 1)

                def group(g):
                    for f in range(FK + 1):
                        for j in range(2):
                            if f < FK:
                                total(g, f, j)
                        if f - 1 in ON_POOL:
                            pool.wait_ge(hT_high, g * FK + f)
                            pool.tensor_tensor(hT[:, 1, f - 1, :], h[:, (f - 1) % 2, :], hT[:, 0, f - 1, :].bitcast(F32),
                                               ALU.subtract).then_inc(low_pool, 1)
                turns(pool, GROUPS, group)

            @block.vector
            def _(vec):
                def low(g, n):
                    vec.wait_ge(yT_high, g * GN + n + 1)
                    vec.tensor_tensor(yT[:, 1, :, n * P:(n + 1) * P], psT[n % 2][:],
                                      yT[:, 0, :, n * P:(n + 1) * P].bitcast(F32), ALU.subtract).then_inc(yT_in, 1)

                for n in range(GN):
                    low(0, n)

                def add(g, f, j):
                    s = (g * FK + f) * 2 + j
                    for k in range(2, KC):
                        half = sums[:, f % 2, j, k - 2, :]
                        vec.wait_ge(partial, s * KC + k + 1)
                        vec.wait_ge(scaled, s * 2 + k - 1)
                        vec.scalar_tensor_tensor(out=half, in0=psP[k][:],
                                                 scalar=W["means"][:, j, f * KC + k:f * KC + k + 1],
                                                 in1=half, op0=ALU.mult, op1=ALU.add).then_inc(added, 1)

                def multiply(g, f):
                    vec.wait_ge(silued, g * FK + f + 1)
                    vec.wait_ge(summed, (g * FK + f) * 2 + 2)
                    if later(g) or f >= 2:
                        vec.wait_ge(hT_high, before(g, f))
                        user = f - 2 if f >= 2 else FK - 1 - f
                        if user in ON_POOL:
                            vec.wait_ge(low_pool, (g if f >= 2 else g - 1) * len(ON_POOL) + ON_POOL.index(user) + 1)
                        else:
                            vec.wait_ge(low_vec, (g if f >= 2 else g - 1) * len(ON_VEC) + ON_VEC.index(user) + 1)
                    vec.tensor_tensor(h[:, f % 2, :], silu[:, f % 2, :], sums[:, f % 2, 1, 0, :],
                                      ALU.mult).then_inc(multiplied, 1)

                def group(g, end):
                    for f in range(FK + 1):
                        if f < FK:
                            add(g, f, 0)
                        if f:
                            multiply(g, f - 1)
                        if f < FK:
                            add(g, f, 1)
                        if f - 1 in ON_VEC:
                            vec.wait_ge(hT_high, g * FK + f)
                            vec.tensor_tensor(hT[:, 1, f - 1, :], h[:, (f - 1) % 2, :], hT[:, 0, f - 1, :].bitcast(F32),
                                              ALU.subtract).then_inc(low_vec, 1)
                    if not end:
                        low(g + 1, 0)
                        low(g + 1, 1)
                    vec.wait_ge(res_in, g * 16 + 16)
                    for n in range(GN):
                        vec.wait_ge(out_done, g * GN + n + 1)
                        vec.tensor_tensor(res[:, n, :], psO[n % 2][:], res[:, n, :], ALU.add).then_inc(done, 1)
                        if not end and n + 2 < GN:
                            low(g + 1, n + 2)
                turns_ahead(vec, GROUPS, group)


def gps_layer(nc, a, out):
    with ExitStack() as whole:
        kept = Memory(nc, whole, "kept")
        T = {}
        xn, k, v, base, x1, y1, x3, y3 = (nc.dram_tensor(n, (NP, C), F32).ap() for n in (
            "xn_rows", "k_rows", "v_rows", "base_rows", "x1_rows", "y1_rows", "x3_rows", "y3_rows"))
        make_constants(nc, kept, T)
        with ExitStack() as edges:
            share_edges(nc, Memory(nc, edges, "edges"), T)
            ordered = [nc.dram_tensor(n, (ET * P, 1), I32).ap() for n in ("ordered_dst", "ordered_src")]
            order_edges(nc, a, T, ordered)
            index_edges(nc, a, T, ordered, xn)
            for layer in range(LAYERS):
                with ExitStack() as stack:
                    m = Memory(nc, stack, f"layer{layer}")
                    scores = m.sb("scores", [P, SLOTS * H])
                    with ExitStack() as queries:
                        T["q_parts"] = Memory(nc, queries, f"layer{layer}").sb("q_parts", [P, 3, NT, C], BF16)
                        project_nodes(nc, a, T, layer, x1 if layer else xn, xn, k, v, base)
                        score_edges(nc, a, T, layer, k, scores)
                    weights = m.sb("weights", [P, SLOTS * H])
                    soften(nc, T, layer, scores, weights)
                    agg = m.sb("agg", [P, NT, AW])
                    x = m.sb("x", [P, NT, C])
                    aggregate(nc, a, T, layer, v, weights, agg, base, x)
                    combine(nc, a, T, layer, agg, x, y1 if layer == LAYERS - 1 else x1)
        with ExitStack() as stack:
            m = Memory(nc, stack, "mix")
            qT = m.sb("qT", [P, 2, NP])
            folded = m.sb("folded", [P, 2, C])
            project_slices(nc, a, T, xn, qT, folded)
            node_mlp(nc, a, T, y1, xn, qT, folded, x3, y3)
        W = {"gateT": kept.sb("gateT", [P, KC, FFN], F32R), "upT": kept.sb("upT", [P, KC, FFN], F32R),
             "downT": kept.sb("downT", [P, 2, FK, C], F32R), "means": kept.sb("means", [P, 2, FK * KC])}
        quantise_weights(nc, a, T, W)
        gated_ffn(nc, a, T, W, x3, y3, out)


def kernel(**inputs):
    import numpy as np
    import concourse.bacc as bacc
    from concourse.bass_utils import run_bass_kernel_spmd

    nc = bacc.Bacc("TRN2", target_bir_lowering=False, num_devices=1)
    arrays, aps = {}, {}
    for name in inputs:
        if name in ("edge_type_10", "edge_weight"):
            continue
        arrays[name] = np.ascontiguousarray(inputs[name])
        aps[name] = nc.dram_tensor(name, arrays[name].shape, mybir.dt.from_np(arrays[name].dtype),
                                   kind="ExternalInput").ap()
    out = nc.dram_tensor("out", (N, C), F32, kind="ExternalOutput").ap()
    gps_layer(nc, aps, out)
    return run_bass_kernel_spmd(nc, [arrays], core_ids=[0]).results[0]["out"]
```
